# Optimizing a Trainium2 kernel written in Bass

```python
import numpy as np
import jax
import jax.numpy as jnp

def _softmax(x, axis=-1):
    return jax.nn.softmax(x, axis=axis)

def _gelu(x):
    return jax.nn.gelu(x, approximate=True)

def _silu(x):
    return jax.nn.silu(x)

def _sigmoid(x):
    return jax.nn.sigmoid(x)

def _layernorm(x, axis=-1, eps=1e-05):
    m = jnp.mean(x, axis=axis, keepdims=True)
    v = jnp.var(x, axis=axis, keepdims=True)
    return (x - m) / jnp.sqrt(v + eps)

def _scatter_add(tgt, idx, src, axis=0):
    return tgt.at[idx].add(src)

def _segment_sum(src, seg, n):
    return jax.ops.segment_sum(src, seg, n)
kernel_name = 'mk_prb_d2_jaxref_r8_6c70c0'

def setup_inputs(seed: int=0):
    np.random.seed(seed)
    _w = jnp.asarray

    def _L0_attn_setup():
        import jax, jax.numpy as jnp
        import numpy as np
        D_MODEL = 128
        N_HEADS = 16
        DH = D_MODEL // N_HEADS
        B, T = (4, 256)
        ROPE_BASE = 10000.0
        EPS = 1e-06

        def _rope(q, k, base=ROPE_BASE):
            half = q.shape[-1] // 2
            freqs = jnp.arange(half, dtype=q.dtype)
            inv_freq = base ** (-freqs / half)
            pos = jnp.arange(q.shape[2], dtype=q.dtype)
            ang = pos[:, None] * inv_freq[None, :]
            c = jnp.cos(ang)[None, None]
            s = jnp.sin(ang)[None, None]

            def rot(x):
                x1 = x[..., :half]
                x2 = x[..., half:2 * half]
                return jnp.concatenate([x1 * c - x2 * s, x1 * s + x2 * c], axis=-1)
            return (rot(q), rot(k))

        def _phi(x):
            return jax.nn.elu(x) + 1.0

        def _forward(x, Wq, Wk, Wv, Wo):
            Bx, Tx, D = x.shape
            H, dh = (N_HEADS, D // N_HEADS)
            q = (x @ Wq.T).reshape(Bx, Tx, H, dh).transpose(0, 2, 1, 3)
            k = (x @ Wk.T).reshape(Bx, Tx, H, dh).transpose(0, 2, 1, 3)
            v = (x @ Wv.T).reshape(Bx, Tx, H, dh).transpose(0, 2, 1, 3)
            q, k = _rope(q, k)
            q = _phi(q)
            k = _phi(k)
            qT = q.transpose(2, 0, 1, 3)
            kT = k.transpose(2, 0, 1, 3)
            vT = v.transpose(2, 0, 1, 3)

            def step(carry, qkv):
                K_sum, KV = carry
                q_t, k_t, v_t = qkv
                K_sum = K_sum + k_t
                KV = KV + k_t[..., :, None] * v_t[..., None, :]
                num = jnp.einsum('bhd,bhde->bhe', q_t, KV)
                den = jnp.maximum(jnp.einsum('bhd,bhd->bh', q_t, K_sum), EPS)
                return ((K_sum, KV), num / den[..., None])
            init = (jnp.zeros((Bx, H, dh), x.dtype), jnp.zeros((Bx, H, dh, dh), x.dtype))
            _, Y = jax.lax.scan(step, init, (qT, kT, vT))
            Y = Y.transpose(1, 0, 2, 3).reshape(Bx, Tx, D)
            return Y @ Wo.T
        key = jax.random.key(seed)
        kx, kq, kk, kv, ko = jax.random.split(key, 5)
        scale = 0.02
        return {'x': jax.random.normal(kx, (B, T, D_MODEL), jnp.float32), 'Wq': jax.random.normal(kq, (D_MODEL, D_MODEL), jnp.float32) * scale, 'Wk': jax.random.normal(kk, (D_MODEL, D_MODEL), jnp.float32) * scale, 'Wv': jax.random.normal(kv, (D_MODEL, D_MODEL), jnp.float32) * scale, 'Wo': jax.random.normal(ko, (D_MODEL, D_MODEL), jnp.float32) * scale}
    _L0_attn_in = _L0_attn_setup()

    def _L0_ffn_setup():
        import jax, jax.numpy as jnp
        import numpy as np
        TOP_K = 2

        def _mlp(x, w_fc, w_proj):
            return jnp.square(jax.nn.relu(x @ w_fc.T)) @ w_proj.T
        key = jax.random.key(seed)
        ks = jax.random.split(key, 6)
        B, S, D, E = (4, 256, 128, 8)
        d_ff = 4 * D
        x = jax.random.normal(ks[0], (B, S, D), dtype=jnp.float32)
        router_w = jax.random.normal(ks[1], (E, D), dtype=jnp.float32) * 0.02
        w_fc = jax.random.normal(ks[2], (E, d_ff, D), dtype=jnp.float32) * 0.02
        w_proj = jax.random.normal(ks[3], (E, D, d_ff), dtype=jnp.float32) * 0.02
        shared_fc = jax.random.normal(ks[4], (d_ff, D), dtype=jnp.float32) * 0.02
        shared_proj = jax.random.normal(ks[5], (D, d_ff), dtype=jnp.float32) * 0.02
        return {'x': x, 'router_w': router_w, 'w_fc': w_fc, 'w_proj': w_proj, 'shared_fc': shared_fc, 'shared_proj': shared_proj}
    _L0_ffn_in = _L0_ffn_setup()

    def _L1_attn_setup():
        import jax, jax.numpy as jnp
        import numpy as np
        N_HEADS = 16
        CHUNK = 64
        TAU = 12.5
        THRESHOLD = 0.5
        N_FHN_STEPS = 2

        def fhn_dynamics(stimulus, a, b, dt, n_steps=N_FHN_STEPS, tau=TAU, threshold=THRESHOLD):
            stim_scale = jnp.clip(jnp.max(jnp.abs(stimulus), axis=-1, keepdims=True), 1e-06, None)
            stim_normed = stimulus / stim_scale
            gate = jax.nn.sigmoid((jnp.abs(stimulus) - threshold) * 10.0)
            I = stim_normed * (0.1 + 0.9 * gate)
            v = jnp.zeros_like(stimulus)
            w = jnp.zeros_like(stimulus)
            alpha = dt / tau
            denom = 1.0 + alpha * b
            for _ in range(n_steps):
                dv_explicit = v - v * v * v / 3.0 - w + I
                v_next = v + dt * dv_explicit
                w_next = (w + alpha * (v_next + a)) / denom
                v = jnp.clip(v_next, -3.0, 3.0)
                w = jnp.clip(w_next, -3.0, 3.0)
            response = v * stim_scale
            return (response, v)

        def chunked_fhn_attention(q, k, v, a, b, dt, chunk_size=CHUNK):
            B, H, T, Dh = q.shape
            n_chunks = (T + chunk_size - 1) // chunk_size
            scale = 1.0 / Dh ** 0.5
            out_chunks = []
            fhn_states = []
            for ci in range(n_chunks):
                s = ci * chunk_size
                e = min(s + chunk_size, T)
                q_c = q[:, :, s:e, :]
                k_c = k[:, :, :e, :]
                v_c = v[:, :, :e, :]
                scores = jnp.einsum('bhtd,bhsd->bhts', q_c, k_c) * scale
                probs = jax.nn.softmax(scores, axis=-1)
                attn_energy = probs.sum(axis=-1)
                stim = jnp.broadcast_to(attn_energy[..., None], (B, H, e - s, Dh))
                fhn_out, fhn_state = fhn_dynamics(stim, a, b, dt)
                fhn_gate = jax.nn.sigmoid(fhn_out.mean(axis=-1))[..., None]
                probs = probs * (0.5 + 0.5 * fhn_gate)
                probs = probs / (probs.sum(axis=-1, keepdims=True) + 1e-08)
                out_chunks.append(jnp.einsum('bhts,bhsd->bhtd', probs, v_c))
                fhn_states.append(fhn_state.mean())
            out = jnp.concatenate(out_chunks, axis=2)
            fhn_state_mean = jnp.stack(fhn_states).mean()
            return (out, fhn_state_mean)
        key = jax.random.key(seed)
        ks = jax.random.split(key, 5)
        B, T, E = (2, 512, 128)
        x = jax.random.normal(ks[0], (B, T, E), dtype=jnp.float32)
        spectral_basis = jax.random.normal(ks[1], (B, T, 32), dtype=jnp.float32)
        W_qkv = jax.random.normal(ks[2], (3 * E, E), dtype=jnp.float32) * E ** (-0.5)
        W_out = jax.random.normal(ks[3], (E, E), dtype=jnp.float32) * E ** (-0.5)
        a = jnp.asarray(0.7, dtype=jnp.float32)
        b = jnp.asarray(0.8, dtype=jnp.float32)
        dt = jnp.asarray(1.0, dtype=jnp.float32)
        return {'x': x, 'spectral_basis': spectral_basis, 'W_qkv': W_qkv, 'W_out': W_out, 'a': a, 'b': b, 'dt': dt}
    _L1_attn_in = _L1_attn_setup()

    def _L1_ffn_setup():
        import jax, jax.numpy as jnp
        import numpy as np
        DIM = 128

        def _reference_tuple_inner(x, W_r, W_k, W_v, mu_r, mu_k):
            B, T, C = x.shape
            x_prev = jnp.concatenate([jnp.zeros((B, 1, C), x.dtype), x[:, :-1, :]], axis=1)
            xr = mu_r * x + (1.0 - mu_r) * x_prev
            xk = mu_k * x + (1.0 - mu_k) * x_prev
            r = jax.nn.sigmoid(jnp.einsum('btc,dc->btd', xr, W_r))
            k = jnp.einsum('btc,dc->btd', xk, W_k)
            k_act = jnp.square(jax.nn.relu(k))
            out = r * jnp.einsum('btc,dc->btd', k_act, W_v)
            new_state = x[:, -1, :]
            return (out, new_state)
        key = jax.random.key(seed)
        ks = jax.random.split(key, 6)
        B, T, C = (8, 256, DIM)
        x = jax.random.normal(ks[0], (B, T, C), dtype=jnp.float32)
        s = 1.0 / np.sqrt(C)
        W_r = jax.random.uniform(ks[1], (C, C), jnp.float32, -s, s)
        W_k = jax.random.uniform(ks[2], (C, C), jnp.float32, -s, s)
        W_v = jax.random.uniform(ks[3], (C, C), jnp.float32, -s, s)
        mu_r = jax.random.uniform(ks[4], (C,), jnp.float32)
        mu_k = jax.random.uniform(ks[5], (C,), jnp.float32)
        return {'x': x, 'W_r': W_r, 'W_k': W_k, 'W_v': W_v, 'mu_r': mu_r, 'mu_k': mu_k}
    _L1_ffn_in = _L1_ffn_setup()
    _d = {'L0_attn_x': _L0_attn_in['x'], 'L0_attn_Wq': _L0_attn_in['Wq'], 'L0_attn_Wk': _L0_attn_in['Wk'], 'L0_attn_Wv': _L0_attn_in['Wv'], 'L0_attn_Wo': _L0_attn_in['Wo'], 'L0_ffn_router_w': _L0_ffn_in['router_w'], 'L0_ffn_w_fc': _L0_ffn_in['w_fc'], 'L0_ffn_w_proj': _L0_ffn_in['w_proj'], 'L0_ffn_shared_fc': _L0_ffn_in['shared_fc'], 'L0_ffn_shared_proj': _L0_ffn_in['shared_proj'], 'L1_attn_spectral_basis': _L1_attn_in['spectral_basis'], 'L1_attn_W_qkv': _L1_attn_in['W_qkv'], 'L1_attn_W_out': _L1_attn_in['W_out'], 'L1_attn_a': _L1_attn_in['a'], 'L1_attn_b': _L1_attn_in['b'], 'L1_attn_dt': _L1_attn_in['dt'], 'L1_ffn_W_r': _L1_ffn_in['W_r'], 'L1_ffn_W_k': _L1_ffn_in['W_k'], 'L1_ffn_W_v': _L1_ffn_in['W_v'], 'L1_ffn_mu_r': _L1_ffn_in['mu_r'], 'L1_ffn_mu_k': _L1_ffn_in['mu_k']}
    _x0 = _d['L0_attn_x']
    _d['L0_attn_x'] = jax.random.normal(jax.random.fold_in(jax.random.key(seed), 1), (16, 512, 128), dtype=_x0.dtype)
    del _x0
    return _d

def reference(L0_attn_x, L0_attn_Wq, L0_attn_Wk, L0_attn_Wv, L0_attn_Wo, L0_ffn_router_w, L0_ffn_w_fc, L0_ffn_w_proj, L0_ffn_shared_fc, L0_ffn_shared_proj, L1_attn_spectral_basis, L1_attn_W_qkv, L1_attn_W_out, L1_attn_a, L1_attn_b, L1_attn_dt, L1_ffn_W_r, L1_ffn_W_k, L1_ffn_W_v, L1_ffn_mu_r, L1_ffn_mu_k):

    def _L0_attn_ref(x, Wq, Wk, Wv, Wo):
        import jax, jax.numpy as jnp
        import numpy as np
        D_MODEL = 128
        N_HEADS = 16
        DH = D_MODEL // N_HEADS
        B, T = (4, 256)
        ROPE_BASE = 10000.0
        EPS = 1e-06

        def _rope(q, k, base=ROPE_BASE):
            half = q.shape[-1] // 2
            freqs = jnp.arange(half, dtype=q.dtype)
            inv_freq = base ** (-freqs / half)
            pos = jnp.arange(q.shape[2], dtype=q.dtype)
            ang = pos[:, None] * inv_freq[None, :]
            c = jnp.cos(ang)[None, None]
            s = jnp.sin(ang)[None, None]

            def rot(x):
                x1 = x[..., :half]
                x2 = x[..., half:2 * half]
                return jnp.concatenate([x1 * c - x2 * s, x1 * s + x2 * c], axis=-1)
            return (rot(q), rot(k))

        def _phi(x):
            return jax.nn.elu(x) + 1.0

        def _forward(x, Wq, Wk, Wv, Wo):
            Bx, Tx, D = x.shape
            H, dh = (N_HEADS, D // N_HEADS)
            q = (x @ Wq.T).reshape(Bx, Tx, H, dh).transpose(0, 2, 1, 3)
            k = (x @ Wk.T).reshape(Bx, Tx, H, dh).transpose(0, 2, 1, 3)
            v = (x @ Wv.T).reshape(Bx, Tx, H, dh).transpose(0, 2, 1, 3)
            q, k = _rope(q, k)
            q = _phi(q)
            k = _phi(k)
            qT = q.transpose(2, 0, 1, 3)
            kT = k.transpose(2, 0, 1, 3)
            vT = v.transpose(2, 0, 1, 3)

            def step(carry, qkv):
                K_sum, KV = carry
                q_t, k_t, v_t = qkv
                K_sum = K_sum + k_t
                KV = KV + k_t[..., :, None] * v_t[..., None, :]
                num = jnp.einsum('bhd,bhde->bhe', q_t, KV)
                den = jnp.maximum(jnp.einsum('bhd,bhd->bh', q_t, K_sum), EPS)
                return ((K_sum, KV), num / den[..., None])
            init = (jnp.zeros((Bx, H, dh), x.dtype), jnp.zeros((Bx, H, dh, dh), x.dtype))
            _, Y = jax.lax.scan(step, init, (qT, kT, vT))
            Y = Y.transpose(1, 0, 2, 3).reshape(Bx, Tx, D)
            return Y @ Wo.T
        return _forward(x, Wq, Wk, Wv, Wo)

    def _L0_ffn_ref(x, router_w, w_fc, w_proj, shared_fc, shared_proj):
        import jax, jax.numpy as jnp
        import numpy as np
        TOP_K = 2

        def _mlp(x, w_fc, w_proj):
            return jnp.square(jax.nn.relu(x @ w_fc.T)) @ w_proj.T
        B, S, D = x.shape
        E = router_w.shape[0]
        T = B * S
        flat = x.reshape(T, D)
        logits = flat @ router_w.T
        probs = jax.nn.softmax(logits.astype(jnp.float32), axis=-1)
        topk_p, topk_i = jax.lax.top_k(probs, TOP_K)
        topk_w = (topk_p / jnp.maximum(topk_p.sum(-1, keepdims=True), 1e-09)).astype(flat.dtype)
        combine = jnp.zeros((T, E), dtype=flat.dtype)
        combine = combine.at[jnp.arange(T)[:, None], topk_i].add(topk_w)
        out = jnp.zeros_like(flat)
        for e in range(E):
            out = out + _mlp(flat, w_fc[e], w_proj[e]) * combine[:, e:e + 1]
        out = out + _mlp(flat, shared_fc, shared_proj)
        return out.reshape(B, S, D)

    def _L1_attn_ref(x, spectral_basis, W_qkv, W_out, a, b, dt):
        import jax, jax.numpy as jnp
        import numpy as np
        N_HEADS = 16
        CHUNK = 64
        TAU = 12.5
        THRESHOLD = 0.5
        N_FHN_STEPS = 2

        def fhn_dynamics(stimulus, a, b, dt, n_steps=N_FHN_STEPS, tau=TAU, threshold=THRESHOLD):
            stim_scale = jnp.clip(jnp.max(jnp.abs(stimulus), axis=-1, keepdims=True), 1e-06, None)
            stim_normed = stimulus / stim_scale
            gate = jax.nn.sigmoid((jnp.abs(stimulus) - threshold) * 10.0)
            I = stim_normed * (0.1 + 0.9 * gate)
            v = jnp.zeros_like(stimulus)
            w = jnp.zeros_like(stimulus)
            alpha = dt / tau
            denom = 1.0 + alpha * b
            for _ in range(n_steps):
                dv_explicit = v - v * v * v / 3.0 - w + I
                v_next = v + dt * dv_explicit
                w_next = (w + alpha * (v_next + a)) / denom
                v = jnp.clip(v_next, -3.0, 3.0)
                w = jnp.clip(w_next, -3.0, 3.0)
            response = v * stim_scale
            return (response, v)

        def chunked_fhn_attention(q, k, v, a, b, dt, chunk_size=CHUNK):
            B, H, T, Dh = q.shape
            n_chunks = (T + chunk_size - 1) // chunk_size
            scale = 1.0 / Dh ** 0.5
            out_chunks = []
            fhn_states = []
            for ci in range(n_chunks):
                s = ci * chunk_size
                e = min(s + chunk_size, T)
                q_c = q[:, :, s:e, :]
                k_c = k[:, :, :e, :]
                v_c = v[:, :, :e, :]
                scores = jnp.einsum('bhtd,bhsd->bhts', q_c, k_c) * scale
                probs = jax.nn.softmax(scores, axis=-1)
                attn_energy = probs.sum(axis=-1)
                stim = jnp.broadcast_to(attn_energy[..., None], (B, H, e - s, Dh))
                fhn_out, fhn_state = fhn_dynamics(stim, a, b, dt)
                fhn_gate = jax.nn.sigmoid(fhn_out.mean(axis=-1))[..., None]
                probs = probs * (0.5 + 0.5 * fhn_gate)
                probs = probs / (probs.sum(axis=-1, keepdims=True) + 1e-08)
                out_chunks.append(jnp.einsum('bhts,bhsd->bhtd', probs, v_c))
                fhn_states.append(fhn_state.mean())
            out = jnp.concatenate(out_chunks, axis=2)
            fhn_state_mean = jnp.stack(fhn_states).mean()
            return (out, fhn_state_mean)
        B, T, E = x.shape
        H = N_HEADS
        Dh = E // H
        qkv = x @ W_qkv.T
        qkv = qkv.reshape(B, T, 3, H, Dh)
        q = jnp.transpose(qkv[:, :, 0], (0, 2, 1, 3))
        k = jnp.transpose(qkv[:, :, 1], (0, 2, 1, 3))
        v = jnp.transpose(qkv[:, :, 2], (0, 2, 1, 3))
        out, fhn_state_mean = chunked_fhn_attention(q, k, v, a, b, dt)
        out = jnp.transpose(out, (0, 2, 1, 3)).reshape(B, T, E)
        out = out @ W_out.T
        return out

    def _L1_ffn_ref(x, W_r, W_k, W_v, mu_r, mu_k):
        import jax, jax.numpy as jnp
        import numpy as np
        DIM = 128

        def _reference_tuple_inner(x, W_r, W_k, W_v, mu_r, mu_k):
            B, T, C = x.shape
            x_prev = jnp.concatenate([jnp.zeros((B, 1, C), x.dtype), x[:, :-1, :]], axis=1)
            xr = mu_r * x + (1.0 - mu_r) * x_prev
            xk = mu_k * x + (1.0 - mu_k) * x_prev
            r = jax.nn.sigmoid(jnp.einsum('btc,dc->btd', xr, W_r))
            k = jnp.einsum('btc,dc->btd', xk, W_k)
            k_act = jnp.square(jax.nn.relu(k))
            out = r * jnp.einsum('btc,dc->btd', k_act, W_v)
            new_state = x[:, -1, :]
            return (out, new_state)
        return _reference_tuple_inner(x, W_r, W_k, W_v, mu_r, mu_k)[0]
    x = L0_attn_x
    xn = _layernorm(x, axis=-1)
    x = x + _L0_attn_ref(xn, L0_attn_Wq, L0_attn_Wk, L0_attn_Wv, L0_attn_Wo) + _L0_ffn_ref(xn, L0_ffn_router_w, L0_ffn_w_fc, L0_ffn_w_proj, L0_ffn_shared_fc, L0_ffn_shared_proj)
    xn = _layernorm(x, axis=-1)
    x = x + _L1_attn_ref(xn, L1_attn_spectral_basis, L1_attn_W_qkv, L1_attn_W_out, L1_attn_a, L1_attn_b, L1_attn_dt) + _L1_ffn_ref(xn, L1_ffn_W_r, L1_ffn_W_k, L1_ffn_W_v, L1_ffn_mu_r, L1_ffn_mu_k)
    return x

_drawn_inputs = setup_inputs


def setup_inputs(seed=0):
    import zlib

    import numpy as np

    out = dict(_drawn_inputs(seed))
    spreads = {}
    factors = {'L0_attn_Wq': 8.0,
     'L0_attn_Wk': 8.0,
     'L0_attn_Wv': 7.044,
     'L0_attn_Wo': 6.85,
     'L0_ffn_router_w': 3.147,
     'L0_ffn_w_fc': 3.024,
     'L0_ffn_w_proj': 2.724,
     'L1_ffn_W_r': 3.196,
     'L1_ffn_mu_r': 6.274}
    for name, (base, spread) in spreads.items():
        noise = np.random.default_rng([zlib.crc32(name.encode()), seed]).standard_normal(out[name].shape)
        drawn = base * np.exp(spread * noise) if base else spread * noise
        out[name] = jnp.asarray(drawn.astype(out[name].dtype))
    for name, factor in factors.items():
        out[name] = (out[name] * factor).astype(out[name].dtype)
    return out
```

```python
import numpy as np
import concourse.bass as bass
from concourse import mybir
from contextlib import ExitStack

F32 = mybir.dt.float32
BF16 = mybir.dt.bfloat16
I32 = mybir.dt.int32
ALU = mybir.AluOpType
ACT = mybir.ActivationFunctionType
AX = mybir.AxisListType

B, T, D = 16, 512, 128
H, DH = 16, 8
E, FF = 8, 512
NB = FF // 128
J = T // 128
CHUNK = 64
SHEETS, G = 4, 4
UNITS = 10
PASS = SHEETS * UNITS
NPROD = 9
ROWS = NPROD * DH
HALF0 = ROWS
SHIFT0 = HALF0 + J
MROWS = SHIFT0
SROWS = SHIFT0 + 2
QK_LOADS = 2 * NPROD
CAP = B * T
GT = 256
REGION = CAP + GT
TB = 4
NTILES = -(-((2 * CAP + E * (GT - 1)) // GT) // TB) * TB
SPARE = NTILES - 2 * CAP // GT
DUMMY = E * REGION
NROWS = DUMMY + SPARE * GT
LN_EPS = 1e-5
DEN_EPS = 1e-6
TAU = 12.5
MASKED = -1e30


class Turn:

    def __init__(self, hi, p, m=2):
        self.hi, self.p, self.m = hi, p, m

    def __add__(self, d):
        return Turn(self.hi + (self.p + d) // self.m, (self.p + d) % self.m, self.m)

    def at(self, n, k):
        return self.hi * (self.m * n) + (n * self.p + k)

    def own(self, n, k):
        return self.hi * n + k

    def known(self):
        return self.m * self.hi + self.p if isinstance(self.hi, int) else None

    def less(self, n):
        return self.known() is not None and self.known() < n


def unit_parts(u):
    a, k = u // 5, u % 5
    if k < 2:
        return [(2 * a + k, 0, 0)]
    if k < 4:
        return [(2 * a + k - 2, 1, 0), (2 * a + k - 2, 3, T - 128)]
    return [(2 * a, 2, 0), (2 * a + 1, 2, T // 2)]


PLACE = {(g, kb): (u, c) for u in range(UNITS) for g, kb, c in unit_parts(u)}

MAX_UNITS = ([(3, g, 1) for g in range(G)] + [(2, g, 1) for g in range(G)]
             + [(1, 0, 2), (1, 2, 2)] + [(0, 0, 4)])
MU = len(MAX_UNITS)


def build(nc, io, out):
    ctx = ExitStack()
    with ctx:
        def sb(name, shape, dt=F32):
            return ctx.enter_context(nc.sbuf_tensor(name, shape, dt))

        def sem(name):
            return ctx.enter_context(nc.semaphore(name))

        def dram(name, shape, dt=F32):
            return nc.dram_tensor(name, shape, dt, kind="Internal").ap()

        x_d = io["x"].rearrange("b (j p) d -> b p j d", p=128)
        out_d = out.rearrange("b (j p) d -> b p j d", p=128)
        parts_d = dram("parts_d", (2, 2, 3, 128, T), BF16)
        shift_d = dram("shift_d", (2, 2, H, T), BF16)
        xa_d = dram("xa_d", (B, 128, J, D))
        res_d = dram("res_d", (B, 128, J, D))
        wts_d = dram("wts_d", (B, 128, 2 * J))
        slot_d = dram("slot_d", (B, 128, 2 * J), I32)
        idx_d = dram("idx_d", (B, 128, 2 * J), I32)
        xs_d = dram("xs_d", (NROWS, D))
        ys_d = dram("ys_d", (NTILES * GT, D))

        bank = [ctx.enter_context(nc.psum_tensor(f"bank{k}", [128, 512], F32)) for k in range(8)]
        OT, W5, W6, W7 = bank[4], bank[5], bank[6], bank[7]

        wqk = sb("wqk", [128, 4, 128])
        wvr = sb("wvr", [128, 128 + E])
        wo = sb("wo", [128, 128])
        sfc = sb("sfc", [128, FF])
        spj = sb("spj", [128, NB, 128])
        rope = sb("rope", [128, 2, T])
        tri = sb("tri", [128, 4, 128])
        ident = sb("ident", [128, 128])
        before = sb("before", [128, 2, 128], BF16)
        lower = sb("lower", [128, E, E])
        incl = sb("incl", [128, E, E])
        ebase = sb("ebase", [128, 2, E])
        tiles = sb("tiles", [128, 3, NTILES])
        steps = sb("steps", [128, CAP // GT])
        eps = sb("eps", [128, 1])
        wqkv2 = sb("wqkv2", [128, 3, 128])
        wo2 = sb("wo2", [128, 128])
        wrkv = sb("wrkv", [128, 3, 128])
        mu = sb("mu", [128, 2])
        omu = sb("omu", [128, 2])
        abd = sb("abd", [128, 3])

        QT = [sb(f"QT{p}", [128, H, T], BF16) for p in range(2)]
        KT = [sb(f"KT{p}", [128, H, T], BF16) for p in range(2)]
        V = [sb(f"V{p}", [128, J, H, 32]) for p in range(2)]
        P = [sb(f"P{p}", [128, UNITS, T]) for p in range(2)]
        oT = [sb(f"oT{p}", [128, T]) for p in range(2)]
        parts = [sb(f"parts{c}", [128, 3, T], BF16) for c in range(2)]
        yb = sb("yb", [128, J, H, DH + 1])
        y = sb("y", [128, J, H, DH])
        yT = sb("yT", [128, T])
        xt = [sb(f"xt{p}", [128, J, D]) for p in range(2)]
        xr = [sb(f"xr{p}", [128, J, D]) for p in range(2)]
        xn = [sb(f"xn{p}", [128, J, D]) for p in range(2)]
        xnT = [sb(f"xnT{p}", [128, T + 1]) for p in range(2)]
        stats = sb("stats", [128, J, 6])
        mv = sb("mv", [128, J, 2])
        std = sb("std", [128, J])
        rstd = sb("rstd", [128, J])
        den = sb("den", [128, J, H])
        rden = sb("rden", [128, J, H])
        t1 = [sb(f"t1{c}", [128, T]) for c in range(2)]
        t2 = [sb(f"t2{c}", [128, T]) for c in range(2)]
        ee = [sb(f"ee{c}", [128, T]) for c in range(2)]
        hr = [sb(f"hr{c}", [128, 512]) for c in range(2)]
        hT = sb("hT", [128, 2, NB, T // 2])

        lg = sb("lg", [128, J, E])
        lmax = sb("lmax", [128, J])
        pr = sb("pr", [128, J, E])
        psum_ = sb("psum_", [128, J])
        gt = sb("gt", [128, J, E, E])
        eq = sb("eq", [128, J, E, E])
        order = sb("order", [128, J, E])
        pick = sb("pick", [128, 2, J, E])
        pickb = sb("pickb", [128, J, E], BF16)
        prod = sb("prod", [128, 2, J, E])
        p12 = sb("p12", [128, 2, J])
        wts = [sb(f"wts{p}", [128, 2, J]) for p in range(2)]
        slotf = sb("slotf", [128, 2, J])
        idx = [sb(f"idx{p}", [128, 2 * J], I32) for p in range(2)]
        fill = sb("fill", [128, E])
        pos = sb("pos", [128, J, E])
        zeros = sb("zeros", [128, GT // 128, D])
        big = P[0][:, :, :].rearrange("p u t -> p (u t)")[:, 0:3 * E * NTILES].rearrange("p (k e t) -> p k e t", k=3, e=E)
        count = sb("count", [128, E])
        ntile = sb("ntile", [128, 3, E])
        tab = sb("tab", [128, 2 * NTILES + E], I32)
        tabf = sb("tabf", [128, 2, NTILES])
        idx_all = sb("idx_all", [128, B * 2 * J], I32)
        moved = sb("moved", [128, B * 2 * J])
        slot_all = P[0][:, UNITS - 3, 0:B * 2 * J]
        above = P[0][:, UNITS - 2:UNITS, :].rearrange("p u t -> p (u t)")[:, 0:B * 2 * J * (E - 1)].rearrange("p (k e) -> p k e", e=E - 1)

        spare = P[1][:, :, :].rearrange("p u t -> p (u t)")
        wfc = [spare[:, k * FF:(k + 1) * FF] for k in range(TB)]
        wpj = [spare[:, (TB + k) * FF:(TB + k + 1) * FF].rearrange("p (k d) -> p k d", k=NB) for k in range(TB)]
        xg, yg = ([P[0][:, k, i * GT:(i + 1) * GT].rearrange("p (c d) -> p c d", c=GT // 128) for k in range(TB)] for i in range(2))
        xgT = [P[0][:, TB + k, 0:GT] for k in range(2)]

        ya = [hT[:, p, :, :].rearrange("p k t -> p (k t)").rearrange("p (k d) -> p k d", d=D) for p in range(2)]
        nmax = sb("nmax", [128, J, H])
        shift = sb("shift", [H, 2, T], BF16)
        fhn = [sb(f"fhn{k}", [128, J, H]) for k in range(8)]
        alpha = sb("alpha", [128, 1])
        rdamp = sb("rdamp", [128, 1])
        one_b = sb("one_b", [128, 1])
        five = sb("five", [128, 1])

        consts_loaded, zeroed, ready_consts = sem("consts_loaded"), sem("zeroed"), sem("ready_consts")
        dummy_zeroed = sem("dummy_zeroed")
        x_loaded = [sem(f"x_loaded{p}") for p in range(2)]
        xr_loaded = [sem(f"xr_loaded{p}") for p in range(2)]
        ln_stats, ln_mean, ln_std, ln_rstd, xn_ready = (sem(s) for s in ("ln_stats", "ln_mean", "ln_std", "ln_rstd", "xn_ready"))
        xnT_ps, xnT_sb = sem("xnT_ps"), sem("xnT_sb")
        qk_ps, qkp_ps = sem("qk_ps"), sem("qkp_ps")
        rot_cos, rot_sin, rot, rot_min, rot_exp, phi = (sem(s) for s in ("rot_cos", "rot_sin", "rot", "rot_min", "rot_exp", "phi"))
        hi_part, res_part, mid_part, lo_part = (sem(s) for s in ("hi_part", "res_part", "mid_part", "lo_part"))
        parts_stored = [sem(f"parts_stored{c}") for c in range(2)]
        qk_loaded = [sem(f"qk_loaded{p}") for p in range(2)]
        v_ps, v_sb, logits = sem("v_ps"), sem("v_sb"), sem("logits")
        router_in, router_exp, router_step, picked = (sem(s) for s in ("router_in", "router_exp", "router_step", "picked"))
        prefix_ps, prefix_read, slots_step, slots_ready = (sem(s) for s in ("prefix_ps", "prefix_read", "slots_step", "slots_ready"))
        scattered = [sem(f"scattered{p}") for p in range(2)]
        route_stored = [sem(f"route_stored{p}") for p in range(2)]
        s_ps, s_sb, masked, pv_done = sem("s_ps"), sem("s_sb"), sem("masked"), sem("pv_done")
        oT_sb, oTT_ps, y_sb = sem("oT_sb"), sem("oTT_ps"), sem("y_sb")
        norm_step, y_ready, yT_ps, yT_sb = sem("norm_step"), sem("y_ready"), sem("yT_ps"), sem("yT_sb")
        fc_ps, h_relu, h_sq, proj_ps, xa_ready = (sem(s) for s in ("fc_ps", "h_relu", "h_sq", "proj_ps", "xa_ready"))
        xa_stored = [sem(f"xa_stored{p}") for p in range(2)]
        plan_step, plan_ready, pad_zeroed = sem("plan_step"), sem("plan_ready"), sem("pad_zeroed")
        slots_loaded, rows_ready, rows_stored = sem("slots_loaded"), sem("rows_ready"), sem("rows_stored")
        xg_loaded = [sem(f"xg_loaded{p}") for p in range(TB)]
        w_loaded = [sem(f"w_loaded{p}") for p in range(TB)]
        xgT_ps, xgT_sb, efc_ps, e_relu, e_sq, ey_ps, ey_sb = (
            sem(s) for s in ("xgT_ps", "xgT_sb", "efc_ps", "e_relu", "e_sq", "ey_ps", "ey_sb"))
        ys_stored = [sem(f"ys_stored{p}") for p in range(TB)]
        route_loaded = [sem(f"route_loaded{p}") for p in range(2)]
        xa_loaded = [sem(f"xa_loaded{p}") for p in range(2)]
        gathered = [sem(f"gathered{p}") for p in range(2)]
        summed, x1_ready = sem("summed"), sem("x1_ready")
        half_loaded = [[sem(f"half{h}_loaded{p}") for h in range(2)] for p in range(2)]
        max_ps, max_read, maxT_ps, shift_hi, shift_lo = (sem(s) for s in ("max_ps", "max_read", "maxT_ps", "shift_hi", "shift_lo"))
        shift_stored, shift_loaded = [[sem(f"shift_{w}{p}") for p in range(2)] for w in ("stored", "loaded")]
        v2_ps, v2_sb = sem("v2_ps"), sem("v2_sb")
        mixed, k_ps, k_relu, k_sq, r_ps, r_tanh, kv_ps, gated = (
            sem(s) for s in ("mixed", "k_ps", "k_relu", "k_sq", "r_ps", "r_tanh", "kv_ps", "gated"))
        res_ready, res_stored = sem("res_ready"), [sem(f"res_stored{p}") for p in range(2)]
        res_loaded = [sem(f"res_loaded{p}") for p in range(2)]
        fhn_step, fhn_stim, fhn_gate, fhn_resp, fhn_sig = (sem(s) for s in ("fhn_step", "fhn_stim", "fhn_gate", "fhn_resp", "fhn_sig"))
        proj2_ps, out_ready, out_stored = sem("proj2_ps"), sem("out_ready"), [sem(f"out_stored{p}") for p in range(2)]
        setup2 = sem("setup2")

        block = ctx.enter_context(nc.Block())

        HALVES = B // 2
        L2 = B
        AFTER = Turn(HALVES, 0)

        def over_batches(eng, body):
            for p in range(2):
                body(Turn(0, p), p == 0, False)
            with eng.Fori(1, HALVES - 1) as i:
                for p in range(2):
                    body(Turn(i, p), False, False)
            for p in range(2):
                body(Turn(HALVES - 1, p), False, p == 1)

        def value(eng, v):
            return v if isinstance(v, int) else eng.snap(eng.to_reg(v))

        def early(b, d):
            return b.less(d)

        def within(b):
            return b.known() is None or L2 <= b.known() < L2 + B

        def over_layer2(eng, body):
            for k in range(-2, 2):
                body(Turn(HALVES, 0) + k)
            with eng.Fori(HALVES + 1, 2 * HALVES - 2) as i:
                for p in range(2):
                    body(Turn(i, p))
            for k in range(-4, 1):
                body(Turn(2 * HALVES, 0) + k)

        def over_tiles(eng, body):
            for p in range(TB):
                body(Turn(0, p, TB))
            with eng.Fori(1, NTILES // TB - 1) as i:
                for p in range(TB):
                    body(Turn(i, p, TB))
            for p in range(TB):
                body(Turn(NTILES // TB - 1, p, TB))

        def row(b):
            return bass.ds(b.hi * 2 + b.p, 1)

        def row2(b):
            return bass.ds(b.hi * 2 + (b.p - L2), 1)

        @block.sync
        def _(sp):
            loads = [(wqk, io["wqk"]), (wvr, io["wvr"]), (wo, io["wo"]), (sfc, io["fc"][E]), (spj, io["proj"][E]),
                     (rope, io["rope"]), (tri, io["tri"]), (ident, io["ident"]), (before, io["before"]),
                     (lower, io["lower"]), (incl, io["incl"]), (ebase, io["ebase"]), (tiles, io["tiles"]), (steps, io["steps"]),
                     (wqkv2, io["wqkv2"]), (wo2, io["wo2"]), (wrkv, io["wrkv"]), (mu, io["mu"]), (abd, io["abd"])]

            def load_x(n):
                if not early(n, 2):
                    sp.wait_ge(xn_ready, (n + -2).at(J, J))
                sp.dma_start(xt[n.p][:, :, :], x_d[bass.ds(n.hi * 2 + n.p, 1)].rearrange("b p j d -> p (b j) d")).then_inc(x_loaded[n.p], 16)

            load_x(Turn(0, 0))
            for t, src in loads:
                ap = t[tuple(slice(None) for _ in t.shape)]
                sp.dma_start(ap, src).then_inc(consts_loaded, 16)
            for p in range(2):
                sp.dma_start(QT[p][HALF0:SHIFT0, :, :], io["half_q"]).then_inc(consts_loaded, 16)
                sp.dma_start(KT[p][HALF0:SROWS, :, :], io["half_k"]).then_inc(consts_loaded, 16)
            load_x(Turn(0, 1))
            sp.wait_ge(zeroed, 1)
            for k in range(SPARE):
                sp.dma_start(xs_d[DUMMY + k * GT:DUMMY + (k + 1) * GT, :].rearrange("(c p) d -> p c d", p=128),
                             zeros[:, :, :]).then_inc(dummy_zeroed, 16)

            def store_parts(n):
                copied = value(sp, n.own(16 * QK_LOADS, 0))
                split_ = [value(sp, n.at(2, c + 1)) for c in range(2)]
                for c in range(2):
                    sp.wait_ge(lo_part, split_[c])
                    if not early(n, 2):
                        sp.wait_ge(qk_loaded[n.p], copied)
                    sp.dma_start(parts_d[n.p, c].rearrange("a p t -> p a t"), parts[c][:, :, :]).then_inc(parts_stored[c], 16)

            def load_parts(n):
                stored = value(sp, n.at(16, 16))
                if not early(n, 2):
                    sp.wait_ge(s_ps, (n + -1).at(PASS, 0))
                for c, dst in ((0, QT), (1, KT)):
                    sp.wait_ge(parts_stored[c], stored)
                    for k in range(NPROD):
                        part = k // 3 if c == 0 else k % 3
                        sp.dma_start(dst[n.p][k * DH:(k + 1) * DH, :, :],
                                     parts_d[n.p, c, part].rearrange("(h d) t -> d h t", d=DH)).then_inc(qk_loaded[n.p], 16)

            def store_route(n):
                sp.wait_ge(slots_ready, n.at(1, 1))
                sp.dma_start(wts_d[bass.ds(n.hi * 2 + n.p, 1)].rearrange("b p k -> p (b k)"),
                             wts[n.p][:, :, :].rearrange("p c j -> p (c j)")).then_inc(route_stored[n.p], 16)
                sp.dma_start(slot_d[bass.ds(n.hi * 2 + n.p, 1)].rearrange("b p k -> p (b k)"),
                             idx[n.p][:, :]).then_inc(route_stored[n.p], 16)

            def load_xr(b):
                if not early(b, 2):
                    sp.wait_ge(xa_stored[b.p], b.own(16, 0))
                sp.dma_start(xr[b.p][:, :, :], x_d[bass.ds(b.hi * 2 + b.p, 1)].rearrange("b p j d -> p (b j) d")).then_inc(xr_loaded[b.p], 16)

            def store_xa(b):
                sp.wait_ge(xa_ready, b.at(1, 1))
                sp.dma_start(xa_d[bass.ds(b.hi * 2 + b.p, 1)].rearrange("b p j d -> p (b j) d"), xr[b.p][:, :, :]).then_inc(xa_stored[b.p], 16)

            def body(b, first, last):
                if not (b.known() is not None and b.known() + 2 >= B):
                    load_x(b + 2)
                if not first:
                    store_xa(b + -1)
                load_xr(b)
                if not last:
                    store_parts(b + 1)
                    load_parts(b + 1)
                    store_route(b + 1)

            store_parts(Turn(0, 0))
            load_parts(Turn(0, 0))
            store_route(Turn(0, 0))
            over_batches(sp, body)
            store_xa(AFTER + -1)
            for p in range(2):
                sp.wait_ge(xa_stored[p], 16 * HALVES)
                sp.wait_ge(route_stored[p], 32 * HALVES)
                sp.wait_ge(scattered[p], 16 * 2 * J * HALVES)
            sp.dma_start(idx_all[:, :].rearrange("p (b k) -> p b k", b=B), slot_d.rearrange("b p k -> p b k")).then_inc(slots_loaded, 16)
            sp.wait_ge(plan_ready, 1)
            for e in range(E):
                k = 2 * NTILES + e
                first_free = sp.value_load(tab[0:1, k:k + 1], min_val=0, max_val=NROWS - GT)
                sp.dma_start(xs_d[bass.ds(first_free, GT), :].rearrange("(c p) d -> p c d", p=128), zeros[:, :, :]).then_inc(pad_zeroed, 16)
            sp.wait_ge(pad_zeroed, 16 * E)
            sp.wait_ge(dummy_zeroed, 16 * SPARE)
            sp.wait_ge(rows_ready, 1)
            sp.dma_start(idx_d.rearrange("b p k -> p b k"), idx_all[:, :].rearrange("p (b k) -> p b k", b=B)).then_inc(rows_stored, 16)

            def load_tile(t):
                at = t.hi * TB + t.p
                first_row = sp.value_load(tab[0:1, bass.ds(at, 1)], min_val=0, max_val=NROWS - GT)
                expert = sp.value_load(tab[0:1, bass.ds(at + NTILES, 1)], min_val=0, max_val=E - 1)
                if not t.less(TB):
                    sp.wait_ge(xgT_ps, t.at(1, 1 - TB))
                sp.dma_start(xg[t.p], xs_d[bass.ds(first_row, GT), :].rearrange("(c p) d -> p c d", p=128)).then_inc(xg_loaded[t.p], 16)
                if not t.less(TB):
                    sp.wait_ge(ey_ps, t.at(1, 1 - TB))
                sp.dma_start(wfc[t.p], io["fc"][bass.ds(expert, 1)].rearrange("e p f -> p (e f)")).then_inc(w_loaded[t.p], 16)
                sp.dma_start(wpj[t.p], io["proj"][bass.ds(expert, 1)].rearrange("e p k d -> p (e k) d")).then_inc(w_loaded[t.p], 16)

            over_tiles(sp, load_tile)
            for p in range(TB):
                sp.wait_ge(ys_stored[p], 16 * (NTILES // TB))

            sp.wait_ge(rows_stored, 16)

            def load_route(n):
                if not n.less(L2 + 2):
                    sp.wait_ge(x1_ready, (n + -1).at(J, -J * L2))
                sp.dma_start(wts[n.p][:, :, :].rearrange("p c j -> p (c j)"), wts_d[row2(n)].rearrange("b p k -> p (b k)")).then_inc(route_loaded[n.p], 16)
                sp.dma_start(idx[n.p][:, :], idx_d[row2(n)].rearrange("b p k -> p (b k)")).then_inc(route_loaded[n.p], 16)

            def load_xa(n):
                if not n.less(L2 + 2):
                    sp.wait_ge(res_stored[n.p], n.own(16, -16 * HALVES))
                sp.dma_start(xt[n.p][:, :, :], xa_d[row2(n)].rearrange("b p j d -> p (b j) d")).then_inc(xa_loaded[n.p], 16)

            def load_half(n, h):
                stored = value(sp, n.at(16, 16))
                if not n.less(L2 + 2):
                    sp.wait_ge(s_ps, (n + -2).at(PASS, (h + 1) * PASS // 2))
                hs = slice(h * H // 2, (h + 1) * H // 2)
                for c, dst in ((0, QT), (1, KT)):
                    sp.wait_ge(parts_stored[c], stored)
                    for k in range(NPROD):
                        part = k // 3 if c == 0 else k % 3
                        sp.dma_start(dst[n.p][k * DH:(k + 1) * DH, hs, :],
                                     parts_d[n.p, c, part].rearrange("(h d) t -> d h t", d=DH)[:, hs, :]).then_inc(half_loaded[n.p][h], 16)

            def store_parts2(n):
                copied = value(sp, n.own(16 * QK_LOADS, -16 * QK_LOADS * HALVES))
                split_ = [value(sp, n.at(2, c + 1)) for c in range(2)]
                for c in range(2):
                    sp.wait_ge(lo_part, split_[c])
                    for h in range(2):
                        if not n.less(L2 + 2):
                            sp.wait_ge(half_loaded[n.p][h], copied)
                    sp.dma_start(parts_d[n.p, c].rearrange("a p t -> p a t"), parts[c][:, :, :]).then_inc(parts_stored[c], 16)

            def store_res(n):
                sp.wait_ge(res_ready, n.at(1, 1 - L2))
                sp.dma_start(res_d[row2(n)].rearrange("b p j d -> p (b j) d"), xt[n.p][:, :, :]).then_inc(res_stored[n.p], 16)

            def load_res(n):
                left = value(sp, n.own(16, -16 * HALVES))
                sp.wait_ge(res_stored[n.p], n.own(16, 16 - 16 * HALVES))
                if not n.less(L2 + 2):
                    sp.wait_ge(out_stored[n.p], left)
                sp.dma_start(xr[n.p][:, :, :], res_d[row2(n)].rearrange("b p j d -> p (b j) d")).then_inc(res_loaded[n.p], 16)

            def body2(b):
                if b.known() == L2 - 2:
                    load_route(b + 2)
                    load_xa(b + 2)
                if within(b + 3):
                    load_route(b + 3)
                if b.known() == L2 - 2:
                    load_xa(b + 3)
                if within(b):
                    load_res(b)
                if within(b + 2):
                    store_parts2(b + 2)
                    load_half(b + 2, 0)
                    load_half(b + 2, 1)
                if within(b + 1):
                    store_res(b + 1)
                if within(b + 3) and b.known() != L2 - 2:
                    load_xa(b + 3)

            over_layer2(sp, body2)
            for p in range(2):
                sp.wait_ge(out_stored[p], 16 * HALVES)
                sp.wait_ge(res_stored[p], 16 * HALVES)
                sp.wait_ge(shift_stored[p], 16 * HALVES)

        @block.gpsimd
        def _(pool):
            for p in range(2):
                nc.gpsimd.memset(V[p][:, :, :, :], 0.0).then_inc(ready_consts, 1)
                nc.gpsimd.memset(xnT[p][:, 0:1], 0.0).then_inc(ready_consts, 1)
            nc.gpsimd.memset(eps[:, :], LN_EPS).then_inc(ready_consts, 1)
            pool.wait_ge(ready_consts, 5)
            for p in range(2):
                nc.gpsimd.memset(V[p][:, :, :, DH:DH + 1], 1.0).then_inc(ready_consts, 1)
            pool.wait_ge(consts_loaded, 16 * 23)

            def mask_pair(b, s, a):
                buf = P[s % 2]
                k0 = s * UNITS + 5 * a

                def diag(out, n):
                    nc.gpsimd.tensor_tensor(out, out, tri[:, 0:n, :], ALU.mult).then_inc(masked, 1)

                pool.wait_ge(s_sb, b.at(PASS, k0 + 2))
                diag(buf[:, 5 * a:5 * a + 2, 0:128], 2)
                pool.wait_ge(s_sb, b.at(PASS, k0 + 3))
                diag(buf[:, 5 * a + 2, :].rearrange("p (k c) -> p k c", c=128)[:, 0:4:3, :], 2)
                pool.wait_ge(s_sb, b.at(PASS, k0 + 4))
                diag(buf[:, 5 * a + 3, :].rearrange("p (k c) -> p k c", c=128)[:, 0:4:3, :], 2)
                pool.wait_ge(s_sb, b.at(PASS, k0 + 5))
                diag(buf[:, 5 * a + 4, :].rearrange("p (k c) -> p k c", c=128)[:, 0:4:2, :], 2)

            def scatter(n):
                count_ = value(pool, n.at(1, 1))
                pool.wait_ge(consts_loaded, 16 * 23)
                pool.wait_ge(slots_ready, count_)
                for c in range(2):
                    for j in range(J):
                        k = c * J + j
                        nc.gpsimd.indirect_dma_start(
                            xs_d[:, :], bass.IndirectOffsetOnAxis(ap=idx[n.p][:, k:k + 1], axis=0),
                            xn[n.p][:, j, :], None).then_inc(scattered[n.p], 16)

            def body(b, first, last):
                for s in range(SHEETS):
                    for a in range(2):
                        mask_pair(b, s, a)
                if not last:
                    scatter(b + 1)

            scatter(Turn(0, 0))
            over_batches(pool, body)

            def store_tile(t):
                count_ = value(pool, t.at(1, 1))
                pool.wait_ge(consts_loaded, 16 * 23)
                pool.wait_ge(ey_sb, count_)
                pool.dma_start(ys_d[bass.ds((t.hi * TB + t.p) * GT, GT), :].rearrange("(c p) d -> p c d", p=128), yg[t.p]).then_inc(ys_stored[t.p], 16)

            over_tiles(pool, store_tile)
            for p in range(TB):
                pool.wait_ge(ys_stored[p], 16 * (NTILES // TB))

            def gather(n):
                count_, summed_ = value(pool, n.own(32, 32 - 32 * HALVES)), value(pool, (n + -1).at(J, -J * L2))
                pool.wait_ge(rows_stored, 16)
                pool.wait_ge(route_loaded[n.p], count_)
                if not n.less(L2 + 2):
                    pool.wait_ge(x1_ready, summed_)
                for k in range(2 * J):
                    nc.gpsimd.indirect_dma_start(ya[n.p][:, k, :], None, ys_d[:, :],
                                                 bass.IndirectOffsetOnAxis(ap=idx[n.p][:, k:k + 1], axis=0)).then_inc(gathered[n.p], 16)

            def shift_rows(n):
                count_ = value(pool, n.at(1, 1 - L2))
                pool.wait_ge(rows_stored, 16)
                pool.wait_ge(shift_lo, count_)
                pool.wait_ge(shift_hi, n.at(1, 1 - L2))
                pool.dma_start(shift_d[n.p].rearrange("a h t -> h a t"), shift[:, :, :]).then_inc(shift_stored[n.p], 16)
                pool.wait_ge(shift_stored[n.p], n.own(16, 16 - 16 * HALVES))
                read = value(pool, (n + -1).at(PASS, 0))
                pool.wait_ge(rows_stored, 16)
                if not n.less(L2 + 2):
                    pool.wait_ge(s_ps, read)
                pool.dma_start(QT[n.p][SHIFT0:SROWS, :, :], shift_d[n.p]).then_inc(shift_loaded[n.p], 16)

            def store_out(b):
                count_ = value(pool, b.at(1, 1 - L2))
                pool.wait_ge(rows_stored, 16)
                pool.wait_ge(out_ready, count_)
                pool.dma_start(out_d[row2(b)].rearrange("b p j d -> p (b j) d"), xr[b.p][:, :, :]).then_inc(out_stored[b.p], 16)

            def body2(b):
                if b.known() == L2 - 2:
                    gather(b + 2)
                if within(b + 3):
                    gather(b + 3)
                if within(b + -1):
                    store_out(b + -1)
                if within(b + 1):
                    shift_rows(b + 1)

            over_layer2(pool, body2)

        @block.scalar
        def _(act):
            act.wait_ge(ready_consts, 7)
            act.wait_ge(consts_loaded, 16 * 23)

            def ln_sqrt(n):
                act.wait_ge(ln_mean, n.at(J, J))
                nc.scalar.activation(std[:, :], mv[:, :, 1], ACT.Sqrt, bias=eps[:, 0:1]).then_inc(ln_std, 1)

            def evac_xnT(n):
                act.wait_ge(xnT_ps, n.at(1, 1))
                nc.scalar.copy(xnT[n.p][:, 1:T + 1], W6[:, :]).then_inc(xnT_sb, 1)

            def exps(n):
                for c in range(2):
                    act.wait_ge(rot_min, n.at(2, c + 1))
                    nc.scalar.activation(ee[c][:, :], t2[c][:, :], ACT.Exp).then_inc(rot_exp, 1)

            def hi(n):
                for c in range(2):
                    act.wait_ge(phi, n.at(2, c + 1))
                    if not early(n, 1):
                        act.wait_ge(parts_stored[c], n.at(16, 0))
                    nc.scalar.copy(parts[c][:, 0, :], t2[c][:, :]).then_inc(hi_part, 1)

            def mid(n):
                for c in range(2):
                    act.wait_ge(res_part, n.at(2, c + 1))
                    nc.scalar.copy(parts[c][:, 1, :], t1[c][:, :]).then_inc(mid_part, 1)

            def evac_v(n):
                for k, w in enumerate((W5, W6)):
                    act.wait_ge(v_ps, n.at(2, k + 1))
                    nc.scalar.copy(V[n.p][:, 2 * k:2 * k + 2, :, 0:DH],
                                   w[:, 0:2 * (128 + E)].rearrange("p (j c) -> p j c", j=2)[:, :, 0:128]
                                   .rearrange("p j (h d) -> p j h d", d=DH)).then_inc(v_sb, 1)

            def exp_router(n):
                act.wait_ge(router_in, n.at(1, 1))
                nc.scalar.activation(pr[:, :, :], lg[:, :, :], ACT.Exp).then_inc(router_exp, 1)

            def evac_oT(b, s):
                act.wait_ge(pv_done, b.at(SHEETS, s + 1))
                if not (early(b, 1) and s < 2):
                    act.wait_ge(oTT_ps, b.at(SHEETS, s - 1))
                nc.scalar.copy(oT[s % 2][:, :], OT[:, :]).then_inc(oT_sb, 1)

            def evac_yT(b):
                act.wait_ge(yT_ps, b.at(1, 1))
                nc.scalar.copy(yT[:, :], W6[:, :]).then_inc(yT_sb, 1)

            def relu_h(b, k):
                act.wait_ge(fc_ps, b.at(NB, k + 1))
                if not (early(b, 1) and k < 2):
                    act.wait_ge(h_sq, b.at(NB, k - 1))
                nc.scalar.activation(hr[k % 2][:, :], W5[:, :], ACT.Relu).then_inc(h_relu, 1)

            def evac_s(b, s, u):
                k = s * UNITS + u
                if u == 0 and not (early(b, 1) and s < 2):
                    act.wait_ge(pv_done, b.at(SHEETS, s - 1))
                act.wait_ge(s_ps, b.at(PASS, k + 1))
                nc.scalar.copy(P[s % 2][:, u, :], bank[k % 4][:, :]).then_inc(s_sb, 1)

            def front(n):
                exps(n)
                hi(n)
                mid(n)
                evac_v(n)
                exp_router(n)

            def body(b, first, last):
                for s in range(SHEETS):
                    for u in range(UNITS):
                        at = (s, u)
                        if at == (0, 0) and not first:
                            evac_oT(b + -1, 3)
                        if at == (0, 8) and not first:
                            evac_yT(b + -1)
                        if at == (0, 4) and not last:
                            evac_xnT(b + 1)
                        if at == (1, 5) and not last:
                            exps(b + 1)
                        if at == (2, 4) and not last:
                            hi(b + 1)
                        if at == (2, 7) and not last:
                            mid(b + 1)
                        if at == (3, 4) and not last:
                            evac_v(b + 1)
                        if at == (3, 9) and not last:
                            exp_router(b + 1)
                        if at in ((2, 2), (3, 2)):
                            evac_oT(b, s - 2)
                        evac_s(b, s, u)
                evac_oT(b, 2)
                for k in range(NB):
                    relu_h(b, k)
                if not (b.known() is not None and b.known() + 2 >= B):
                    ln_sqrt(b + 2)

            ln_sqrt(Turn(0, 0))
            evac_xnT(Turn(0, 0))
            front(Turn(0, 0))
            ln_sqrt(Turn(0, 1))
            over_batches(act, body)
            evac_oT(AFTER + -1, 3)
            evac_yT(AFTER + -1)

            def tile(t):
                act.wait_ge(xgT_ps, t.at(1, 1))
                if not t.less(2):
                    act.wait_ge(efc_ps, (t + -1).at(2, 0))
                nc.scalar.copy(xgT[t.p % 2], bank[t.p % 2][:, 0:GT]).then_inc(xgT_sb, 1)
                for k in range(2):
                    act.wait_ge(efc_ps, t.at(2, k + 1))
                    if not t.less(1):
                        act.wait_ge(e_sq, t.at(2, k - 1))
                    nc.scalar.activation(hr[k][:, :], bank[2 + 2 * (t.p % 2) + k][:, :], ACT.Relu).then_inc(e_relu, 1)

            over_tiles(act, tile)

            def hi2(n):
                for c, w in enumerate((W5, W6)):
                    act.wait_ge(qk_ps, n.at(2, c + 1))
                    act.wait_ge(parts_stored[c], n.at(16, 0))
                    nc.scalar.copy(parts[c][:, 0, :], w[:, :]).then_inc(hi_part, 1)

            def evac_v2(n):
                act.wait_ge(v2_ps, n.at(1, 1 - L2))
                nc.scalar.copy(V[n.p][:, :, :, 0:DH], W5[:, :].rearrange("p (j h d) -> p j h d", j=J, d=DH)).then_inc(v2_sb, 1)

            def shift_high(n):
                act.wait_ge(maxT_ps, n.at(1, 1 - L2))
                if not n.less(L2 + 1):
                    act.wait_ge(shift_stored[1 - n.p], (n + -1).own(16, 16 - 16 * HALVES))
                nc.scalar.copy(shift[:, 0, :], W6[0:H, :]).then_inc(shift_hi, 1)

            def exp_scores(b, s, u):
                k = s * UNITS + u
                if u == 0 and not (b.less(L2 + 1) and s < 2):
                    act.wait_ge(pv_done, b.at(SHEETS, s - 1))
                act.wait_ge(s_ps, b.at(PASS, k + 1))
                nc.scalar.activation(P[s % 2][:, u, :], bank[k % 2][:, :], ACT.Exp, scale=float(DH) ** -0.5).then_inc(s_sb, 1)

            def relu_k(n):
                act.wait_ge(k_ps, n.at(1, 1 - L2))
                nc.scalar.activation(hr[0][:, :], W5[:, :], ACT.Relu).then_inc(k_relu, 1)

            def tanh_r(n):
                act.wait_ge(r_ps, n.at(1, 1 - L2))
                nc.scalar.activation(ee[0][:, :], W6[:, :], ACT.Tanh, scale=0.5).then_inc(r_tanh, 1)

            def exp_gate(b):
                act.wait_ge(fhn_stim, b.at(1, 1 - L2))
                nc.scalar.activation(fhn[3][:, :, :], fhn[0][:, :, :], ACT.Exp, bias=five[:, 0:1], scale=-10.0).then_inc(fhn_gate, 1)

            def exp_resp(b):
                act.wait_ge(fhn_resp, b.at(1, 1 - L2))
                nc.scalar.activation(fhn[3][:, :, :], fhn[2][:, :, :], ACT.Exp, scale=-1.0).then_inc(fhn_sig, 1)

            def body2(b):
                core, front, after, before_ = within(b), within(b + 2), within(b + 1), within(b + -1)
                for s in range(SHEETS):
                    for u in range(UNITS):
                        at = (s, u)
                        if at == (0, 0) and before_:
                            evac_oT(b + -1, 3)
                        if at == (0, 8) and front:
                            ln_sqrt(b + 2)
                        if at == (1, 3) and front:
                            evac_xnT(b + 2)
                        if at == (1, 4) and before_:
                            exp_gate(b + -1)
                        if at == (2, 1) and front:
                            hi2(b + 2)
                        if at == (2, 2) and core:
                            evac_oT(b, 0)
                        if at == (2, 4) and front:
                            mid(b + 2)
                        if at == (2, 6) and before_:
                            exp_resp(b + -1)
                        if at == (2, 9) and after:
                            evac_v2(b + 1)
                        if at == (3, 2) and core:
                            evac_oT(b, 1)
                        if at == (3, 4) and before_:
                            evac_yT(b + -1)
                        if core:
                            exp_scores(b, s, u)
                if after:
                    shift_high(b + 1)
                if core:
                    evac_oT(b, 2)
                if after:
                    relu_k(b + 1)
                    tanh_r(b + 1)

            over_layer2(act, body2)

        @block.vector
        def _(dve):
            nc.vector.memset(zeros[:, :, :], 0.0).then_inc(zeroed, 1)

            LR = 5

            def ln_moments(n):
                for j in range(J):
                    nc.vector.bn_stats(stats[:, j, :], xt[n.p][:, j, :]).then_inc(ln_stats, 1)
                measured = value(dve, n.at(J, J))
                dve.wait_ge(ready_consts, 7)
                dve.wait_ge(ln_stats, measured)
                for j in range(J):
                    nc.vector.bn_aggr(mv[:, j, :], stats[:, j, :]).then_inc(ln_mean, 1)

            def ln(n, first_layer=True):
                dve.wait_ge(ln_std, n.at(1, 1))
                nc.vector.reciprocal(rstd[:, :], std[:, :]).then_inc(ln_rstd, 1)
                dve.wait_ge(ln_rstd, n.at(LR, 1))
                nc.vector.tensor_tensor(std[:, :], rstd[:, :], rstd[:, :], ALU.mult).then_inc(ln_rstd, 1)
                dve.wait_ge(ln_rstd, n.at(LR, 2))
                nc.vector.scalar_tensor_tensor(out=std[:, :], in0=mv[:, :, 1], scalar=LN_EPS, in1=std[:, :],
                                               op0=ALU.add, op1=ALU.mult).then_inc(ln_rstd, 1)
                dve.wait_ge(ln_rstd, n.at(LR, 3))
                nc.vector.tensor_scalar(std[:, :], std[:, :], -0.5, 1.5, ALU.mult, ALU.add).then_inc(ln_rstd, 1)
                dve.wait_ge(ln_rstd, n.at(LR, 4))
                nc.vector.tensor_tensor(rstd[:, :], rstd[:, :], std[:, :], ALU.mult).then_inc(ln_rstd, 1)
                dve.wait_ge(ln_rstd, n.at(LR, LR))
                if not early(n, 2) and first_layer:
                    dve.wait_ge(scattered[n.p], n.own(16 * 2 * J, 0))
                for j in range(J):
                    nc.vector.tensor_scalar(xn[n.p][:, j, :], xt[n.p][:, j, :], mv[:, j, 0:1], rstd[:, j:j + 1],
                                            ALU.subtract, ALU.mult).then_inc(xn_ready, 1)

            def rotate(n):
                for c in range(2):
                    dve.wait_ge(qk_ps, n.at(2, c + 1))
                    nc.vector.tensor_tensor(t1[c][:, :], W5[:, :], rope[:, 0, :], ALU.mult).then_inc(rot_cos, 1)
                    dve.wait_ge(qkp_ps, n.at(2, c + 1))
                    nc.vector.tensor_tensor(t2[c][:, :], W6[:, :], rope[:, 1, :], ALU.mult).then_inc(rot_sin, 1)
                    dve.wait_ge(rot_cos, n.at(2, c + 1))
                    dve.wait_ge(rot_sin, n.at(2, c + 1))
                    nc.vector.tensor_tensor(t1[c][:, :], t1[c][:, :], t2[c][:, :], ALU.add).then_inc(rot, 1)
                    dve.wait_ge(rot, n.at(2, c + 1))
                    nc.vector.tensor_scalar(t2[c][:, :], t1[c][:, :], 0.0, None, ALU.min).then_inc(rot_min, 1)

            def feature(n):
                for c in range(2):
                    dve.wait_ge(rot_exp, n.at(2, c + 1))
                    nc.vector.scalar_tensor_tensor(out=t2[c][:, :], in0=t1[c][:, :], scalar=0.0, in1=ee[c][:, :],
                                                   op0=ALU.max, op1=ALU.add).then_inc(phi, 1)

            def split(n):
                for c in range(2):
                    dve.wait_ge(hi_part, n.at(2, c + 1))
                    dve.wait_ge(phi, n.at(2, c + 1))
                    nc.vector.tensor_tensor(t1[c][:, :], t2[c][:, :], parts[c][:, 0, :], ALU.subtract).then_inc(res_part, 1)
                for c in range(2):
                    dve.wait_ge(mid_part, n.at(2, c + 1))
                    dve.wait_ge(res_part, n.at(2, c + 1))
                    nc.vector.tensor_tensor(parts[c][:, 2, :], t1[c][:, :], parts[c][:, 1, :], ALU.subtract).then_inc(lo_part, 1)

            def logits_out(n):
                for k, w in enumerate((W5, W6)):
                    dve.wait_ge(v_sb, n.at(2, k + 1))
                    nc.vector.tensor_copy(lg[:, 2 * k:2 * k + 2, :],
                                          w[:, 0:2 * (128 + E)].rearrange("p (j c) -> p j c", j=2)[:, :, 128:]).then_inc(logits, 1)

            def router(n):
                RS = 13
                done = [0]

                def step(ins):
                    done[0] += 1
                    ins.then_inc(router_step, 1)
                    dve.wait_ge(router_step, n.at(RS, done[0]))

                dve.wait_ge(logits, n.at(2, 2))
                step(nc.vector.tensor_reduce(lmax[:, :], lg[:, :, :], AX.X, ALU.max))
                nc.vector.tensor_tensor(lg[:, :, :], lg[:, :, :], lmax[:, :].unsqueeze(2).to_broadcast([128, J, E]),
                                        ALU.subtract).then_inc(router_in, 1)
                dve.wait_ge(router_exp, n.at(1, 1))
                step(nc.vector.tensor_reduce(psum_[:, :], pr[:, :, :], AX.X, ALU.add))
                step(nc.vector.reciprocal(psum_[:, :], psum_[:, :]))
                step(nc.vector.tensor_tensor(pr[:, :, :], pr[:, :, :], psum_[:, :].unsqueeze(2).to_broadcast([128, J, E]), ALU.mult))
                other = pr[:, :, :].unsqueeze(2).to_broadcast([128, J, E, E])
                own = pr[:, :, :].unsqueeze(3).to_broadcast([128, J, E, E])
                step(nc.vector.tensor_tensor(eq[:, :, :, :], other, own, ALU.is_equal))
                step(nc.vector.tensor_tensor(eq[:, :, :, :], eq[:, :, :, :],
                                             lower[:, :, :].unsqueeze(1).to_broadcast([128, J, E, E]), ALU.mult))
                step(nc.vector.tensor_tensor(gt[:, :, :, :], other, own, ALU.is_gt))
                step(nc.vector.tensor_tensor(gt[:, :, :, :], gt[:, :, :, :], eq[:, :, :, :], ALU.add))
                step(nc.vector.tensor_reduce(order[:, :, :], gt[:, :, :, :], AX.X, ALU.add))
                nc.vector.tensor_scalar(pickb[:, :, :], order[:, :, :], 1.5, None, ALU.is_lt).then_inc(picked, 1)
                nc.vector.tensor_scalar(pick[:, 0, :, :], order[:, :, :], 0.0, None, ALU.is_equal)
                step(nc.vector.tensor_scalar(pick[:, 1, :, :], order[:, :, :], 1.0, None, ALU.is_equal))
                step(nc.vector.tensor_tensor(prod[:, :, :, :], pick[:, :, :, :],
                                             pr[:, :, :].unsqueeze(1).to_broadcast([128, 2, J, E]), ALU.mult))
                step(nc.vector.tensor_reduce(p12[:, :, :], prod[:, :, :, :], AX.X, ALU.add))
                step(nc.vector.tensor_tensor(psum_[:, :], p12[:, 0, :], p12[:, 1, :], ALU.add))
                assert done[0] == RS

            def slots(n):
                SS = 5
                done = [0]

                def step(ins):
                    done[0] += 1
                    ins.then_inc(slots_step, 1)
                    dve.wait_ge(slots_step, n.at(SS, done[0]))

                step(nc.vector.tensor_scalar(psum_[:, :], psum_[:, :], 1e-9, None, ALU.max))
                step(nc.vector.reciprocal(psum_[:, :], psum_[:, :]))
                if not early(n, 2):
                    dve.wait_ge(route_stored[n.p], n.own(32, 0))
                    dve.wait_ge(scattered[n.p], n.own(16 * 2 * J, 0))
                nc.vector.tensor_tensor(wts[n.p][:, :, :], p12[:, :, :],
                                        psum_[:, :].unsqueeze(1).to_broadcast([128, 2, J]), ALU.mult)
                dve.wait_ge(prefix_ps, n.at(1, 1))
                if not early(n, 1):
                    dve.wait_ge(prefix_read, n.at(1, 0))
                step(nc.vector.tensor_tensor(pos[:, :, :], W6[:, 0:J * E].rearrange("p (j e) -> p j e", e=E),
                                             fill[:, :].unsqueeze(1).to_broadcast([128, J, E]), ALU.add))
                nc.vector.tensor_tensor(fill[:, :], fill[:, :], W6[:, J * E:J * E + E], ALU.add).then_inc(prefix_read, 1)
                step(nc.vector.tensor_tensor(prod[:, :, :, :], pick[:, :, :, :],
                                             pos[:, :, :].unsqueeze(1).to_broadcast([128, 2, J, E]), ALU.mult))
                step(nc.vector.tensor_reduce(slotf[:, :, :], prod[:, :, :, :], AX.X, ALU.add))
                nc.vector.tensor_copy(idx[n.p][:, :], slotf[:, :, :].rearrange("p c j -> p (c j)")).then_inc(slots_ready, 1)
                assert done[0] == SS

            def y_out(b, s):
                dve.wait_ge(oTT_ps, b.at(SHEETS, s + 1))
                nc.vector.tensor_copy(yb[:, :, G * s:G * s + G, :],
                                      W7[:, :].rearrange("p (j g c) -> p j g c", j=J, g=G)[:, :, :, 0:DH + 1]).then_inc(y_sb, 1)

            def normalise(b):
                NS = 2
                dve.wait_ge(y_sb, b.at(SHEETS, SHEETS))
                nc.vector.tensor_scalar(den[:, :, :], yb[:, :, :, DH], DEN_EPS, None, ALU.max).then_inc(norm_step, 1)
                dve.wait_ge(norm_step, b.at(NS, 1))
                nc.vector.reciprocal(rden[:, :, :], den[:, :, :]).then_inc(norm_step, 1)
                dve.wait_ge(norm_step, b.at(NS, 2))
                nc.vector.tensor_tensor(y[:, :, :, :], yb[:, :, :, 0:DH],
                                        rden[:, :, :].unsqueeze(3).to_broadcast([128, J, H, DH]), ALU.mult).then_inc(y_ready, 1)

            def square_h(b, k):
                dve.wait_ge(h_relu, b.at(NB, k + 1))
                if k == 0 and not early(b, 1):
                    dve.wait_ge(proj_ps, b.at(1, 0))
                h = hr[k % 2][:, :].rearrange("p (c t) -> p c t", c=2)
                nc.vector.tensor_tensor(hT[:, :, k, :], h, h, ALU.mult).then_inc(h_sq, 1)

            def residual(b):
                dve.wait_ge(proj_ps, b.at(1, 1))
                dve.wait_ge(xr_loaded[b.p], b.own(16, 16))
                nc.vector.tensor_tensor(xr[b.p][:, :, :], xr[b.p][:, :, :],
                                        W7[:, :].rearrange("p (j d) -> p j d", j=J), ALU.add).then_inc(xa_ready, 1)

            def front(n):
                rotate(n)
                feature(n)
                split(n)
                logits_out(n)
                router(n)
                slots(n)

            def body(b, first, last):
                if not first:
                    y_out(b + -1, 3)
                    normalise(b + -1)
                if not last:
                    rotate(b + 1)
                if not first:
                    residual(b + -1)
                if not last:
                    feature(b + 1)
                y_out(b, 0)
                if not last:
                    split(b + 1)
                    logits_out(b + 1)
                y_out(b, 1)
                if not last:
                    router(b + 1)
                y_out(b, 2)
                for k in range(NB):
                    square_h(b, k)
                if not last:
                    slots(b + 1)
                if not (b.known() is not None and b.known() + 2 >= B):
                    dve.wait_ge(x_loaded[b.p], (b + 2).own(16, 16))
                    ln_moments(b + 2)
                    ln(b + 2)

            dve.wait_ge(ready_consts, 7)
            dve.wait_ge(x_loaded[0], 16)
            ln_moments(Turn(0, 0))
            ln(Turn(0, 0))
            dve.wait_ge(consts_loaded, 16 * 23)
            nc.vector.tensor_copy(fill[:, :], ebase[:, 0, :]).then_inc(zeroed, 1)
            dve.wait_ge(zeroed, 2)
            front(Turn(0, 0))
            dve.wait_ge(x_loaded[1], 16)
            ln_moments(Turn(0, 1))
            ln(Turn(0, 1))
            over_batches(dve, body)
            y_out(AFTER + -1, 3)
            normalise(AFTER + -1)
            residual(AFTER + -1)

            planned = [0]

            def plan(ins):
                planned[0] += 1
                ins.then_inc(plan_step, 1)
                dve.wait_ge(plan_step, planned[0])

            cnt, (nt, end, start) = count[:, :], [ntile[:, k, :] for k in range(3)]
            wide = [128, E, NTILES]
            cmp = gt[:, :, :, :].rearrange("p a b c -> p (a b c)")[:, 0:E * (CAP // GT)].rearrange("p (e k) -> p e k", e=E)
            cum = eq[:, 0, :, :]
            dve.wait_ge(prefix_read, B)
            plan(nc.vector.tensor_tensor(cnt, fill[:, :], ebase[:, 0, :], ALU.subtract))
            plan(nc.vector.tensor_tensor(cmp, cnt.unsqueeze(2).to_broadcast([128, E, CAP // GT]),
                                         steps[:, :].unsqueeze(1).to_broadcast([128, E, CAP // GT]), ALU.is_gt))
            plan(nc.vector.tensor_reduce(nt, cmp, AX.X, ALU.add))
            plan(nc.vector.tensor_tensor(cum, incl[:, :, :], nt.unsqueeze(1).to_broadcast([128, E, E]), ALU.mult))
            plan(nc.vector.tensor_reduce(end, cum, AX.X, ALU.add))
            plan(nc.vector.tensor_tensor(start, end, nt, ALU.subtract))
            number = tiles[:, 0, :].unsqueeze(1).to_broadcast(wide)
            plan(nc.vector.tensor_tensor(big[:, 0, :, :], number, start.unsqueeze(2).to_broadcast(wide), ALU.is_ge))
            plan(nc.vector.tensor_tensor(big[:, 1, :, :], number, end.unsqueeze(2).to_broadcast(wide), ALU.is_lt))
            plan(nc.vector.tensor_tensor(big[:, 0, :, :], big[:, 0, :, :], big[:, 1, :, :], ALU.mult))
            plan(nc.vector.scalar_tensor_tensor(out=cnt, in0=start, scalar=float(-GT), in1=ebase[:, 0, :], op0=ALU.mult, op1=ALU.add))
            plan(nc.vector.tensor_tensor(big[:, 1, :, :], tiles[:, 1, :].unsqueeze(1).to_broadcast(wide),
                                         cnt.unsqueeze(2).to_broadcast(wide), ALU.add))
            plan(nc.vector.tensor_tensor(big[:, 1, :, :], big[:, 1, :, :], big[:, 0, :, :], ALU.mult))
            plan(nc.vector.tensor_tensor(big[:, 2, :, :], big[:, 0, :, :], ebase[:, 1, :].unsqueeze(2).to_broadcast(wide), ALU.mult))
            for k in range(2):
                plan(nc.vector.tensor_reduce(tabf[:, k, :], big[:, 1 + k, :, :].rearrange("p e t -> p t e"), AX.X, ALU.add))
            plan(nc.vector.tensor_tensor(tab[:, 0:NTILES], tabf[:, 0, :], tiles[:, 2, :], ALU.add))
            plan(nc.vector.tensor_copy(tab[:, NTILES:2 * NTILES], tabf[:, 1, :]))
            nc.vector.tensor_copy(tab[:, 2 * NTILES:], fill[:, :]).then_inc(plan_ready, 1)
            every = [128, B * 2 * J, E - 1]
            plan(nc.vector.tensor_scalar(nt, nt, float(GT), float(-REGION), ALU.mult, ALU.add))
            dve.wait_ge(slots_loaded, 16)
            plan(nc.vector.tensor_copy(slot_all, idx_all[:, :]))
            plan(nc.vector.tensor_tensor(above, slot_all.unsqueeze(2).to_broadcast(every),
                                         ebase[:, 0, 1:E].unsqueeze(1).to_broadcast(every), ALU.is_ge))
            plan(nc.vector.tensor_tensor(above, above, nt[:, 0:E - 1].unsqueeze(1).to_broadcast(every), ALU.mult))
            plan(nc.vector.tensor_reduce(moved[:, :], above, AX.X, ALU.add))
            nc.vector.tensor_tensor(idx_all[:, :], slot_all, moved[:, :], ALU.add).then_inc(rows_ready, 1)

            def square_tile(t):
                for k in range(2):
                    dve.wait_ge(e_relu, t.at(2, k + 1))
                    if k == 0 and not t.less(2):
                        dve.wait_ge(ey_ps, t.at(1, -1))
                    h = hr[k][:, :].rearrange("p (k t) -> p k t", k=2)
                    nc.vector.tensor_tensor(hT[:, t.p % 2, 2 * k:2 * k + 2, :], h, h, ALU.mult).then_inc(e_sq, 1)

            def evac_tile(t):
                dve.wait_ge(ey_ps, t.at(1, 1))
                if not t.less(TB):
                    dve.wait_ge(ys_stored[t.p], t.own(16, 0))
                nc.vector.tensor_copy(yg[t.p], bank[6 + t.p % 2][:, 0:GT].rearrange("p (c d) -> p c d", d=D)).then_inc(ey_sb, 1)

            def tile(t):
                square_tile(t)
                if not t.less(1):
                    evac_tile(t + -1)

            over_tiles(dve, tile)
            evac_tile(Turn(NTILES // TB, 0, TB) + -1)

            nc.vector.memset(five[:, :], 5.0).then_inc(setup2, 1)
            nc.vector.tensor_scalar(omu[:, :], mu[:, :], -1.0, 1.0, ALU.mult, ALU.add).then_inc(setup2, 1)
            nc.vector.tensor_scalar(alpha[:, :], abd[:, 2:3], 1.0 / TAU, None, ALU.mult).then_inc(setup2, 1)
            dve.wait_ge(setup2, 3)
            nc.vector.tensor_tensor(one_b[:, :], alpha[:, :], abd[:, 1:2], ALU.mult).then_inc(setup2, 1)
            dve.wait_ge(setup2, 4)
            nc.vector.tensor_scalar(one_b[:, :], one_b[:, :], 1.0, None, ALU.add).then_inc(setup2, 1)
            dve.wait_ge(setup2, 5)
            nc.vector.reciprocal(rdamp[:, :], one_b[:, :]).then_inc(setup2, 1)
            dve.wait_ge(setup2, 6)

            def combine(n):
                dve.wait_ge(xa_loaded[n.p], n.own(16, 16 - 16 * HALVES))
                dve.wait_ge(gathered[n.p], n.own(32 * J, 32 * J - 32 * J * HALVES))
                for c in range(2):
                    for j in range(J):
                        x = xt[n.p][:, j, :]
                        if c == 1:
                            dve.wait_ge(summed, n.at(J, j + 1 - J * L2))
                        nc.vector.scalar_tensor_tensor(out=x, in0=ya[n.p][:, c * J + j, :], scalar=wts[n.p][:, c, j:j + 1],
                                                       in1=x, op0=ALU.mult, op1=ALU.add).then_inc(x1_ready if c else summed, 1)
                dve.wait_ge(x1_ready, n.at(J, J - J * L2))

            def row_max(n, k):
                s, (j, g, nh) = k // MU, MAX_UNITS[k % MU]
                h = G * s + g
                dve.wait_ge(max_ps, n.at(MU * SHEETS, k + 1 - MU * SHEETS * L2))
                w = 128 * (j + 1)
                nc.vector.tensor_reduce(nmax[:, j, h:h + nh], bank[2 + k % 2][:, 0:nh * w].rearrange("p (h w) -> p h w", h=nh),
                                        AX.X, ALU.max, negate=True).then_inc(max_read, 1)

            def split2(n):
                for c, w in enumerate((W5, W6)):
                    dve.wait_ge(hi_part, n.at(2, c + 1))
                    nc.vector.tensor_tensor(t1[c][:, :], w[:, :], parts[c][:, 0, :], ALU.subtract).then_inc(res_part, 1)
                for c in range(2):
                    dve.wait_ge(mid_part, n.at(2, c + 1))
                    dve.wait_ge(res_part, n.at(2, c + 1))
                    nc.vector.tensor_tensor(parts[c][:, 2, :], t1[c][:, :], parts[c][:, 1, :], ALU.subtract).then_inc(lo_part, 1)

            def shift_low(n):
                dve.wait_ge(shift_hi, n.at(1, 1 - L2))
                nc.vector.tensor_tensor(shift[:, 1, :], W6[0:H, :], shift[:, 0, :], ALU.subtract).then_inc(shift_lo, 1)

            def mix(n):
                for c in range(2):
                    nc.vector.tensor_scalar(t2[c][:, :], xnT[n.p][:, 1:T + 1], mu[:, c:c + 1], None, ALU.mult).then_inc(mixed, 1)
                for c in range(2):
                    dve.wait_ge(mixed, n.at(4, 1 + c - 4 * L2))
                    nc.vector.scalar_tensor_tensor(out=t2[c][:, :], in0=xnT[n.p][:, 0:T], scalar=omu[:, c:c + 1], in1=t2[c][:, :],
                                                   op0=ALU.mult, op1=ALU.add).then_inc(mixed, 1)

            def square_k(n):
                dve.wait_ge(k_relu, n.at(1, 1 - L2))
                nc.vector.tensor_tensor(hr[1][:, :], hr[0][:, :], hr[0][:, :], ALU.mult).then_inc(k_sq, 1)

            def gate(n):
                dve.wait_ge(r_tanh, n.at(1, 1 - L2))
                dve.wait_ge(kv_ps, n.at(1, 1 - L2))
                nc.vector.scalar_tensor_tensor(out=ee[1][:, :], in0=ee[0][:, :], scalar=1.0, in1=W5[:, :],
                                               op0=ALU.add, op1=ALU.mult).then_inc(gated, 1)
                dve.wait_ge(gated, n.at(1, 1 - L2))
                x = xt[n.p][:, :, :].rearrange("p j d -> p (j d)")
                nc.vector.scalar_tensor_tensor(out=x, in0=ee[1][:, :], scalar=0.5, in1=x, op0=ALU.mult, op1=ALU.add).then_inc(res_ready, 1)

            FS = 29
            a_, dt_ = abd[:, 0:1], abd[:, 2:3]
            f0, f1, f2, f3, f4, f5, f6, f7 = [f[:, :, :] for f in fhn]

            def fhn_chain(b, done):
                def step(ins):
                    done[0] += 1
                    ins.then_inc(fhn_step, 1)
                    dve.wait_ge(fhn_step, b.at(FS, done[0] - FS * L2))
                return step

            def reweigh_stim(b, done, fill_in):
                step = fhn_chain(b, done)
                dve.wait_ge(y_sb, b.at(SHEETS, SHEETS))
                step(nc.vector.tensor_copy(f7, yb[:, :, :, DH]))
                fill_in()
                step(nc.vector.reciprocal(rden[:, :, :], f7))
                fill_in()
                nc.vector.tensor_tensor(f0, f7, rden[:, :, :], ALU.mult).then_inc(fhn_stim, 1)
                dve.wait_ge(fhn_stim, b.at(1, 1 - L2))
                step(nc.vector.tensor_scalar(f1, f0, 1e-6, None, ALU.max))
                fill_in()
                step(nc.vector.reciprocal(f2, f1))
                fill_in()
                step(nc.vector.tensor_tensor(f2, f0, f2, ALU.mult))

            def reweigh_steps(b, done, fill_in):
                step = fhn_chain(b, done)
                dve.wait_ge(fhn_gate, b.at(1, 1 - L2))
                step(nc.vector.tensor_scalar(f3, f3, 1.0, None, ALU.add))
                fill_in()
                step(nc.vector.reciprocal(f4, f3))
                fill_in()
                step(nc.vector.tensor_scalar(f4, f4, 0.9, 0.1, ALU.mult, ALU.add))
                step(nc.vector.tensor_tensor(f2, f2, f4, ALU.mult))
                fill_in()
                step(nc.vector.tensor_scalar(f3, f2, dt_, None, ALU.mult))
                step(nc.vector.tensor_scalar(f4, f3, a_, alpha[:, 0:1], ALU.add, ALU.mult))
                fill_in()
                step(nc.vector.tensor_scalar(f4, f4, rdamp[:, 0:1], -3.0, ALU.mult, ALU.max))
                step(nc.vector.tensor_scalar(f4, f4, 3.0, None, ALU.min))
                step(nc.vector.tensor_scalar(f3, f3, -3.0, 3.0, ALU.max, ALU.min))
                fill_in()
                step(nc.vector.tensor_tensor(f5, f3, f3, ALU.mult))
                step(nc.vector.tensor_tensor(f5, f5, f3, ALU.mult))
                fill_in()
                step(nc.vector.scalar_tensor_tensor(out=f5, in0=f5, scalar=-1.0 / 3.0, in1=f3, op0=ALU.mult, op1=ALU.add))
                step(nc.vector.tensor_tensor(f5, f5, f4, ALU.subtract))
                fill_in()
                step(nc.vector.tensor_tensor(f5, f5, f2, ALU.add))
                step(nc.vector.scalar_tensor_tensor(out=f5, in0=f5, scalar=dt_, in1=f3, op0=ALU.mult, op1=ALU.add))
                fill_in()
                step(nc.vector.tensor_scalar(f5, f5, -3.0, 3.0, ALU.max, ALU.min))
                nc.vector.tensor_tensor(f2, f5, f1, ALU.mult).then_inc(fhn_resp, 1)

            def reweigh(b, done, fill_in):
                step = fhn_chain(b, done)
                dve.wait_ge(fhn_sig, b.at(1, 1 - L2))
                step(nc.vector.tensor_scalar(f3, f3, 1.0, None, ALU.add))
                fill_in()
                step(nc.vector.reciprocal(f4, f3))
                fill_in()
                step(nc.vector.tensor_scalar(f4, f4, 0.5, 0.5, ALU.mult, ALU.add))
                step(nc.vector.tensor_tensor(f5, f0, f4, ALU.mult))
                step(nc.vector.tensor_scalar(f5, f5, 1e-8, None, ALU.add))
                fill_in()
                step(nc.vector.tensor_tensor(f4, f4, rden[:, :, :], ALU.mult))
                step(nc.vector.reciprocal(f6, f5))
                fill_in()
                step(nc.vector.tensor_tensor(f6, f6, f4, ALU.mult))
                fill_in()
                nc.vector.tensor_tensor(y[:, :, :, :], yb[:, :, :, 0:DH],
                                        f6.unsqueeze(3).to_broadcast([128, J, H, DH]), ALU.mult).then_inc(y_ready, 1)
                assert done[0] == FS

            def output(b):
                dve.wait_ge(proj2_ps, b.at(1, 1 - L2))
                dve.wait_ge(res_loaded[b.p], b.own(16, 16 - 16 * HALVES))
                nc.vector.tensor_tensor(xr[b.p][:, :, :], xr[b.p][:, :, :],
                                        W5[:, :].rearrange("p (j d) -> p j d", j=J), ALU.add).then_inc(out_ready, 1)

            def body2(b):
                core, front, after, before_ = within(b), within(b + 2), within(b + 1), within(b + -1)
                at, done = [0], [0]

                def maxes(n=1):
                    for _ in range(n):
                        if after and at[0] < MU * SHEETS:
                            row_max(b + 1, at[0])
                            at[0] += 1

                def maxes_to(k):
                    if at[0] < k:
                        maxes(k - at[0])

                if before_:
                    y_out(b + -1, 3)
                maxes_to(2)
                if front:
                    combine(b + 2)
                    ln_moments(b + 2)
                maxes_to(9)
                if front:
                    ln(b + 2, False)
                if before_:
                    reweigh_stim(b + -1, done, maxes)
                maxes_to(16)
                if after:
                    mix(b + 1)
                maxes_to(18)
                if before_:
                    reweigh_steps(b + -1, done, maxes)
                maxes_to(26)
                if front:
                    split2(b + 2)
                maxes_to(28)
                if before_:
                    reweigh(b + -1, done, maxes)
                maxes_to(36)
                if core:
                    if not b.less(L2 + 1):
                        dve.wait_ge(y_ready, b.at(1, 0))
                    y_out(b, 0)
                maxes_to(MU * SHEETS)
                if before_:
                    output(b + -1)
                if core:
                    y_out(b, 1)
                if after:
                    shift_low(b + 1)
                    square_k(b + 1)
                if core:
                    y_out(b, 2)
                if after:
                    gate(b + 1)

            over_layer2(dve, body2)

        @block.tensor
        def _(pe):
            pe.wait_ge(consts_loaded, 16 * 23)
            pe.wait_ge(ready_consts, 7)

            def turn_xn(n, first_layer=True):
                pe.wait_ge(xn_ready, n.at(J, J))
                if first_layer and not early(n, 1):
                    pe.wait_ge(prefix_read, n.at(1, 0))
                for j in range(J):
                    ins = pe.transpose(W6[:, j * 128:(j + 1) * 128], xn[n.p][:, j, :], ident[:, :])
                ins.then_inc(xnT_ps, 1)

            def project_qk(n, c):
                if c == 0:
                    pe.wait_ge(xnT_sb, n.at(1, 1))
                    if not early(n, 2):
                        pe.wait_ge(h_relu, (n + -1).at(NB, 0))
                        pe.wait_ge(yT_sb, (n + -1).at(1, 0))
                    elif not early(n, 1):
                        pe.wait_ge(logits, n.at(2, 0))
                else:
                    pe.wait_ge(rot_cos, n.at(2, 1))
                    pe.wait_ge(rot_sin, n.at(2, 1))
                rhs = xnT[n.p][:, 1:T + 1]
                pe.matmul(W5[:, :], wqk[:, 2 * c, :], rhs, start=True, stop=True).then_inc(qk_ps, 1)
                pe.matmul(W6[:, :], wqk[:, 2 * c + 1, :], rhs, start=True, stop=True).then_inc(qkp_ps, 1)

            def project_v(n):
                pe.wait_ge(rot_cos, n.at(2, 2))
                pe.wait_ge(rot_sin, n.at(2, 2))
                for k, w in enumerate((W5, W6)):
                    for j in range(2):
                        t0 = 1 + (2 * k + j) * 128
                        ins = pe.matmul(w[:, j * (128 + E):(j + 1) * (128 + E)], xnT[n.p][:, t0:t0 + 128], wvr[:, :],
                                        start=True, stop=True)
                    ins.then_inc(v_ps, 1)

            def prefix(n):
                pe.wait_ge(picked, n.at(1, 1))
                pe.wait_ge(logits, n.at(2, 2))
                for j in range(J + 1):
                    terms = [(1, i) for i in range(j)] + ([(0, j)] if j < J else [])
                    for k, (m, i) in enumerate(terms):
                        ins = pe.matmul(W6[:, j * E:(j + 1) * E], before[:, m, :], pickb[:, i, :],
                                        start=(k == 0), stop=(k == len(terms) - 1))
                ins.then_inc(prefix_ps, 1)

            def scores(b, s, u):
                k = s * UNITS + u
                if k == 0:
                    pe.wait_ge(qk_loaded[b.p], b.own(16 * QK_LOADS, 16 * QK_LOADS))
                if not (early(b, 1) and k < 4):
                    pe.wait_ge(s_sb, b.at(PASS, k - 3))
                for g, kb, c in unit_parts(u):
                    h = G * s + g
                    n = T - 128 * kb
                    ins = pe.matmul(bank[k % 4][:, c:c + n], KT[b.p][0:ROWS, h, 128 * kb:128 * kb + 128],
                                    QT[b.p][0:ROWS, h, 128 * kb:T], start=True, stop=True)
                ins.then_inc(s_ps, 1)

            def pv(b, s, kb, first_layer=True):
                if kb == 0:
                    if first_layer:
                        pe.wait_ge(masked, b.at(8 * SHEETS, 8 * (s + 1)))
                        if s == 0:
                            pe.wait_ge(v_sb, b.at(2, 2))
                    elif s == 0:
                        pe.wait_ge(v2_sb, b.at(1, 1 - L2))
                    pe.wait_ge(s_sb, b.at(PASS, UNITS * (s + 1)))
                    if not (early(b, 1) and s == 0):
                        pe.wait_ge(oT_sb, b.at(SHEETS, s))
                n = T - 128 * kb
                for g in range(G):
                    u, c = PLACE[g, kb]
                    ins = pe.matmul(OT[32 * g:32 * g + 32, 128 * kb:T], V[b.p][:, kb, G * s + g, :],
                                    P[s % 2][:, u, c:c + n], start=(kb == 0), stop=(kb == J - 1), skip_group_check=True)
                if kb == J - 1:
                    ins.then_inc(pv_done, 1)

            def turn_oT(b, s, first_layer=True):
                pe.wait_ge(oT_sb, b.at(SHEETS, s + 1))
                if not (early(b, 1) and s == 0):
                    pe.wait_ge(y_sb, b.at(SHEETS, s))
                if s == 0 and first_layer and not early(b, 1):
                    pe.wait_ge(xa_ready, b.at(1, 0))
                for j in range(J):
                    ins = pe.transpose(W7[:, j * 128:(j + 1) * 128], oT[s % 2][:, j * 128:(j + 1) * 128], ident[:, :])
                ins.then_inc(oTT_ps, 1)

            def turn_y(b, last):
                pe.wait_ge(y_ready, b.at(1, 1))
                if last:
                    pe.wait_ge(prefix_read, B)
                else:
                    pe.wait_ge(xnT_sb, (b + 2).at(1, 1))
                for j in range(J):
                    ins = pe.transpose(W6[:, j * 128:(j + 1) * 128],
                                       y[:, j, :, :].rearrange("p h d -> p (h d)"), ident[:, :])
                ins.then_inc(yT_ps, 1)

            def shared_fc(b, k, last):
                if k > 0:
                    pe.wait_ge(h_relu, b.at(NB, k))
                elif not last:
                    pe.wait_ge(logits, (b + 1).at(2, 1))
                elif not early(b, 1):
                    pe.wait_ge(h_relu, b.at(NB, 0))
                pe.matmul(W5[:, :], sfc[:, k * 128:(k + 1) * 128], xnT[b.p][:, 1:T + 1], start=True, stop=True).then_inc(fc_ps, 1)

            def project_out(b):
                pe.wait_ge(yT_sb, b.at(1, 1))
                pe.wait_ge(h_sq, b.at(NB, NB))
                pe.wait_ge(y_sb, b.at(SHEETS, SHEETS))
                for j in range(J):
                    o = W7[:, j * 128:(j + 1) * 128]
                    for k in range(NB):
                        c0 = (j % 2) * 128
                        pe.matmul(o, hT[:, j // 2, k, c0:c0 + 128], spj[:, k, :], start=(k == 0), stop=False)
                    ins = pe.matmul(o, yT[:, j * 128:(j + 1) * 128], wo[:, :], start=False, stop=True)
                ins.then_inc(proj_ps, 1)

            def body(b, first, last):
                for u in range(UNITS):
                    scores(b, 0, u)
                    if u == 1 and not first:
                        turn_oT(b + -1, 3)
                    if u == 3 and not last:
                        turn_xn(b + 1)
                    if u == 7 and not first:
                        turn_y(b + -1, last)
                if not last:
                    project_qk(b + 1, 0)
                for s in range(1, SHEETS):
                    for k in range(J):
                        scores(b, s, 2 * k)
                        scores(b, s, 2 * k + 1)
                        pv(b, s - 1, k)
                        if s == 1 and k == 0 and not last:
                            project_qk(b + 1, 1)
                        if s == 1 and k == 2 and not first:
                            project_out(b + -1)
                    scores(b, s, 8)
                    scores(b, s, 9)
                    if s == 2 and not last:
                        project_v(b + 1)
                    if s >= 2:
                        turn_oT(b, s - 2)
                for k in range(J):
                    pv(b, SHEETS - 1, k)
                    if k == 1:
                        turn_oT(b, 2)
                    shared_fc(b, k, last)
                if not last:
                    prefix(b + 1)

            n0 = Turn(0, 0)
            turn_xn(n0)
            project_qk(n0, 0)
            project_qk(n0, 1)
            project_v(n0)
            prefix(n0)
            over_batches(pe, body)
            turn_oT(AFTER + -1, 3)
            turn_y(AFTER + -1, True)
            project_out(AFTER + -1)

            def turn_tile(t):
                pe.wait_ge(xg_loaded[t.p], t.own(16, 16))
                if not t.less(2):
                    pe.wait_ge(xgT_sb, t.at(1, -1))
                for c in range(GT // 128):
                    ins = pe.transpose(bank[t.p % 2][:, c * 128:(c + 1) * 128], xg[t.p][:, c, :], ident[:, :])
                ins.then_inc(xgT_ps, 1)

            def fc_tile(t):
                pe.wait_ge(xgT_sb, t.at(1, 1))
                pe.wait_ge(w_loaded[t.p], t.own(32, 32))
                for k in range(2):
                    w = bank[2 + 2 * (t.p % 2) + k]
                    if not t.less(2):
                        pe.wait_ge(e_relu, t.at(2, k - 3))
                    for i in range(2):
                        c = 2 * k + i
                        ins = pe.matmul(w[:, i * GT:(i + 1) * GT], wfc[t.p][:, c * 128:(c + 1) * 128], xgT[t.p % 2], start=True, stop=True)
                    ins.then_inc(efc_ps, 1)

            def proj_tile(t):
                pe.wait_ge(e_sq, t.at(2, 2))
                if not t.less(2):
                    pe.wait_ge(ey_sb, t.at(1, -1))
                for c in range(GT // 128):
                    for k in range(NB):
                        ins = pe.matmul(bank[6 + t.p % 2][:, c * 128:(c + 1) * 128], hT[:, t.p % 2, k, c * 128:(c + 1) * 128],
                                        wpj[t.p][:, k, :], start=(k == 0), stop=(k == NB - 1))
                ins.then_inc(ey_ps, 1)

            def tile(t):
                if t.known() is None or t.known() + 1 < NTILES:
                    turn_tile(t + 1)
                fc_tile(t)
                if not t.less(1):
                    proj_tile(t + -1)

            turn_tile(Turn(0, 0, TB))
            over_tiles(pe, tile)
            proj_tile(Turn(NTILES // TB, 0, TB) + -1)

            def q_rows(n, c):
                pe.wait_ge(xnT_sb, n.at(1, 1))
                if c == 0 and not n.less(L2 + 2):
                    pe.wait_ge(gated, (n + -1).at(1, -L2))
                pe.matmul((W5, W6)[c][:, :], wqkv2[:, c, :], xnT[n.p][:, 1:T + 1], start=True, stop=True).then_inc(qk_ps, 1)

            def v_rows(n, front):
                if front:
                    pe.wait_ge(res_part, (n + 1).at(2, 1))
                elif not n.less(L2 + 1):
                    pe.wait_ge(gated, n.at(1, -L2))
                for j in range(J):
                    ins = pe.matmul(W5[:, j * 128:(j + 1) * 128], xnT[n.p][:, 1 + j * 128:1 + (j + 1) * 128], wqkv2[:, 2, :],
                                    start=True, stop=True)
                ins.then_inc(v2_ps, 1)

            def max_scores(n, k):
                s, (j, g, nh) = k // MU, MAX_UNITS[k % MU]
                if k % (2 * MU) == 0:
                    half = k // (2 * MU)
                    pe.wait_ge(half_loaded[n.p][half], n.own(16 * QK_LOADS, 16 * QK_LOADS - 16 * QK_LOADS * HALVES))
                if not (n.less(L2 + 1) and k < 2):
                    pe.wait_ge(max_read, n.at(MU * SHEETS, k - 1 - MU * SHEETS * L2))
                w = 128 * (j + 1)
                for i in range(nh):
                    h = G * s + g + i
                    ins = pe.matmul(bank[2 + k % 2][:, i * w:(i + 1) * w], QT[n.p][0:MROWS, h, j * 128:(j + 1) * 128],
                                    KT[n.p][0:MROWS, h, 0:w], start=True, stop=True)
                ins.then_inc(max_ps, 1)

            def turn_max(n, before_, front):
                pe.wait_ge(max_read, n.at(MU * SHEETS, MU * SHEETS - MU * SHEETS * L2))
                if before_:
                    pe.wait_ge(yT_sb, (n + -1).at(1, 0))
                elif front:
                    pe.wait_ge(res_part, (n + 1).at(2, 2))
                for j in range(J):
                    ins = pe.transpose(W6[0:H, j * 128:(j + 1) * 128], nmax[:, j, :], ident[:, :])
                ins.then_inc(maxT_ps, 1)

            def shifted_scores(b, s, u):
                k = s * UNITS + u
                if k == 0:
                    pe.wait_ge(shift_loaded[b.p], b.own(16, 16 - 16 * HALVES))
                if not (b.less(L2 + 1) and k < 2):
                    pe.wait_ge(s_sb, b.at(PASS, k - 1))
                for g, kb, c in unit_parts(u):
                    h = G * s + g
                    n = T - 128 * kb
                    ins = pe.matmul(bank[k % 2][:, c:c + n], KT[b.p][0:SROWS, h, 128 * kb:128 * kb + 128],
                                    QT[b.p][0:SROWS, h, 128 * kb:T], start=True, stop=True)
                ins.then_inc(s_ps, 1)

            def turn_y2(b, front):
                pe.wait_ge(y_ready, b.at(1, 1))
                if front:
                    pe.wait_ge(res_part, (b + 3).at(2, 2))
                else:
                    pe.wait_ge(r_tanh, (b + 1).at(1, 1 - L2) if within(b + 1) else B)
                for j in range(J):
                    ins = pe.transpose(W6[:, j * 128:(j + 1) * 128], y[:, j, :, :].rearrange("p h d -> p (h d)"), ident[:, :])
                ins.then_inc(yT_ps, 1)

            def project_out2(b):
                pe.wait_ge(yT_sb, b.at(1, 1))
                if within(b + 2):
                    pe.wait_ge(v2_sb, (b + 2).at(1, 1 - L2))
                else:
                    pe.wait_ge(gated, B)
                    if not within(b + 1):
                        pe.wait_ge(out_ready, b.at(1, -L2))
                for j in range(J):
                    ins = pe.matmul(W5[:, j * 128:(j + 1) * 128], yT[:, j * 128:(j + 1) * 128], wo2[:, :], start=True, stop=True)
                ins.then_inc(proj2_ps, 1)

            def k_rows(n, before_):
                pe.wait_ge(mixed, n.at(4, 4 - 4 * L2))
                if before_:
                    pe.wait_ge(out_ready, (n + -1).at(1, -L2))
                else:
                    pe.wait_ge(v2_sb, n.at(1, 1 - L2))
                pe.matmul(W5[:, :], wrkv[:, 1, :], t2[1][:, :], start=True, stop=True).then_inc(k_ps, 1)

            def r_rows(n):
                pe.wait_ge(shift_lo, n.at(1, 1 - L2))
                for j in range(J):
                    ins = pe.matmul(W6[:, j * 128:(j + 1) * 128], t2[0][:, j * 128:(j + 1) * 128], wrkv[:, 0, :], start=True, stop=True)
                ins.then_inc(r_ps, 1)

            def kv_rows(n):
                pe.wait_ge(k_sq, n.at(1, 1 - L2))
                for j in range(J):
                    ins = pe.matmul(W5[:, j * 128:(j + 1) * 128], hr[1][:, j * 128:(j + 1) * 128], wrkv[:, 2, :], start=True, stop=True)
                ins.then_inc(kv_ps, 1)

            def body2(b):
                core, front, after, before_ = within(b), within(b + 2), within(b + 1), within(b + -1)
                at = [0]

                def maxes(n):
                    for _ in range(n):
                        if after and at[0] < MU * SHEETS:
                            max_scores(b + 1, at[0])
                            at[0] += 1

                for u in range(UNITS):
                    if core:
                        shifted_scores(b, 0, u)
                    if u == 1 and before_:
                        turn_oT(b + -1, 3, False)
                    maxes(1)
                for s in range(1, SHEETS):
                    for k in range(J):
                        if core:
                            shifted_scores(b, s, 2 * k)
                            shifted_scores(b, s, 2 * k + 1)
                            pv(b, s - 1, k, False)
                        if (s, k) == (1, 1) and front:
                            turn_xn(b + 2, False)
                        if (s, k) == (3, 0) and before_:
                            turn_y2(b + -1, front)
                        if (s, k) == (3, 2) and before_:
                            project_out2(b + -1)
                        maxes(3)
                    if core:
                        shifted_scores(b, s, 8)
                        shifted_scores(b, s, 9)
                    if s == 1 and front:
                        q_rows(b + 2, 0)
                        q_rows(b + 2, 1)
                    if s == 2 and after:
                        v_rows(b + 1, front)
                    if s >= 2 and core:
                        turn_oT(b, s - 2, False)
                maxes(MU * SHEETS)
                if after:
                    turn_max(b + 1, before_, front)
                for k in range(J):
                    if core:
                        pv(b, SHEETS - 1, k, False)
                    if k == 0 and after:
                        k_rows(b + 1, before_)
                    if k == 1 and core:
                        turn_oT(b, 2, False)
                    if k == 1 and after:
                        r_rows(b + 1)
                    if k == 3 and after:
                        kv_rows(b + 1)

            over_layer2(pe, body2)


def layout(inputs):
    import numpy as _np

    c = _np.ascontiguousarray
    a = {k: _np.asarray(v) for k, v in inputs.items()}
    half = DH // 2
    swap = _np.arange(D).reshape(H, 2, half)[:, ::-1].reshape(D)
    wq, wk = a["L0_attn_Wq"], a["L0_attn_Wk"]
    arrays = {"x": c(a["L0_attn_x"])}
    arrays["wqk"] = c(_np.stack([wq.T, wq[swap].T, wk.T, wk[swap].T], axis=1))
    arrays["wvr"] = c(_np.concatenate([a["L0_attn_Wv"].T, a["L0_ffn_router_w"].T], axis=1))
    arrays["wo"] = c(a["L0_attn_Wo"].T)
    fc = _np.concatenate([a["L0_ffn_w_fc"], a["L0_ffn_shared_fc"][None]])
    pj = _np.concatenate([a["L0_ffn_w_proj"], a["L0_ffn_shared_proj"][None]])
    arrays["fc"] = c(fc.transpose(0, 2, 1))
    arrays["proj"] = c(pj.transpose(0, 2, 1).reshape(E + 1, NB, 128, D).transpose(0, 2, 1, 3))
    w = a["L1_attn_W_qkv"]
    arrays["wqkv2"] = c(w.reshape(3, D, D).transpose(2, 0, 1))
    arrays["wo2"] = c(a["L1_attn_W_out"].T)
    arrays["wrkv"] = c(_np.stack([a["L1_ffn_W_r"].T, a["L1_ffn_W_k"].T, a["L1_ffn_W_v"].T], axis=1))
    arrays["mu"] = c(_np.stack([a["L1_ffn_mu_r"], a["L1_ffn_mu_k"]], axis=1))
    arrays["abd"] = c(_np.broadcast_to(_np.stack([a["L1_attn_a"], a["L1_attn_b"], a["L1_attn_dt"]])[None], (128, 3)))

    f = _np.float32
    freq = (f(10000.0) ** (-_np.arange(half, dtype=f) / f(half))).astype(f)
    ang = _np.arange(T, dtype=f)[None, :] * freq[_np.arange(D) % half][:, None]
    sign = _np.where(_np.arange(D) % DH < half, -1, 1).astype(f)[:, None]
    arrays["rope"] = c(_np.stack([_np.cos(ang), sign * _np.sin(ang)], axis=1).astype(f))
    i = _np.arange(128)
    causal = (i[:, None] <= i[None, :]).astype(f)
    arrays["tri"] = c(_np.broadcast_to(causal[:, None], (128, 4, 128)))
    arrays["ident"] = _np.eye(128, dtype=f)
    arrays["before"] = c(_np.stack([i[:, None] < i[None, :], _np.ones((128, 128))], axis=1).astype(mybir.dt.np(BF16)))
    e = _np.arange(E)
    arrays["lower"] = c(_np.broadcast_to((e[None, :] < e[:, None]).astype(f), (128, E, E)))
    arrays["incl"] = c(_np.broadcast_to((e[None, :] <= e[:, None]).astype(f), (128, E, E)))
    arrays["ebase"] = c(_np.broadcast_to(_np.stack([e * REGION, e]).astype(f), (128, 2, E)))
    t = _np.arange(NTILES)
    empty = DUMMY + t % SPARE * GT
    arrays["tiles"] = c(_np.broadcast_to(_np.stack([t, t * GT - empty, empty]).astype(f), (128, 3, NTILES)))
    arrays["steps"] = c(_np.broadcast_to((_np.arange(CAP // GT) * GT).astype(f), (128, CAP // GT)))
    tok = _np.arange(T)
    hq = _np.zeros((J, H, T), f)
    hk = _np.zeros((J + 2, H, T), f)
    for j in range(J):
        hq[j][:, (tok // 128 == j) & (tok % 128 < CHUNK)] = 1
        hk[j][:, (tok // 128 == j) & (tok % 128 >= CHUNK)] = MASKED
    hk[J:] = 1
    arrays["half_q"], arrays["half_k"] = hq.astype(mybir.dt.np(BF16)), hk.astype(mybir.dt.np(BF16))
    return arrays


def kernel(**inputs):
    import concourse.bacc as _bacc
    from concourse import mybir as _mybir
    from concourse.bass_utils import run_bass_kernel_spmd as _run

    nc = _bacc.Bacc("TRN2", target_bir_lowering=False, num_devices=1)
    arrays = layout(inputs)
    io = {n: nc.dram_tensor("in_" + n, a.shape, _mybir.dt.from_np(a.dtype), kind="ExternalInput").ap() for n, a in arrays.items()}
    out = nc.dram_tensor("out", (B, T, D), F32, kind="ExternalOutput").ap()
    build(nc, io, out)
    r = _run(nc, [{"in_" + n: a for n, a in arrays.items()}], core_ids=[0])
    return r.results[0]["out"]
```

```python
import numpy as np
import concourse.bass as bass
from concourse import mybir
from contextlib import ExitStack

F32 = mybir.dt.float32
BF16 = mybir.dt.bfloat16
I32 = mybir.dt.int32
ALU = mybir.AluOpType
ACT = mybir.ActivationFunctionType
AX = mybir.AxisListType

B, T, D = 16, 512, 128
H, DH = 16, 8
E, FF = 8, 512
NB = FF // 128
J = T // 128
CHUNK = 64
SHEETS, G = 4, 4
UNITS = 10
PASS = SHEETS * UNITS
NPROD = 9
ROWS = NPROD * DH
HALF0 = ROWS
SHIFT0 = HALF0 + J
MROWS = SHIFT0
SROWS = SHIFT0 + 2
LOADS = [(0, 0, 0, 3), (0, 24, 0, 3), (0, 48, 0, 3),
         (1, 0, 0, 3), (1, 24, 1, 2), (1, 40, 0, 1), (1, 48, 2, 1), (1, 56, 0, 2)]
QK_LOADS = len(LOADS)
CAP = B * T
GT = 256
REGION = CAP + GT
TB = 4
NTILES = -(-((2 * CAP + E * (GT - 1)) // GT) // TB) * TB
SPARE = NTILES - 2 * CAP // GT
DUMMY = E * REGION
NROWS = DUMMY + SPARE * GT
LN_EPS = 1e-5
DEN_EPS = 1e-6
CONSTS = 24
TAU = 12.5
MASKED = -1e30


class Turn:

    def __init__(self, hi, p, m=2):
        self.hi, self.p, self.m = hi, p, m

    def __add__(self, d):
        return Turn(self.hi + (self.p + d) // self.m, (self.p + d) % self.m, self.m)

    def at(self, n, k):
        return self.hi * (self.m * n) + (n * self.p + k)

    def own(self, n, k):
        return self.hi * n + k

    def known(self):
        return self.m * self.hi + self.p if isinstance(self.hi, int) else None

    def less(self, n):
        return self.known() is not None and self.known() < n


def unit_parts(u):
    if u < G:
        return [(u, 0, 0)]
    if u < 2 * G:
        return [(u - G, 1, 0), (u - G, 3, T - 128)]
    return [(2 * (u - 2 * G) + i, 2, i * T // 2) for i in range(2)]


PV_ORDER = [(0, G), (1, 2 * G), (3, 2 * G), (2, UNITS)]
PLACE = {(g, kb): (u, c) for u in range(UNITS) for g, kb, c in unit_parts(u)}

MAX_UNITS = ([(3, g, 1) for g in range(G)] + [(2, g, 1) for g in range(G)]
             + [(1, 0, 2), (1, 2, 2)] + [(0, 0, 4)])
MU = len(MAX_UNITS)


def build(nc, io, out):
    ctx = ExitStack()
    with ctx:
        def sb(name, shape, dt=F32):
            return ctx.enter_context(nc.sbuf_tensor(name, shape, dt))

        def sem(name):
            return ctx.enter_context(nc.semaphore(name))

        def dram(name, shape, dt=F32):
            return nc.dram_tensor(name, shape, dt, kind="Internal").ap()

        x_d = io["x"].rearrange("b (j p) d -> b p j d", p=128)
        out_d = out.rearrange("b (j p) d -> b p j d", p=128)
        parts_d = dram("parts_d", (2, 2, 3, 128, T), BF16)
        shift_d = dram("shift_d", (2, 2, H, T), BF16)
        xa_d = dram("xa_d", (B, 128, J, D))
        wts_d = dram("wts_d", (B, 128, 2 * J))
        slot_d = dram("slot_d", (B, 128, 2 * J), I32)
        idx_d = dram("idx_d", (B, 128, 2 * J), I32)
        xs_d = dram("xs_d", (NROWS, D))
        ys_d = dram("ys_d", (NTILES * GT, D))

        bank = [ctx.enter_context(nc.psum_tensor(f"bank{k}", [128, 512], F32)) for k in range(8)]
        OT, W5, W6, W7 = bank[4], bank[5], bank[6], bank[7]

        wqk = sb("wqk", [128, 4, 128])
        wvr = sb("wvr", [128, 128 + E])
        wo = sb("wo", [128, 128])
        sfc = sb("sfc", [128, FF])
        spj = sb("spj", [128, NB, 128])
        rope = sb("rope", [128, 2, T])
        tri = sb("tri", [128, 4, 128])
        ident = sb("ident", [128, 128])
        before = sb("before", [128, 2, 128], BF16)
        lower = sb("lower", [128, E, E])
        incl = sb("incl", [128, E, E])
        ebase = sb("ebase", [128, 2, E])
        tiles = sb("tiles", [128, 3, NTILES])
        steps = sb("steps", [128, CAP // GT])
        eps = sb("eps", [128, 1])
        own = sb("own", [128, H, DH + 1])
        wqkv2 = sb("wqkv2", [128, 3, 128])
        wo2 = sb("wo2", [128, 128])
        wrkv = sb("wrkv", [128, 3, 128])
        mu = sb("mu", [128, 2])
        omu = sb("omu", [128, 2])
        abd = sb("abd", [128, 3])

        QT = [sb(f"QT{p}", [128, H, T], BF16) for p in range(2)]
        KT = [sb(f"KT{p}", [128, H, T], BF16) for p in range(2)]
        V = [sb(f"V{p}", [128, J, H, 32]) for p in range(2)]
        P = [sb(f"P{p}", [128, UNITS, T]) for p in range(2)]
        state = [P[p][:, G:G + J - 1, :].rearrange("p u (h c) -> p u h c", c=32) for p in range(2)]
        qf = [P[p][:, G + J - 1, :] for p in range(2)]
        ktok = P[0][:, G + J, 0:(J - 1) * 128].rearrange("p (j c) -> p j c", c=128)
        oT = [sb(f"oT{p}", [128, T]) for p in range(2)]
        parts = [sb(f"parts{c}", [128, 3, T], BF16) for c in range(2)]
        yb = sb("yb", [128, J, H, DH + 1])
        y = sb("y", [128, J, H, DH])
        yT = sb("yT", [128, T])
        xt = [sb(f"xt{p}", [128, J, D]) for p in range(2)]
        xr = [sb(f"xr{p}", [128, J, D]) for p in range(2)]
        xn = [sb(f"xn{p}", [128, J, D]) for p in range(2)]
        xnT = [sb(f"xnT{p}", [128, T + 1]) for p in range(2)]
        stats = sb("stats", [128, J, 6])
        mv = sb("mv", [128, J, 2])
        std = sb("std", [128, J])
        rstd = sb("rstd", [128, J])
        den = sb("den", [128, J, H])
        rden = sb("rden", [128, J, H])
        t1 = [sb(f"t1{c}", [128, T]) for c in range(2)]
        t2 = [sb(f"t2{c}", [128, T]) for c in range(2)]
        ee = [sb(f"ee{c}", [128, T]) for c in range(2)]
        hr = [sb(f"hr{c}", [128, 512]) for c in range(2)]
        hT = sb("hT", [128, 2, NB, T // 2])

        lg = sb("lg", [128, J, E])
        lmax = sb("lmax", [128, J])
        pr = sb("pr", [128, J, E])
        psum_ = sb("psum_", [128, J])
        gt = sb("gt", [128, J, E, E])
        eq = sb("eq", [128, J, E, E])
        order = sb("order", [128, J, E])
        pick = sb("pick", [128, 2, J, E])
        pickb = sb("pickb", [128, J, E], BF16)
        prod = sb("prod", [128, 2, J, E])
        p12 = sb("p12", [128, 2, J])
        wts = [sb(f"wts{p}", [128, 2, J]) for p in range(2)]
        slotf = sb("slotf", [128, 2, J])
        idx = [sb(f"idx{p}", [128, 2 * J], I32) for p in range(2)]
        fill = sb("fill", [128, E])
        pos = sb("pos", [128, J, E])
        zeros = sb("zeros", [128, GT // 128, D])
        big = P[0][:, :, :].rearrange("p u t -> p (u t)")[:, 0:3 * E * NTILES].rearrange("p (k e t) -> p k e t", k=3, e=E)
        count = sb("count", [128, E])
        ntile = sb("ntile", [128, 3, E])
        tab = sb("tab", [128, 2 * NTILES + E], I32)
        tabf = sb("tabf", [128, 2, NTILES])
        idx_all = sb("idx_all", [128, B * 2 * J], I32)
        moved = sb("moved", [128, B * 2 * J])
        slot_all = P[0][:, UNITS - 3, 0:B * 2 * J]
        above = P[0][:, UNITS - 2:UNITS, :].rearrange("p u t -> p (u t)")[:, 0:B * 2 * J * (E - 1)].rearrange("p (k e) -> p k e", e=E - 1)

        spare = P[1][:, :, :].rearrange("p u t -> p (u t)")
        wfc = [spare[:, k * FF:(k + 1) * FF] for k in range(TB)]
        wpj = [spare[:, (TB + k) * FF:(TB + k + 1) * FF].rearrange("p (k d) -> p k d", k=NB) for k in range(TB)]
        xg, yg = ([P[0][:, k, i * GT:(i + 1) * GT].rearrange("p (c d) -> p c d", c=GT // 128) for k in range(TB)] for i in range(2))
        xgT = [P[0][:, TB + k, 0:GT] for k in range(2)]

        ya = [hT[:, p, :, :].rearrange("p k t -> p (k t)").rearrange("p (k d) -> p k d", d=D) for p in range(2)]
        x1 = [rope[:, p, :].rearrange("p (j d) -> p j d", d=D) for p in range(2)]
        nmax = sb("nmax", [128, J, H])
        shift = sb("shift", [H, 2, T], BF16)
        fhn = [sb(f"fhn{k}", [128, J, H]) for k in range(8)]
        alpha = sb("alpha", [128, 1])
        rdamp = sb("rdamp", [128, 1])
        one_b = sb("one_b", [128, 1])
        five = sb("five", [128, 1])

        consts_loaded, zeroed, ready_consts = sem("consts_loaded"), sem("zeroed"), sem("ready_consts")
        dummy_zeroed = sem("dummy_zeroed")
        x_loaded = [sem(f"x_loaded{p}") for p in range(2)]
        xr_loaded = [sem(f"xr_loaded{p}") for p in range(2)]
        ln_stats, ln_mean, ln_std, ln_rstd, xn_ready = (sem(s) for s in ("ln_stats", "ln_mean", "ln_std", "ln_rstd", "xn_ready"))
        xnT_ps, xnT_sb = sem("xnT_ps"), sem("xnT_sb")
        qk_ps, qkp_ps = sem("qk_ps"), sem("qkp_ps")
        rot_cos, rot_sin, rot, rot_min, rot_exp, phi = (sem(s) for s in ("rot_cos", "rot_sin", "rot", "rot_min", "rot_exp", "phi"))
        hi_part, res_part, mid_part, lo_part = (sem(s) for s in ("hi_part", "res_part", "mid_part", "lo_part"))
        parts_stored = [sem(f"parts_stored{c}") for c in range(2)]
        qk_loaded = [sem(f"qk_loaded{p}") for p in range(2)]
        v_ps, v_sb, logits = sem("v_ps"), sem("v_sb"), sem("logits")
        router_in, router_exp, router_step, picked = (sem(s) for s in ("router_in", "router_exp", "router_step", "picked"))
        prefix_ps, prefix_read, slots_step, slots_ready = (sem(s) for s in ("prefix_ps", "prefix_read", "slots_step", "slots_ready"))
        scattered = [sem(f"scattered{p}") for p in range(2)]
        route_stored = [sem(f"route_stored{p}") for p in range(2)]
        a_ps, a_sb, a_masked = sem("a_ps"), sem("a_sb"), sem("a_masked")
        kT_ps, ktok_sb, state_ps, state_sb = sem("kT_ps"), sem("ktok_sb"), sem("state_ps"), sem("state_sb")
        pv_done = sem("pv_done")
        oT_sb, oTT_ps, y_sb = sem("oT_sb"), sem("oTT_ps"), sem("y_sb")
        norm_step, y_ready, yT_ps, yT_sb = sem("norm_step"), sem("y_ready"), sem("yT_ps"), sem("yT_sb")
        fc_ps, h_relu, h_sq, proj_ps, xa_ready = (sem(s) for s in ("fc_ps", "h_relu", "h_sq", "proj_ps", "xa_ready"))
        xa_stored = [sem(f"xa_stored{p}") for p in range(2)]
        plan_step, plan_ready, pad_zeroed = sem("plan_step"), sem("plan_ready"), sem("pad_zeroed")
        slots_loaded, rows_ready, rows_stored = sem("slots_loaded"), sem("rows_ready"), sem("rows_stored")
        xg_loaded = [sem(f"xg_loaded{p}") for p in range(TB)]
        w_loaded = [sem(f"w_loaded{p}") for p in range(TB)]
        xgT_ps, xgT_sb, efc_ps, e_relu, e_sq, ey_ps, ey_sb = (
            sem(s) for s in ("xgT_ps", "xgT_sb", "efc_ps", "e_relu", "e_sq", "ey_ps", "ey_sb"))
        ys_stored = [sem(f"ys_stored{p}") for p in range(TB)]
        s_ps, s_sb = sem("s_ps"), sem("s_sb")
        route_loaded = [sem(f"route_loaded{p}") for p in range(2)]
        xa_loaded = [sem(f"xa_loaded{p}") for p in range(2)]
        gathered = [sem(f"gathered{p}") for p in range(2)]
        summed, x1_ready = sem("summed"), sem("x1_ready")
        half_loaded = [[sem(f"half{h}_loaded{p}") for h in range(2)] for p in range(2)]
        max_ps, max_read, maxT_ps, shift_hi, shift_lo = (sem(s) for s in ("max_ps", "max_read", "maxT_ps", "shift_hi", "shift_lo"))
        shift_stored, shift_loaded = [[sem(f"shift_{w}{p}") for p in range(2)] for w in ("stored", "loaded")]
        v2_ps, v2_sb = sem("v2_ps"), sem("v2_sb")
        mixed, k_ps, k_relu, k_sq, r_ps, r_tanh, kv_ps, gated = (
            sem(s) for s in ("mixed", "k_ps", "k_relu", "k_sq", "r_ps", "r_tanh", "kv_ps", "gated"))
        res_ready = sem("res_ready")
        fhn_step, fhn_stim, fhn_gate, fhn_resp, fhn_sig = (sem(s) for s in ("fhn_step", "fhn_stim", "fhn_gate", "fhn_resp", "fhn_sig"))
        proj2_ps, out_ready, out_stored = sem("proj2_ps"), sem("out_ready"), [sem(f"out_stored{p}") for p in range(2)]
        setup2 = sem("setup2")

        block = ctx.enter_context(nc.Block())

        HALVES = B // 2
        L2 = B
        AFTER = Turn(HALVES, 0)

        def over_batches(eng, body):
            for p in range(2):
                body(Turn(0, p), p == 0, False)
            with eng.Fori(1, HALVES - 1) as i:
                for p in range(2):
                    body(Turn(i, p), False, False)
            for p in range(2):
                body(Turn(HALVES - 1, p), False, p == 1)

        def value(eng, v):
            return v if isinstance(v, int) else eng.snap(eng.to_reg(v))

        def early(b, d):
            return b.less(d)

        def within(b):
            return b.known() is None or L2 <= b.known() < L2 + B

        def over_layer2(eng, body):
            for k in range(-2, 2):
                body(Turn(HALVES, 0) + k)
            with eng.Fori(HALVES + 1, 2 * HALVES - 2) as i:
                for p in range(2):
                    body(Turn(i, p))
            for k in range(-4, 1):
                body(Turn(2 * HALVES, 0) + k)

        def over_tiles(eng, body):
            for p in range(TB):
                body(Turn(0, p, TB))
            with eng.Fori(1, NTILES // TB - 1) as i:
                for p in range(TB):
                    body(Turn(i, p, TB))
            for p in range(TB):
                body(Turn(NTILES // TB - 1, p, TB))

        def row(b):
            return bass.ds(b.hi * 2 + b.p, 1)

        def row2(b):
            return bass.ds(b.hi * 2 + (b.p - L2), 1)

        @block.sync
        def _(sp):
            loads = [(wqk, io["wqk"]), (wvr, io["wvr"]), (wo, io["wo"]), (sfc, io["fc"][E]), (spj, io["proj"][E]),
                     (own, io["own"]), (rope, io["rope"]), (tri, io["tri"]), (ident, io["ident"]), (before, io["before"]),
                     (lower, io["lower"]), (incl, io["incl"]), (ebase, io["ebase"]), (tiles, io["tiles"]), (steps, io["steps"]),
                     (wqkv2, io["wqkv2"]), (wo2, io["wo2"]), (wrkv, io["wrkv"]), (mu, io["mu"]), (abd, io["abd"])]

            def load_x(n):
                if not early(n, 2):
                    sp.wait_ge(xn_ready, (n + -2).at(J, J))
                sp.dma_start(xt[n.p][:, :, :], x_d[bass.ds(n.hi * 2 + n.p, 1)].rearrange("b p j d -> p (b j) d")).then_inc(x_loaded[n.p], 16)

            load_x(Turn(0, 0))
            for t, src in loads:
                ap = t[tuple(slice(None) for _ in t.shape)]
                sp.dma_start(ap, src).then_inc(consts_loaded, 16)
            for p in range(2):
                sp.dma_start(QT[p][HALF0:SHIFT0, :, :], io["half_q"]).then_inc(consts_loaded, 16)
                sp.dma_start(KT[p][HALF0:SROWS, :, :], io["half_k"]).then_inc(consts_loaded, 16)
            load_x(Turn(0, 1))
            sp.wait_ge(zeroed, 1)
            for k in range(SPARE):
                sp.dma_start(xs_d[DUMMY + k * GT:DUMMY + (k + 1) * GT, :].rearrange("(c p) d -> p c d", p=128),
                             zeros[:, :, :]).then_inc(dummy_zeroed, 16)

            def store_parts(n):
                copied = value(sp, n.own(16 * QK_LOADS, 0))
                split_ = [value(sp, n.at(2, c + 1)) for c in range(2)]
                for c in range(2):
                    sp.wait_ge(lo_part, split_[c])
                    if not early(n, 2):
                        sp.wait_ge(qk_loaded[n.p], copied)
                    sp.dma_start(parts_d[n.p, c].rearrange("a p t -> p a t"), parts[c][:, :, :]).then_inc(parts_stored[c], 16)

            def load_parts(n):
                stored = value(sp, n.at(16, 16))
                if not early(n, 2):
                    sp.wait_ge(a_ps, (n + -1).at(H, 0))
                for c, row0, part, parts_ in LOADS:
                    if row0 == 0:
                        sp.wait_ge(parts_stored[c], stored)
                    sp.dma_start((QT, KT)[c][n.p][row0:row0 + parts_ * DH, :, :],
                                 parts_d[n.p, c, part:part + parts_].rearrange("a (d h) t -> (a d) h t", d=DH)).then_inc(qk_loaded[n.p], 16)

            def store_route(n):
                sp.wait_ge(slots_ready, n.at(1, 1))
                sp.dma_start(wts_d[bass.ds(n.hi * 2 + n.p, 1)].rearrange("b p k -> p (b k)"),
                             wts[n.p][:, :, :].rearrange("p c j -> p (c j)")).then_inc(route_stored[n.p], 16)
                sp.dma_start(slot_d[bass.ds(n.hi * 2 + n.p, 1)].rearrange("b p k -> p (b k)"),
                             idx[n.p][:, :]).then_inc(route_stored[n.p], 16)

            def load_xr(b):
                if not early(b, 2):
                    sp.wait_ge(xa_stored[b.p], b.own(16, 0))
                sp.dma_start(xr[b.p][:, :, :], x_d[bass.ds(b.hi * 2 + b.p, 1)].rearrange("b p j d -> p (b j) d")).then_inc(xr_loaded[b.p], 16)

            def store_xa(b):
                sp.wait_ge(xa_ready, b.at(1, 1))
                sp.dma_start(xa_d[bass.ds(b.hi * 2 + b.p, 1)].rearrange("b p j d -> p (b j) d"), xr[b.p][:, :, :]).then_inc(xa_stored[b.p], 16)

            def body(b, first, last):
                if not (b.known() is not None and b.known() + 2 >= B):
                    load_x(b + 2)
                if not first:
                    store_xa(b + -1)
                load_xr(b)
                if not last:
                    store_parts(b + 1)
                    load_parts(b + 1)
                    store_route(b + 1)

            store_parts(Turn(0, 0))
            load_parts(Turn(0, 0))
            store_route(Turn(0, 0))
            over_batches(sp, body)
            for p in range(2):
                sp.wait_ge(route_stored[p], 32 * HALVES)
                sp.wait_ge(scattered[p], 16 * 2 * J * HALVES)
            sp.dma_start(idx_all[:, :].rearrange("p (b k) -> p b k", b=B), slot_d.rearrange("b p k -> p b k")).then_inc(slots_loaded, 16)
            sp.wait_ge(plan_ready, 1)
            for e in range(E):
                k = 2 * NTILES + e
                first_free = sp.value_load(tab[0:1, k:k + 1], min_val=0, max_val=NROWS - GT)
                sp.dma_start(xs_d[bass.ds(first_free, GT), :].rearrange("(c p) d -> p c d", p=128), zeros[:, :, :]).then_inc(pad_zeroed, 16)
            sp.wait_ge(pad_zeroed, 16 * E)
            sp.wait_ge(dummy_zeroed, 16 * SPARE)
            store_xa(AFTER + -1)

            def load_tile(t):
                at = t.hi * TB + t.p
                first_row = sp.value_load(tab[0:1, bass.ds(at, 1)], min_val=0, max_val=NROWS - GT)
                expert = sp.value_load(tab[0:1, bass.ds(at + NTILES, 1)], min_val=0, max_val=E - 1)
                if not t.less(TB):
                    sp.wait_ge(xgT_ps, t.at(1, 1 - TB))
                sp.dma_start(xg[t.p], xs_d[bass.ds(first_row, GT), :].rearrange("(c p) d -> p c d", p=128)).then_inc(xg_loaded[t.p], 16)
                if not t.less(TB):
                    sp.wait_ge(ey_ps, t.at(1, 1 - TB))
                sp.dma_start(wfc[t.p], io["fc"][bass.ds(expert, 1)].rearrange("e p f -> p (e f)")).then_inc(w_loaded[t.p], 16)
                sp.dma_start(wpj[t.p], io["proj"][bass.ds(expert, 1)].rearrange("e p k d -> p (e k) d")).then_inc(w_loaded[t.p], 16)

            def tile(t):
                load_tile(t)
                if t.known() == TB - 1:
                    sp.wait_ge(rows_ready, 1)
                    sp.dma_start(idx_d.rearrange("b p k -> p b k"), idx_all[:, :].rearrange("p (b k) -> p b k", b=B)).then_inc(rows_stored, 16)

            over_tiles(sp, tile)
            for p in range(2):
                sp.wait_ge(xa_stored[p], 16 * HALVES)
            for p in range(TB):
                sp.wait_ge(ys_stored[p], 16 * (NTILES // TB))

            sp.wait_ge(rows_stored, 16)

            def load_route(n):
                if not n.less(L2 + 2):
                    sp.wait_ge(x1_ready, (n + -1).at(J, -J * L2))
                sp.dma_start(wts[n.p][:, :, :].rearrange("p c j -> p (c j)"), wts_d[row2(n)].rearrange("b p k -> p (b k)")).then_inc(route_loaded[n.p], 16)
                sp.dma_start(idx[n.p][:, :], idx_d[row2(n)].rearrange("b p k -> p (b k)")).then_inc(route_loaded[n.p], 16)

            def load_xa(n):
                if not n.less(L2 + 2):
                    sp.wait_ge(x1_ready, (n + -1).at(J, -J * L2))
                sp.dma_start(xt[n.p][:, :, :], xa_d[row2(n)].rearrange("b p j d -> p (b j) d")).then_inc(xa_loaded[n.p], 16)

            def load_half(n, h):
                stored = value(sp, n.at(16, 16))
                if not n.less(L2 + 2):
                    sp.wait_ge(s_ps, (n + -2).at(PASS, (h + 1) * PASS // 2 - PASS * L2))
                hs = slice(h * H // 2, (h + 1) * H // 2)
                for c, row0, part, parts_ in LOADS:
                    if row0 == 0:
                        sp.wait_ge(parts_stored[c], stored)
                    sp.dma_start((QT, KT)[c][n.p][row0:row0 + parts_ * DH, hs, :],
                                 parts_d[n.p, c, part:part + parts_].rearrange("a (d h) t -> (a d) h t", d=DH)[:, hs, :]
                                 ).then_inc(half_loaded[n.p][h], 16)

            def store_parts2(n):
                copied = value(sp, n.own(16 * QK_LOADS, -16 * QK_LOADS * HALVES))
                split_ = [value(sp, n.at(2, c + 1)) for c in range(2)]
                for c in range(2):
                    sp.wait_ge(lo_part, split_[c])
                    for h in range(2):
                        if not n.less(L2 + 2):
                            sp.wait_ge(half_loaded[n.p][h], copied)
                    sp.dma_start(parts_d[n.p, c].rearrange("a p t -> p a t"), parts[c][:, :, :]).then_inc(parts_stored[c], 16)

            def body2(b):
                if b.known() == L2 - 2:
                    load_route(b + 2)
                    load_xa(b + 2)
                if within(b + 3):
                    load_route(b + 3)
                if within(b + 3):
                    load_xa(b + 3)
                if within(b + 2):
                    store_parts2(b + 2)
                    load_half(b + 2, 0)
                    load_half(b + 2, 1)

            over_layer2(sp, body2)
            for p in range(2):
                sp.wait_ge(out_stored[p], 16 * HALVES)
                sp.wait_ge(shift_stored[p], 16 * HALVES)

        @block.gpsimd
        def _(pool):
            for p in range(2):
                nc.gpsimd.memset(V[p][:, :, :, :], 0.0).then_inc(ready_consts, 1)
                nc.gpsimd.memset(xnT[p][:, 0:1], 0.0).then_inc(ready_consts, 1)
            nc.gpsimd.memset(eps[:, :], LN_EPS).then_inc(ready_consts, 1)
            for p in range(2):
                nc.gpsimd.memset(state[p], 0.0).then_inc(ready_consts, 1)
            pool.wait_ge(ready_consts, 7)
            for p in range(2):
                nc.gpsimd.memset(V[p][:, :, :, DH:DH + 1], 1.0).then_inc(ready_consts, 1)
            pool.wait_ge(consts_loaded, 16 * CONSTS)

            def mask(b, s, g):
                pool.wait_ge(a_sb, b.at(H, G * s + g + 1))
                blocks = P[s % 2][:, g, :].rearrange("p (j c) -> p j c", c=128)
                nc.gpsimd.tensor_tensor(blocks, blocks, tri[:, :, :], ALU.mult).then_inc(a_masked, 1)

            def scatter(n, ks):
                written = value(pool, n.at(1, 1))
                pool.wait_ge(consts_loaded, 16 * CONSTS)
                pool.wait_ge(slots_ready, written)
                for k in ks:
                    nc.gpsimd.indirect_dma_start(
                        xs_d[:, :], bass.IndirectOffsetOnAxis(ap=idx[n.p][:, k:k + 1], axis=0),
                        xn[n.p][:, k % J, :], None).then_inc(scattered[n.p], 16)

            def body(b, first, last):
                for s in range(SHEETS):
                    for g in range(G):
                        mask(b, s, g)
                    if s < SHEETS - 1:
                        scatter(b, range(3 * s, min(3 * s + 3, 2 * J)))

            over_batches(pool, body)

            def store_tile(t):
                count_ = value(pool, t.at(1, 1))
                pool.wait_ge(consts_loaded, 16 * CONSTS)
                pool.wait_ge(ey_sb, count_)
                pool.dma_start(ys_d[bass.ds((t.hi * TB + t.p) * GT, GT), :].rearrange("(c p) d -> p c d", p=128), yg[t.p]).then_inc(ys_stored[t.p], 16)

            over_tiles(pool, store_tile)
            for p in range(TB):
                pool.wait_ge(ys_stored[p], 16 * (NTILES // TB))

            def gather(n):
                count_, summed_ = value(pool, n.own(32, 32 - 32 * HALVES)), value(pool, (n + -1).at(J, -J * L2))
                pool.wait_ge(rows_stored, 16)
                pool.wait_ge(route_loaded[n.p], count_)
                if not n.less(L2 + 2):
                    pool.wait_ge(x1_ready, summed_)
                for k in range(2 * J):
                    nc.gpsimd.indirect_dma_start(ya[n.p][:, k, :], None, ys_d[:, :],
                                                 bass.IndirectOffsetOnAxis(ap=idx[n.p][:, k:k + 1], axis=0)).then_inc(gathered[n.p], 16)

            def shift_rows(n):
                count_ = value(pool, n.at(1, 1 - L2))
                pool.wait_ge(rows_stored, 16)
                pool.wait_ge(shift_lo, count_)
                pool.wait_ge(shift_hi, n.at(1, 1 - L2))
                pool.dma_start(shift_d[n.p].rearrange("a h t -> h a t"), shift[:, :, :]).then_inc(shift_stored[n.p], 16)
                pool.wait_ge(shift_stored[n.p], n.own(16, 16 - 16 * HALVES))
                read = value(pool, (n + -1).at(PASS, -PASS * L2))
                pool.wait_ge(rows_stored, 16)
                if not n.less(L2 + 2):
                    pool.wait_ge(s_ps, read)
                pool.dma_start(QT[n.p][SHIFT0:SROWS, :, :], shift_d[n.p]).then_inc(shift_loaded[n.p], 16)

            def store_out(b):
                count_ = value(pool, b.at(1, 1 - L2))
                pool.wait_ge(rows_stored, 16)
                pool.wait_ge(out_ready, count_)
                pool.dma_start(out_d[row2(b)].rearrange("b p j d -> p (b j) d"), xr[b.p][:, :, :]).then_inc(out_stored[b.p], 16)

            def body2(b):
                if b.known() == L2 - 2:
                    gather(b + 2)
                if within(b + 3):
                    gather(b + 3)
                if within(b + -1):
                    store_out(b + -1)
                if within(b + 1):
                    shift_rows(b + 1)

            over_layer2(pool, body2)

        @block.scalar
        def _(act):
            act.wait_ge(ready_consts, 9)
            act.wait_ge(consts_loaded, 16 * CONSTS)

            def ln_sqrt(n):
                act.wait_ge(ln_mean, n.at(J, J))
                nc.scalar.activation(std[:, :], mv[:, :, 1], ACT.Sqrt, bias=eps[:, 0:1]).then_inc(ln_std, 1)

            def evac_xnT(n):
                act.wait_ge(xnT_ps, n.at(1, 1))
                nc.scalar.copy(xnT[n.p][:, 1:T + 1], W6[:, :]).then_inc(xnT_sb, 1)

            def exps(n):
                for c in range(2):
                    act.wait_ge(rot_min, n.at(2, c + 1))
                    nc.scalar.activation(ee[c][:, :], t2[c][:, :], ACT.Exp).then_inc(rot_exp, 1)

            def hi(n):
                for c in range(2):
                    act.wait_ge(phi, n.at(2, c + 1))
                    if not early(n, 1):
                        act.wait_ge(parts_stored[c], n.at(16, 0))
                    nc.scalar.copy(parts[c][:, 0, :], qf[n.p] if c == 0 else t2[1][:, :]).then_inc(hi_part, 1)

            def mid(n):
                for c in range(2):
                    act.wait_ge(res_part, n.at(2, c + 1))
                    nc.scalar.copy(parts[c][:, 1, :], t1[c][:, :]).then_inc(mid_part, 1)

            def evac_v(n):
                for k, w in enumerate((W5, W6)):
                    act.wait_ge(v_ps, n.at(2, k + 1))
                    nc.scalar.copy(V[n.p][:, 2 * k:2 * k + 2, :, 0:DH],
                                   w[:, 0:2 * (128 + E)].rearrange("p (j c) -> p j c", j=2)[:, :, 0:128]
                                   .rearrange("p j (h d) -> p j h d", d=DH)).then_inc(v_sb, 1)

            def exp_router(n):
                act.wait_ge(router_in, n.at(1, 1))
                nc.scalar.activation(pr[:, :, :], lg[:, :, :], ACT.Exp).then_inc(router_exp, 1)

            def evac_oT(b, s):
                act.wait_ge(pv_done, b.at(SHEETS, s + 1))
                if not (early(b, 1) and s < 2):
                    act.wait_ge(oTT_ps, b.at(SHEETS, s - 1))
                nc.scalar.copy(oT[s % 2][:, :], OT[:, :]).then_inc(oT_sb, 1)

            def evac_yT(b):
                act.wait_ge(yT_ps, b.at(1, 1))
                nc.scalar.copy(yT[:, :], W6[:, :]).then_inc(yT_sb, 1)

            def relu_h(b, k):
                act.wait_ge(fc_ps, b.at(NB, k + 1))
                if not (early(b, 1) and k < 2):
                    act.wait_ge(h_sq, b.at(NB, k - 1))
                nc.scalar.activation(hr[k % 2][:, :], (W5, W6)[k % 2][:, :], ACT.Relu).then_inc(h_relu, 1)

            def evac_s(b, s):
                for g in range(G):
                    if g == 0 and not (early(b, 1) and s < 2):
                        act.wait_ge(pv_done, b.at(SHEETS, s - 1))
                    act.wait_ge(a_ps, b.at(H, G * s + g + 1))
                    nc.scalar.copy(P[s % 2][:, g, :], bank[g][:, :]).then_inc(a_sb, 1)

            def evac_ktok(n):
                act.wait_ge(kT_ps, n.at(1, 1))
                if not early(n, 1):
                    act.wait_ge(state_ps, n.at(1, 0))
                nc.scalar.copy(ktok, W6[:, 0:(J - 1) * 128].rearrange("p (j c) -> p j c", c=128)).then_inc(ktok_sb, 1)

            def front(n):
                exps(n)
                hi(n)
                mid(n)
                evac_v(n)
                evac_ktok(n)
                exp_router(n)

            def body(b, first, last):
                if not first:
                    evac_oT(b + -1, 3)
                evac_s(b, 0)
                if not last:
                    evac_xnT(b + 1)
                evac_s(b, 1)
                if not first:
                    evac_yT(b + -1)
                evac_oT(b, 0)
                evac_s(b, 2)
                if not last:
                    exps(b + 1)
                evac_oT(b, 1)
                if not last:
                    hi(b + 1)
                evac_s(b, 3)
                if not last:
                    evac_v(b + 1)
                    mid(b + 1)
                evac_oT(b, 2)
                if not last:
                    evac_ktok(b + 1)
                    exp_router(b + 1)
                if not (b.known() is not None and b.known() + 2 >= B):
                    ln_sqrt(b + 2)
                for k in range(NB):
                    relu_h(b, k)

            ln_sqrt(Turn(0, 0))
            evac_xnT(Turn(0, 0))
            front(Turn(0, 0))
            ln_sqrt(Turn(0, 1))
            over_batches(act, body)
            evac_oT(AFTER + -1, 3)
            evac_yT(AFTER + -1)

            def tile(t):
                act.wait_ge(xgT_ps, t.at(1, 1))
                if not t.less(2):
                    act.wait_ge(efc_ps, (t + -1).at(2, 0))
                nc.scalar.copy(xgT[t.p % 2], bank[t.p % 2][:, 0:GT]).then_inc(xgT_sb, 1)
                for k in range(2):
                    act.wait_ge(efc_ps, t.at(2, k + 1))
                    if not t.less(1):
                        act.wait_ge(e_sq, t.at(2, k - 1))
                    nc.scalar.activation(hr[k][:, :], bank[2 + 2 * (t.p % 2) + k][:, :], ACT.Relu).then_inc(e_relu, 1)

            over_tiles(act, tile)

            def hi2(n, c):
                act.wait_ge(qk_ps, n.at(2, c + 1))
                act.wait_ge(parts_stored[c], n.at(16, 0))
                nc.scalar.copy(parts[c][:, 0, :], (W5, W6)[c][:, :]).then_inc(hi_part, 1)

            def mid2(n, c):
                act.wait_ge(res_part, n.at(2, c + 1))
                nc.scalar.copy(parts[c][:, 1, :], t1[c][:, :]).then_inc(mid_part, 1)

            def evac_v2(n):
                act.wait_ge(v2_ps, n.at(1, 1 - L2))
                nc.scalar.copy(V[n.p][:, :, :, 0:DH], W5[:, :].rearrange("p (j h d) -> p j h d", j=J, d=DH)).then_inc(v2_sb, 1)

            def shift_high(n):
                act.wait_ge(maxT_ps, n.at(1, 1 - L2))
                if not n.less(L2 + 1):
                    act.wait_ge(shift_stored[1 - n.p], (n + -1).own(16, 16 - 16 * HALVES))
                nc.scalar.copy(shift[:, 0, :], W6[0:H, :]).then_inc(shift_hi, 1)

            def exp_scores(b, s, u):
                k = s * UNITS + u
                if u == 0 and not (b.less(L2 + 1) and s < 2):
                    act.wait_ge(pv_done, b.at(SHEETS, s - 1))
                act.wait_ge(s_ps, b.at(PASS, k + 1 - PASS * L2))
                nc.scalar.activation(P[s % 2][:, u, :], bank[k % 2][:, :], ACT.Exp, scale=float(DH) ** -0.5).then_inc(s_sb, 1)

            def square_k(n):
                act.wait_ge(k_ps, n.at(1, 1 - L2))
                nc.scalar.activation(hr[0][:, :], W5[:, :], ACT.Relu).then_inc(k_relu, 1)
                act.wait_ge(k_relu, n.at(1, 1 - L2))
                nc.scalar.activation(hr[1][:, :], hr[0][:, :], ACT.Square).then_inc(k_sq, 1)

            def tanh_r(n):
                act.wait_ge(r_ps, n.at(1, 1 - L2))
                nc.scalar.activation(ee[0][:, :], W6[:, :], ACT.Tanh, scale=0.5).then_inc(r_tanh, 1)

            def exp_gate(b):
                act.wait_ge(fhn_stim, b.at(1, 1 - L2))
                nc.scalar.activation(fhn[3][:, :, :], fhn[0][:, :, :], ACT.Exp, bias=five[:, 0:1], scale=-10.0).then_inc(fhn_gate, 1)

            def exp_resp(b):
                act.wait_ge(fhn_resp, b.at(1, 1 - L2))
                nc.scalar.activation(fhn[3][:, :, :], fhn[2][:, :, :], ACT.Exp, scale=-1.0).then_inc(fhn_sig, 1)

            def body2(b):
                core, front, after, before_ = within(b), within(b + 2), within(b + 1), within(b + -1)
                for s in range(SHEETS):
                    for u in range(UNITS):
                        at = (s, u)
                        if at == (0, 0) and before_:
                            evac_oT(b + -1, 3)
                        if at == (1, 0) and front:
                            ln_sqrt(b + 2)
                        if at == (1, 3) and front:
                            evac_xnT(b + 2)
                        if at == (1, 4) and before_:
                            exp_gate(b + -1)
                        if at in ((2, 0), (2, 3)) and front:
                            hi2(b + 2, u // 3)
                        if s > 0 and u == 8 and core:
                            evac_oT(b, s - 1)
                        if at in ((2, 2), (2, 6)) and front:
                            mid2(b + 2, u // 6)
                        if at == (2, 5) and before_:
                            exp_resp(b + -1)
                        if at == (2, 9) and after:
                            evac_v2(b + 1)
                        if at == (3, 4) and before_:
                            evac_yT(b + -1)
                        if core:
                            exp_scores(b, s, u)
                if after:
                    shift_high(b + 1)
                    square_k(b + 1)
                    tanh_r(b + 1)

            over_layer2(act, body2)

        @block.vector
        def _(dve):
            nc.vector.memset(zeros[:, :, :], 0.0).then_inc(zeroed, 1)

            LR = 5

            def ln_moments(n, first_layer=True):
                if not first_layer:
                    dve.wait_ge(x1_ready, n.at(J, J - J * L2))
                for j in range(J):
                    nc.vector.bn_stats(stats[:, j, :], (xt if first_layer else x1)[n.p][:, j, :]).then_inc(ln_stats, 1)
                measured = value(dve, n.at(J, J))
                dve.wait_ge(ready_consts, 9)
                dve.wait_ge(ln_stats, measured)
                for j in range(J):
                    nc.vector.bn_aggr(mv[:, j, :], stats[:, j, :]).then_inc(ln_mean, 1)

            def ln(n, first_layer=True):
                dve.wait_ge(ln_std, n.at(1, 1))
                nc.vector.reciprocal(rstd[:, :], std[:, :]).then_inc(ln_rstd, 1)
                dve.wait_ge(ln_rstd, n.at(LR, 1))
                nc.vector.tensor_tensor(std[:, :], rstd[:, :], rstd[:, :], ALU.mult).then_inc(ln_rstd, 1)
                dve.wait_ge(ln_rstd, n.at(LR, 2))
                nc.vector.scalar_tensor_tensor(out=std[:, :], in0=mv[:, :, 1], scalar=LN_EPS, in1=std[:, :],
                                               op0=ALU.add, op1=ALU.mult).then_inc(ln_rstd, 1)
                dve.wait_ge(ln_rstd, n.at(LR, 3))
                nc.vector.tensor_scalar(std[:, :], std[:, :], -0.5, 1.5, ALU.mult, ALU.add).then_inc(ln_rstd, 1)
                dve.wait_ge(ln_rstd, n.at(LR, 4))
                nc.vector.tensor_tensor(rstd[:, :], rstd[:, :], std[:, :], ALU.mult).then_inc(ln_rstd, 1)
                dve.wait_ge(ln_rstd, n.at(LR, LR))
                if not early(n, 2) and first_layer:
                    dve.wait_ge(scattered[n.p], n.own(16 * 2 * J, 0))
                for j in range(J):
                    nc.vector.tensor_scalar(xn[n.p][:, j, :], (xt if first_layer else x1)[n.p][:, j, :], mv[:, j, 0:1], rstd[:, j:j + 1],
                                            ALU.subtract, ALU.mult).then_inc(xn_ready, 1)

            def rotate(n, c):
                dve.wait_ge(qk_ps, n.at(2, c + 1))
                nc.vector.tensor_tensor(t1[c][:, :], W5[:, :], rope[:, 0, :], ALU.mult).then_inc(rot_cos, 1)
                dve.wait_ge(qkp_ps, n.at(2, c + 1))
                nc.vector.tensor_tensor(t2[c][:, :], W6[:, :], rope[:, 1, :], ALU.mult).then_inc(rot_sin, 1)
                dve.wait_ge(rot_cos, n.at(2, c + 1))
                dve.wait_ge(rot_sin, n.at(2, c + 1))
                nc.vector.tensor_tensor(t1[c][:, :], t1[c][:, :], t2[c][:, :], ALU.add).then_inc(rot, 1)
                dve.wait_ge(rot, n.at(2, c + 1))
                nc.vector.tensor_scalar(t2[c][:, :], t1[c][:, :], 0.0, None, ALU.min).then_inc(rot_min, 1)

            def states(n):
                dve.wait_ge(state_ps, n.at(1, 1))
                if not early(n, 2):
                    dve.wait_ge(pv_done, (n + -1).at(SHEETS, 0))
                nc.vector.tensor_tensor(state[n.p][:, :, :, 0:DH + 1],
                                        W5[:, 0:(J - 1) * H * (DH + 1)].rearrange("p (j h c) -> p j h c", j=J - 1, h=H),
                                        own[:, :, :].unsqueeze(1).to_broadcast([128, J - 1, H, DH + 1]), ALU.mult).then_inc(state_sb, 1)

            def feature(n):
                for c in range(2):
                    dve.wait_ge(rot_exp, n.at(2, c + 1))
                    if c == 0 and not early(n, 2):
                        dve.wait_ge(pv_done, (n + -1).at(SHEETS, 0))
                    nc.vector.scalar_tensor_tensor(out=qf[n.p] if c == 0 else t2[1][:, :], in0=t1[c][:, :], scalar=0.0, in1=ee[c][:, :],
                                                   op0=ALU.max, op1=ALU.add).then_inc(phi, 1)

            def split(n):
                residue(n)
                low(n)

            def residue(n):
                for c in range(2):
                    dve.wait_ge(hi_part, n.at(2, c + 1))
                    dve.wait_ge(phi, n.at(2, c + 1))
                    nc.vector.tensor_tensor(t1[c][:, :], qf[n.p] if c == 0 else t2[1][:, :], parts[c][:, 0, :],
                                            ALU.subtract).then_inc(res_part, 1)

            def low(n):
                for c in range(2):
                    dve.wait_ge(mid_part, n.at(2, c + 1))
                    dve.wait_ge(res_part, n.at(2, c + 1))
                    nc.vector.tensor_tensor(parts[c][:, 2, :], t1[c][:, :], parts[c][:, 1, :], ALU.subtract).then_inc(lo_part, 1)

            def logits_out(n):
                for k, w in enumerate((W5, W6)):
                    dve.wait_ge(v_sb, n.at(2, k + 1))
                    nc.vector.tensor_copy(lg[:, 2 * k:2 * k + 2, :],
                                          w[:, 0:2 * (128 + E)].rearrange("p (j c) -> p j c", j=2)[:, :, 128:]).then_inc(logits, 1)

            def router(n):
                RS = 13
                done = [0]

                def step(ins):
                    done[0] += 1
                    ins.then_inc(router_step, 1)
                    dve.wait_ge(router_step, n.at(RS, done[0]))

                dve.wait_ge(logits, n.at(2, 2))
                step(nc.vector.tensor_reduce(lmax[:, :], lg[:, :, :], AX.X, ALU.max))
                nc.vector.tensor_tensor(lg[:, :, :], lg[:, :, :], lmax[:, :].unsqueeze(2).to_broadcast([128, J, E]),
                                        ALU.subtract).then_inc(router_in, 1)
                dve.wait_ge(router_exp, n.at(1, 1))
                step(nc.vector.tensor_reduce(psum_[:, :], pr[:, :, :], AX.X, ALU.add))
                step(nc.vector.reciprocal(psum_[:, :], psum_[:, :]))
                step(nc.vector.tensor_tensor(pr[:, :, :], pr[:, :, :], psum_[:, :].unsqueeze(2).to_broadcast([128, J, E]), ALU.mult))
                other = pr[:, :, :].unsqueeze(2).to_broadcast([128, J, E, E])
                own = pr[:, :, :].unsqueeze(3).to_broadcast([128, J, E, E])
                step(nc.vector.tensor_tensor(eq[:, :, :, :], other, own, ALU.is_equal))
                step(nc.vector.tensor_tensor(eq[:, :, :, :], eq[:, :, :, :],
                                             lower[:, :, :].unsqueeze(1).to_broadcast([128, J, E, E]), ALU.mult))
                step(nc.vector.tensor_tensor(gt[:, :, :, :], other, own, ALU.is_gt))
                step(nc.vector.tensor_tensor(gt[:, :, :, :], gt[:, :, :, :], eq[:, :, :, :], ALU.add))
                step(nc.vector.tensor_reduce(order[:, :, :], gt[:, :, :, :], AX.X, ALU.add))
                nc.vector.tensor_scalar(pickb[:, :, :], order[:, :, :], 1.5, None, ALU.is_lt).then_inc(picked, 1)
                nc.vector.tensor_scalar(pick[:, 0, :, :], order[:, :, :], 0.0, None, ALU.is_equal)
                step(nc.vector.tensor_scalar(pick[:, 1, :, :], order[:, :, :], 1.0, None, ALU.is_equal))
                step(nc.vector.tensor_tensor(prod[:, :, :, :], pick[:, :, :, :],
                                             pr[:, :, :].unsqueeze(1).to_broadcast([128, 2, J, E]), ALU.mult))
                step(nc.vector.tensor_reduce(p12[:, :, :], prod[:, :, :, :], AX.X, ALU.add))
                step(nc.vector.tensor_tensor(psum_[:, :], p12[:, 0, :], p12[:, 1, :], ALU.add))
                assert done[0] == RS

            def slots(n):
                SS = 5
                done = [0]

                def step(ins):
                    done[0] += 1
                    ins.then_inc(slots_step, 1)
                    dve.wait_ge(slots_step, n.at(SS, done[0]))

                step(nc.vector.tensor_scalar(psum_[:, :], psum_[:, :], 1e-9, None, ALU.max))
                step(nc.vector.reciprocal(psum_[:, :], psum_[:, :]))
                if not early(n, 2):
                    dve.wait_ge(route_stored[n.p], n.own(32, 0))
                    dve.wait_ge(scattered[n.p], n.own(16 * 2 * J, 0))
                nc.vector.tensor_tensor(wts[n.p][:, :, :], p12[:, :, :],
                                        psum_[:, :].unsqueeze(1).to_broadcast([128, 2, J]), ALU.mult)
                dve.wait_ge(prefix_ps, n.at(1, 1))
                if not early(n, 1):
                    dve.wait_ge(prefix_read, n.at(1, 0))
                step(nc.vector.tensor_tensor(pos[:, :, :], W6[:, 0:J * E].rearrange("p (j e) -> p j e", e=E),
                                             fill[:, :].unsqueeze(1).to_broadcast([128, J, E]), ALU.add))
                nc.vector.tensor_tensor(fill[:, :], fill[:, :], W6[:, J * E:J * E + E], ALU.add).then_inc(prefix_read, 1)
                step(nc.vector.tensor_tensor(prod[:, :, :, :], pick[:, :, :, :],
                                             pos[:, :, :].unsqueeze(1).to_broadcast([128, 2, J, E]), ALU.mult))
                step(nc.vector.tensor_reduce(slotf[:, :, :], prod[:, :, :, :], AX.X, ALU.add))
                nc.vector.tensor_copy(idx[n.p][:, :], slotf[:, :, :].rearrange("p c j -> p (c j)")).then_inc(slots_ready, 1)
                assert done[0] == SS

            def y_out(b, s):
                dve.wait_ge(oTT_ps, b.at(SHEETS, s + 1))
                nc.vector.tensor_copy(yb[:, :, G * s:G * s + G, :],
                                      W7[:, :].rearrange("p (j g c) -> p j g c", j=J, g=G)[:, :, :, 0:DH + 1]).then_inc(y_sb, 1)

            def normalise(b):
                NS = 2
                dve.wait_ge(y_sb, b.at(SHEETS, SHEETS))
                nc.vector.tensor_scalar(den[:, :, :], yb[:, :, :, DH], DEN_EPS, None, ALU.max).then_inc(norm_step, 1)
                dve.wait_ge(norm_step, b.at(NS, 1))
                nc.vector.reciprocal(rden[:, :, :], den[:, :, :]).then_inc(norm_step, 1)
                dve.wait_ge(norm_step, b.at(NS, 2))
                nc.vector.tensor_tensor(y[:, :, :, :], yb[:, :, :, 0:DH],
                                        rden[:, :, :].unsqueeze(3).to_broadcast([128, J, H, DH]), ALU.mult).then_inc(y_ready, 1)

            def square_h(b, k):
                dve.wait_ge(h_relu, b.at(NB, k + 1))
                if k == 0 and not early(b, 1):
                    dve.wait_ge(proj_ps, b.at(1, 0))
                h = hr[k % 2][:, :].rearrange("p (c t) -> p c t", c=2)
                nc.vector.tensor_tensor(hT[:, :, k, :], h, h, ALU.mult).then_inc(h_sq, 1)

            def residual(b):
                dve.wait_ge(proj_ps, b.at(1, 1))
                dve.wait_ge(xr_loaded[b.p], b.own(16, 16))
                nc.vector.tensor_tensor(xr[b.p][:, :, :], xr[b.p][:, :, :],
                                        W7[:, :].rearrange("p (j d) -> p j d", j=J), ALU.add).then_inc(xa_ready, 1)

            def front(n):
                rotate(n, 0)
                rotate(n, 1)
                feature(n)
                split(n)
                logits_out(n)
                states(n)
                router(n)
                slots(n)

            def body(b, first, last):
                if not first:
                    y_out(b + -1, 3)
                    normalise(b + -1)
                if not last:
                    rotate(b + 1, 0)
                if not first:
                    residual(b + -1)
                y_out(b, 0)
                if not last:
                    rotate(b + 1, 1)
                    feature(b + 1)
                if not last:
                    residue(b + 1)
                    logits_out(b + 1)
                    low(b + 1)
                more = not (b.known() is not None and b.known() + 2 >= B)
                if more:
                    dve.wait_ge(x_loaded[b.p], (b + 2).own(16, 16))
                    ln_moments(b + 2)
                y_out(b, 1)
                if not last:
                    states(b + 1)
                    router(b + 1)
                y_out(b, 2)
                for k in range(NB):
                    square_h(b, k)
                if not last:
                    slots(b + 1)
                if more:
                    ln(b + 2)

            dve.wait_ge(ready_consts, 9)
            dve.wait_ge(x_loaded[0], 16)
            ln_moments(Turn(0, 0))
            ln(Turn(0, 0))
            dve.wait_ge(consts_loaded, 16 * CONSTS)
            nc.vector.tensor_copy(fill[:, :], ebase[:, 0, :]).then_inc(zeroed, 1)
            dve.wait_ge(zeroed, 2)
            front(Turn(0, 0))
            dve.wait_ge(x_loaded[1], 16)
            ln_moments(Turn(0, 1))
            ln(Turn(0, 1))
            over_batches(dve, body)

            planned = [0]

            def plan(ins):
                planned[0] += 1
                ins.then_inc(plan_step, 1)
                dve.wait_ge(plan_step, planned[0])

            cnt, (nt, end, start) = count[:, :], [ntile[:, k, :] for k in range(3)]
            wide = [128, E, NTILES]
            cmp = gt[:, :, :, :].rearrange("p a b c -> p (a b c)")[:, 0:E * (CAP // GT)].rearrange("p (e k) -> p e k", e=E)
            cum = eq[:, 0, :, :]
            dve.wait_ge(prefix_read, B)
            dve.wait_ge(pv_done, SHEETS * B - 1)
            plan(nc.vector.tensor_tensor(cnt, fill[:, :], ebase[:, 0, :], ALU.subtract))
            plan(nc.vector.tensor_tensor(cmp, cnt.unsqueeze(2).to_broadcast([128, E, CAP // GT]),
                                         steps[:, :].unsqueeze(1).to_broadcast([128, E, CAP // GT]), ALU.is_gt))
            plan(nc.vector.tensor_reduce(nt, cmp, AX.X, ALU.add))
            plan(nc.vector.tensor_tensor(cum, incl[:, :, :], nt.unsqueeze(1).to_broadcast([128, E, E]), ALU.mult))
            plan(nc.vector.tensor_reduce(end, cum, AX.X, ALU.add))
            plan(nc.vector.tensor_tensor(start, end, nt, ALU.subtract))
            number = tiles[:, 0, :].unsqueeze(1).to_broadcast(wide)
            plan(nc.vector.tensor_tensor(big[:, 0, :, :], number, start.unsqueeze(2).to_broadcast(wide), ALU.is_ge))
            plan(nc.vector.tensor_tensor(big[:, 1, :, :], number, end.unsqueeze(2).to_broadcast(wide), ALU.is_lt))
            plan(nc.vector.tensor_tensor(big[:, 0, :, :], big[:, 0, :, :], big[:, 1, :, :], ALU.mult))
            plan(nc.vector.scalar_tensor_tensor(out=cnt, in0=start, scalar=float(-GT), in1=ebase[:, 0, :], op0=ALU.mult, op1=ALU.add))
            plan(nc.vector.tensor_tensor(big[:, 1, :, :], tiles[:, 1, :].unsqueeze(1).to_broadcast(wide),
                                         cnt.unsqueeze(2).to_broadcast(wide), ALU.add))
            plan(nc.vector.tensor_tensor(big[:, 1, :, :], big[:, 1, :, :], big[:, 0, :, :], ALU.mult))
            plan(nc.vector.tensor_tensor(big[:, 2, :, :], big[:, 0, :, :], ebase[:, 1, :].unsqueeze(2).to_broadcast(wide), ALU.mult))
            for k in range(2):
                plan(nc.vector.tensor_reduce(tabf[:, k, :], big[:, 1 + k, :, :].rearrange("p e t -> p t e"), AX.X, ALU.add))
            plan(nc.vector.tensor_tensor(tab[:, 0:NTILES], tabf[:, 0, :], tiles[:, 2, :], ALU.add))
            plan(nc.vector.tensor_copy(tab[:, NTILES:2 * NTILES], tabf[:, 1, :]))
            nc.vector.tensor_copy(tab[:, 2 * NTILES:], fill[:, :]).then_inc(plan_ready, 1)
            y_out(AFTER + -1, 3)
            normalise(AFTER + -1)
            residual(AFTER + -1)
            every = [128, B * 2 * J, E - 1]
            plan(nc.vector.tensor_scalar(nt, nt, float(GT), float(-REGION), ALU.mult, ALU.add))
            dve.wait_ge(slots_loaded, 16)
            plan(nc.vector.tensor_copy(slot_all, idx_all[:, :]))
            plan(nc.vector.tensor_tensor(above, slot_all.unsqueeze(2).to_broadcast(every),
                                         ebase[:, 0, 1:E].unsqueeze(1).to_broadcast(every), ALU.is_ge))
            plan(nc.vector.tensor_tensor(above, above, nt[:, 0:E - 1].unsqueeze(1).to_broadcast(every), ALU.mult))
            plan(nc.vector.tensor_reduce(moved[:, :], above, AX.X, ALU.add))
            nc.vector.tensor_tensor(idx_all[:, :], slot_all, moved[:, :], ALU.add).then_inc(rows_ready, 1)

            def square_tile(t):
                for k in range(2):
                    dve.wait_ge(e_relu, t.at(2, k + 1))
                    if k == 0 and not t.less(2):
                        dve.wait_ge(ey_ps, t.at(1, -1))
                    h = hr[k][:, :].rearrange("p (k t) -> p k t", k=2)
                    nc.vector.tensor_tensor(hT[:, t.p % 2, 2 * k:2 * k + 2, :], h, h, ALU.mult).then_inc(e_sq, 1)

            def evac_tile(t):
                dve.wait_ge(ey_ps, t.at(1, 1))
                if not t.less(TB):
                    dve.wait_ge(ys_stored[t.p], t.own(16, 0))
                nc.vector.tensor_copy(yg[t.p], bank[6 + t.p % 2][:, 0:GT].rearrange("p (c d) -> p c d", d=D)).then_inc(ey_sb, 1)

            def tile(t):
                square_tile(t)
                if not t.less(1):
                    evac_tile(t + -1)

            over_tiles(dve, tile)
            evac_tile(Turn(NTILES // TB, 0, TB) + -1)

            nc.vector.memset(five[:, :], 5.0).then_inc(setup2, 1)
            nc.vector.tensor_scalar(omu[:, :], mu[:, :], -1.0, 1.0, ALU.mult, ALU.add).then_inc(setup2, 1)
            nc.vector.tensor_scalar(alpha[:, :], abd[:, 2:3], 1.0 / TAU, None, ALU.mult).then_inc(setup2, 1)
            dve.wait_ge(setup2, 3)
            nc.vector.tensor_tensor(one_b[:, :], alpha[:, :], abd[:, 1:2], ALU.mult).then_inc(setup2, 1)
            dve.wait_ge(setup2, 4)
            nc.vector.tensor_scalar(one_b[:, :], one_b[:, :], 1.0, None, ALU.add).then_inc(setup2, 1)
            dve.wait_ge(setup2, 5)
            nc.vector.reciprocal(rdamp[:, :], one_b[:, :]).then_inc(setup2, 1)
            dve.wait_ge(setup2, 6)

            def combine(n, c):
                if c == 0:
                    combine_waits(n)
                for j in range(J):
                    x = x1[n.p][:, j, :]
                    if c == 1:
                        dve.wait_ge(summed, n.at(J, j + 1 - J * L2))
                    nc.vector.scalar_tensor_tensor(out=x, in0=ya[n.p][:, c * J + j, :], scalar=wts[n.p][:, c, j:j + 1],
                                                   in1=x if c else xt[n.p][:, j, :], op0=ALU.mult, op1=ALU.add).then_inc(x1_ready if c else summed, 1)

            def combine_waits(n):
                dve.wait_ge(xa_loaded[n.p], n.own(16, 16 - 16 * HALVES))
                dve.wait_ge(gathered[n.p], n.own(32 * J, 32 * J - 32 * J * HALVES))
                if not n.less(L2 + 2):
                    dve.wait_ge(res_ready, (n + -1).at(1, -L2))

            def row_max(n, k):
                s, (j, g, nh) = k // MU, MAX_UNITS[k % MU]
                h = G * s + g
                dve.wait_ge(max_ps, n.at(MU * SHEETS, k + 1 - MU * SHEETS * L2))
                w = 128 * (j + 1)
                nc.vector.tensor_reduce(nmax[:, j, h:h + nh], bank[2 + k % 2][:, 0:nh * w].rearrange("p (h w) -> p h w", h=nh),
                                        AX.X, ALU.max, negate=True).then_inc(max_read, 1)

            def residue2(n, c):
                dve.wait_ge(hi_part, n.at(2, c + 1))
                nc.vector.tensor_tensor(t1[c][:, :], (W5, W6)[c][:, :], parts[c][:, 0, :], ALU.subtract).then_inc(res_part, 1)

            def low2(n, c):
                dve.wait_ge(mid_part, n.at(2, c + 1))
                dve.wait_ge(res_part, n.at(2, c + 1))
                nc.vector.tensor_tensor(parts[c][:, 2, :], t1[c][:, :], parts[c][:, 1, :], ALU.subtract).then_inc(lo_part, 1)

            def shift_low(n):
                dve.wait_ge(shift_hi, n.at(1, 1 - L2))
                nc.vector.tensor_tensor(shift[:, 1, :], W6[0:H, :], shift[:, 0, :], ALU.subtract).then_inc(shift_lo, 1)

            def mix(n):
                for c in range(2):
                    nc.vector.tensor_scalar(t2[c][:, :], xnT[n.p][:, 1:T + 1], mu[:, c:c + 1], None, ALU.mult).then_inc(mixed, 1)
                for c in range(2):
                    dve.wait_ge(mixed, n.at(4, 1 + c - 4 * L2))
                    nc.vector.scalar_tensor_tensor(out=t2[c][:, :], in0=xnT[n.p][:, 0:T], scalar=omu[:, c:c + 1], in1=t2[c][:, :],
                                                   op0=ALU.mult, op1=ALU.add).then_inc(mixed, 1)

            def gate(n):
                dve.wait_ge(r_tanh, n.at(1, 1 - L2))
                dve.wait_ge(kv_ps, n.at(1, 1 - L2))
                nc.vector.scalar_tensor_tensor(out=ee[1][:, :], in0=ee[0][:, :], scalar=1.0, in1=W5[:, :],
                                               op0=ALU.add, op1=ALU.mult).then_inc(gated, 1)
                dve.wait_ge(gated, n.at(1, 1 - L2))
                if not n.less(L2 + 2):
                    dve.wait_ge(out_stored[n.p], n.own(16, -16 * HALVES))
                nc.vector.scalar_tensor_tensor(out=xr[n.p][:, :, :].rearrange("p j d -> p (j d)"), in0=ee[1][:, :], scalar=0.5,
                                               in1=rope[:, n.p, :], op0=ALU.mult, op1=ALU.add).then_inc(res_ready, 1)

            FS = 29
            a_, dt_ = abd[:, 0:1], abd[:, 2:3]
            f0, f1, f2, f3, f4, f5, f6, f7 = [f[:, :, :] for f in fhn]

            def fhn_chain(b, done):
                def last():
                    dve.wait_ge(fhn_step, b.at(FS, done[0] - FS * L2))

                def step(ins):
                    done[0] += 1
                    ins.then_inc(fhn_step, 1)
                return last, step

            def reweigh_stim(b, done, fill_in):
                last, step = fhn_chain(b, done)
                dve.wait_ge(y_sb, b.at(SHEETS, SHEETS))
                step(nc.vector.tensor_copy(f7, yb[:, :, :, DH]))
                fill_in()
                last()
                step(nc.vector.reciprocal(rden[:, :, :], f7))
                fill_in()
                last()
                nc.vector.tensor_tensor(f0, f7, rden[:, :, :], ALU.mult).then_inc(fhn_stim, 1)
                dve.wait_ge(fhn_stim, b.at(1, 1 - L2))
                last()
                step(nc.vector.tensor_scalar(f1, f0, 1e-6, None, ALU.max))
                fill_in()
                last()
                step(nc.vector.reciprocal(f2, f1))
                fill_in()
                last()
                step(nc.vector.tensor_tensor(f2, f0, f2, ALU.mult))

            def reweigh_steps(b, done, fill_in):
                last, step = fhn_chain(b, done)
                dve.wait_ge(fhn_gate, b.at(1, 1 - L2))
                last()
                step(nc.vector.tensor_scalar(f3, f3, 1.0, None, ALU.add))
                fill_in()
                last()
                step(nc.vector.reciprocal(f4, f3))
                fill_in()
                last()
                step(nc.vector.tensor_scalar(f4, f4, 0.9, 0.1, ALU.mult, ALU.add))
                last()
                step(nc.vector.tensor_tensor(f2, f2, f4, ALU.mult))
                fill_in()
                last()
                step(nc.vector.tensor_scalar(f3, f2, dt_, None, ALU.mult))
                last()
                step(nc.vector.tensor_scalar(f4, f3, a_, alpha[:, 0:1], ALU.add, ALU.mult))
                fill_in()
                last()
                step(nc.vector.tensor_scalar(f4, f4, rdamp[:, 0:1], -3.0, ALU.mult, ALU.max))
                last()
                step(nc.vector.tensor_scalar(f4, f4, 3.0, None, ALU.min))
                last()
                step(nc.vector.tensor_scalar(f3, f3, -3.0, 3.0, ALU.max, ALU.min))
                fill_in()
                last()
                step(nc.vector.tensor_tensor(f5, f3, f3, ALU.mult))
                last()
                step(nc.vector.tensor_tensor(f5, f5, f3, ALU.mult))
                fill_in()
                last()
                step(nc.vector.scalar_tensor_tensor(out=f5, in0=f5, scalar=-1.0 / 3.0, in1=f3, op0=ALU.mult, op1=ALU.add))
                last()
                step(nc.vector.tensor_tensor(f5, f5, f4, ALU.subtract))
                fill_in()
                last()
                step(nc.vector.tensor_tensor(f5, f5, f2, ALU.add))
                last()
                step(nc.vector.scalar_tensor_tensor(out=f5, in0=f5, scalar=dt_, in1=f3, op0=ALU.mult, op1=ALU.add))
                fill_in()
                last()
                step(nc.vector.tensor_scalar(f5, f5, -3.0, 3.0, ALU.max, ALU.min))
                last()
                nc.vector.tensor_tensor(f2, f5, f1, ALU.mult).then_inc(fhn_resp, 1)

            def reweigh(b, done, fill_in):
                last, step = fhn_chain(b, done)
                dve.wait_ge(fhn_sig, b.at(1, 1 - L2))
                last()
                step(nc.vector.tensor_scalar(f3, f3, 1.0, None, ALU.add))
                fill_in()
                last()
                step(nc.vector.reciprocal(f4, f3))
                fill_in()
                last()
                step(nc.vector.tensor_scalar(f4, f4, 0.5, 0.5, ALU.mult, ALU.add))
                last()
                step(nc.vector.tensor_tensor(f5, f0, f4, ALU.mult))
                last()
                step(nc.vector.tensor_scalar(f5, f5, 1e-8, None, ALU.add))
                fill_in()
                last()
                step(nc.vector.tensor_tensor(f4, f4, rden[:, :, :], ALU.mult))
                last()
                step(nc.vector.reciprocal(f6, f5))
                fill_in()
                last()
                step(nc.vector.tensor_tensor(f6, f6, f4, ALU.mult))
                fill_in()
                last()
                nc.vector.tensor_tensor(y[:, :, :, :], yb[:, :, :, 0:DH],
                                        f6.unsqueeze(3).to_broadcast([128, J, H, DH]), ALU.mult).then_inc(y_ready, 1)
                assert done[0] == FS

            def output(b):
                dve.wait_ge(proj2_ps, b.at(1, 1 - L2))
                dve.wait_ge(res_ready, b.at(1, 1 - L2))
                nc.vector.tensor_tensor(xr[b.p][:, :, :], xr[b.p][:, :, :],
                                        W5[:, :].rearrange("p (j d) -> p j d", j=J), ALU.add).then_inc(out_ready, 1)

            def body2(b):
                core, front, after, before_ = within(b), within(b + 2), within(b + 1), within(b + -1)
                at, done = [0], [0]

                def maxes(n=1):
                    for _ in range(n):
                        if after and at[0] < MU * SHEETS:
                            row_max(b + 1, at[0])
                            at[0] += 1

                def maxes_to(k):
                    if at[0] < k:
                        maxes(k - at[0])

                maxes_to(1)
                if before_:
                    y_out(b + -1, 3)
                for c in range(2):
                    maxes_to(3 + 2 * c)
                    if front:
                        combine(b + 2, c)
                maxes_to(7)
                if front:
                    ln_moments(b + 2, False)
                maxes_to(8)
                if before_:
                    reweigh_stim(b + -1, done, maxes)
                maxes_to(13)
                if front:
                    ln(b + 2, False)
                maxes_to(14)
                if after:
                    mix(b + 1)
                maxes_to(15)
                if before_:
                    reweigh_steps(b + -1, done, maxes)
                maxes_to(24)
                for c in range(2):
                    maxes_to(24 + 2 * c)
                    if front:
                        residue2(b + 2, c)
                for c in range(2):
                    maxes_to(27 + c)
                    if front:
                        low2(b + 2, c)
                maxes_to(29)
                if before_:
                    reweigh(b + -1, done, maxes)
                maxes_to(36)
                if core:
                    if not b.less(L2 + 1):
                        dve.wait_ge(y_ready, b.at(1, 0))
                    y_out(b, 0)
                maxes_to(MU * SHEETS)
                if before_:
                    output(b + -1)
                if core:
                    y_out(b, 1)
                if after:
                    shift_low(b + 1)
                if core:
                    y_out(b, 2)
                if after:
                    gate(b + 1)

            over_layer2(dve, body2)

        @block.tensor
        def _(pe):
            pe.wait_ge(consts_loaded, 16 * CONSTS)
            pe.wait_ge(ready_consts, 9)

            def turn_xn(n, first_layer=True):
                pe.wait_ge(xn_ready, n.at(J, J))
                if first_layer and not early(n, 1):
                    pe.wait_ge(prefix_read, n.at(1, 0))
                for j in range(J):
                    ins = pe.transpose(W6[:, j * 128:(j + 1) * 128], xn[n.p][:, j, :], ident[:, :])
                ins.then_inc(xnT_ps, 1)

            def project_qk(n, c):
                if c == 0:
                    pe.wait_ge(xnT_sb, n.at(1, 1))
                    if not early(n, 2):
                        pe.wait_ge(h_relu, (n + -1).at(NB, 0))
                        pe.wait_ge(yT_sb, (n + -1).at(1, 0))
                    elif not early(n, 1):
                        pe.wait_ge(state_sb, n.at(1, 0))
                else:
                    pe.wait_ge(rot_cos, n.at(2, 1))
                    pe.wait_ge(rot_sin, n.at(2, 1))
                rhs = xnT[n.p][:, 1:T + 1]
                pe.matmul(W5[:, :], wqk[:, 2 * c, :], rhs, start=True, stop=True).then_inc(qk_ps, 1)
                pe.matmul(W6[:, :], wqk[:, 2 * c + 1, :], rhs, start=True, stop=True).then_inc(qkp_ps, 1)

            def project_v(n):
                pe.wait_ge(rot_cos, n.at(2, 2))
                pe.wait_ge(rot_sin, n.at(2, 2))
                for k, w in enumerate((W5, W6)):
                    for j in range(2):
                        t0 = 1 + (2 * k + j) * 128
                        ins = pe.matmul(w[:, j * (128 + E):(j + 1) * (128 + E)], xnT[n.p][:, t0:t0 + 128], wvr[:, :],
                                        start=True, stop=True)
                    ins.then_inc(v_ps, 1)

            def prefix(n):
                pe.wait_ge(picked, n.at(1, 1))
                if early(n, 1):
                    pe.wait_ge(ktok_sb, n.at(1, 1))
                else:
                    pe.wait_ge(h_relu, n.at(NB, 0))
                for j in range(J + 1):
                    terms = [(1, i) for i in range(j)] + ([(0, j)] if j < J else [])
                    for k, (m, i) in enumerate(terms):
                        ins = pe.matmul(W6[:, j * E:(j + 1) * E], before[:, m, :], pickb[:, i, :],
                                        start=(k == 0), stop=(k == len(terms) - 1))
                ins.then_inc(prefix_ps, 1)

            def turn_k(n):
                pe.wait_ge(phi, n.at(2, 2))
                pe.wait_ge(logits, n.at(2, 2))
                for j in range(J - 1):
                    ins = pe.transpose(W6[:, j * 128:(j + 1) * 128], t2[1][:, j * 128:(j + 1) * 128], ident[:, :])
                ins.then_inc(kT_ps, 1)

            def sum_states(n):
                pe.wait_ge(ktok_sb, n.at(1, 1))
                pe.wait_ge(v_sb, n.at(2, 2))
                pe.wait_ge(logits, n.at(2, 2))
                n_state = H * (DH + 1)
                for j in range(1, J):
                    for i in range(j):
                        ins = pe.matmul(W5[:, (j - 1) * n_state:j * n_state], ktok[:, i, :], V[n.p][:, i, :, 0:DH + 1],
                                        start=(i == 0), stop=(i == j - 1))
                ins.then_inc(state_ps, 1)

            def scores(b, s):
                if s == 0:
                    pe.wait_ge(qk_loaded[b.p], b.own(16 * QK_LOADS, 16 * QK_LOADS))
                for g in range(G):
                    if not (early(b, 1) and s == 0):
                        pe.wait_ge(a_sb, b.at(H, G * (s - 1) + g + 1))
                    for j in range(J):
                        tile = slice(j * 128, (j + 1) * 128)
                        ins = pe.matmul(bank[g][:, tile], KT[b.p][0:ROWS, G * s + g, tile], QT[b.p][0:ROWS, G * s + g, tile],
                                        start=True, stop=True)
                    ins.then_inc(a_ps, 1)

            def attend(b, s):
                if s == 0:
                    pe.wait_ge(v_sb, b.at(2, 2))
                    pe.wait_ge(state_sb, b.at(1, 1))
                if not (early(b, 1) and s == 0):
                    pe.wait_ge(oT_sb, b.at(SHEETS, s))
                pe.wait_ge(a_masked, b.at(H, G * (s + 1)))
                for j in range(J):
                    tile = slice(j * 128, (j + 1) * 128)
                    if j > 0:
                        pe.matmul(OT[:, tile], state[b.p][:, j - 1, G * s:G * (s + 1), :].rearrange("p h c -> p (h c)"), qf[b.p][:, tile],
                                  start=True, stop=False, skip_group_check=True)
                    for g in range(G):
                        ins = pe.matmul(OT[32 * g:32 * g + 32, tile], V[b.p][:, j, G * s + g, :], P[s % 2][:, g, tile],
                                        start=(j == 0), stop=True, skip_group_check=True)
                ins.then_inc(pv_done, 1)

            def pv(b, s, k):
                kb, units = PV_ORDER[k]
                if k == 0:
                    if s == 0:
                        pe.wait_ge(v2_sb, b.at(1, 1 - L2))
                    pe.wait_ge(oT_sb, b.at(SHEETS, s))
                pe.wait_ge(s_sb, b.at(PASS, UNITS * s + units - PASS * L2))
                n = T - 128 * kb
                for g in range(G):
                    u, c = PLACE[g, kb]
                    ins = pe.matmul(OT[32 * g:32 * g + 32, 128 * kb:T], V[b.p][:, kb, G * s + g, :],
                                    P[s % 2][:, u, c:c + n], start=(k == 0), stop=(k == J - 1), skip_group_check=True)
                if k == J - 1:
                    ins.then_inc(pv_done, 1)

            def turn_oT(b, s, first_layer=True):
                pe.wait_ge(oT_sb, b.at(SHEETS, s + 1))
                if not (early(b, 1) and s == 0):
                    pe.wait_ge(y_sb, b.at(SHEETS, s))
                if s == 0 and first_layer and not early(b, 1):
                    pe.wait_ge(xa_ready, b.at(1, 0))
                for j in range(J):
                    ins = pe.transpose(W7[:, j * 128:(j + 1) * 128], oT[s % 2][:, j * 128:(j + 1) * 128], ident[:, :])
                ins.then_inc(oTT_ps, 1)

            def turn_y(b, last):
                pe.wait_ge(y_ready, b.at(1, 1))
                if last:
                    pe.wait_ge(prefix_read, B)
                    pe.wait_ge(h_relu, b.at(NB, NB))
                else:
                    pe.wait_ge(xnT_sb, (b + 2).at(1, 1))
                for j in range(J):
                    ins = pe.transpose(W6[:, j * 128:(j + 1) * 128],
                                       y[:, j, :, :].rearrange("p h d -> p (h d)"), ident[:, :])
                ins.then_inc(yT_ps, 1)

            def shared_fc(b, k, last):
                if k >= 2:
                    pe.wait_ge(h_relu, b.at(NB, k - 1))
                elif not last:
                    pe.wait_ge((state_sb, ktok_sb)[k], (b + 1).at(1, 1))
                else:
                    pe.wait_ge((state_sb, yT_sb)[k], (b, b + -1)[k].at(1, 1))
                pe.matmul((W5, W6)[k % 2][:, :], sfc[:, k * 128:(k + 1) * 128], xnT[b.p][:, 1:T + 1], start=True, stop=True).then_inc(fc_ps, 1)

            def project_out(b):
                pe.wait_ge(yT_sb, b.at(1, 1))
                pe.wait_ge(h_sq, b.at(NB, NB))
                pe.wait_ge(y_sb, b.at(SHEETS, SHEETS))
                for j in range(J):
                    o = W7[:, j * 128:(j + 1) * 128]
                    for k in range(NB):
                        c0 = (j % 2) * 128
                        pe.matmul(o, hT[:, j // 2, k, c0:c0 + 128], spj[:, k, :], start=(k == 0), stop=False)
                    ins = pe.matmul(o, yT[:, j * 128:(j + 1) * 128], wo[:, :], start=False, stop=True)
                ins.then_inc(proj_ps, 1)

            def body(b, first, last):
                scores(b, 0)
                if not first:
                    turn_oT(b + -1, 3)
                if not last:
                    turn_xn(b + 1)
                scores(b, 1)
                if not first:
                    turn_y(b + -1, last)
                attend(b, 0)
                if not last:
                    project_qk(b + 1, 0)
                scores(b, 2)
                if not first:
                    project_out(b + -1)
                turn_oT(b, 0)
                if not last:
                    project_qk(b + 1, 1)
                attend(b, 1)
                scores(b, 3)
                if not last:
                    project_v(b + 1)
                attend(b, 2)
                turn_oT(b, 1)
                if not last:
                    turn_k(b + 1)
                    sum_states(b + 1)
                turn_oT(b, 2)
                attend(b, 3)
                for k in range(NB):
                    shared_fc(b, k, last)
                if not last:
                    prefix(b + 1)

            n0 = Turn(0, 0)
            turn_xn(n0)
            project_qk(n0, 0)
            project_qk(n0, 1)
            project_v(n0)
            turn_k(n0)
            sum_states(n0)
            prefix(n0)
            over_batches(pe, body)
            turn_oT(AFTER + -1, 3)
            turn_y(AFTER + -1, True)
            project_out(AFTER + -1)

            def turn_tile(t):
                pe.wait_ge(xg_loaded[t.p], t.own(16, 16))
                if not t.less(2):
                    pe.wait_ge(xgT_sb, t.at(1, -1))
                for c in range(GT // 128):
                    ins = pe.transpose(bank[t.p % 2][:, c * 128:(c + 1) * 128], xg[t.p][:, c, :], ident[:, :])
                ins.then_inc(xgT_ps, 1)

            def fc_tile(t):
                pe.wait_ge(xgT_sb, t.at(1, 1))
                pe.wait_ge(w_loaded[t.p], t.own(32, 32))
                for k in range(2):
                    w = bank[2 + 2 * (t.p % 2) + k]
                    if not t.less(2):
                        pe.wait_ge(e_relu, t.at(2, k - 3))
                    for i in range(2):
                        c = 2 * k + i
                        ins = pe.matmul(w[:, i * GT:(i + 1) * GT], wfc[t.p][:, c * 128:(c + 1) * 128], xgT[t.p % 2], start=True, stop=True)
                    ins.then_inc(efc_ps, 1)

            def proj_tile(t):
                pe.wait_ge(e_sq, t.at(2, 2))
                if not t.less(2):
                    pe.wait_ge(ey_sb, t.at(1, -1))
                for c in range(GT // 128):
                    for k in range(NB):
                        ins = pe.matmul(bank[6 + t.p % 2][:, c * 128:(c + 1) * 128], hT[:, t.p % 2, k, c * 128:(c + 1) * 128],
                                        wpj[t.p][:, k, :], start=(k == 0), stop=(k == NB - 1))
                ins.then_inc(ey_ps, 1)

            def tile(t):
                if t.known() is None or t.known() + 1 < NTILES:
                    turn_tile(t + 1)
                fc_tile(t)
                if not t.less(1):
                    proj_tile(t + -1)

            turn_tile(Turn(0, 0, TB))
            over_tiles(pe, tile)
            proj_tile(Turn(NTILES // TB, 0, TB) + -1)

            def q_rows(n, c):
                pe.wait_ge(xnT_sb, n.at(1, 1))
                if c == 0 and not n.less(L2 + 2):
                    pe.wait_ge(gated, (n + -1).at(1, -L2))
                pe.matmul((W5, W6)[c][:, :], wqkv2[:, c, :], xnT[n.p][:, 1:T + 1], start=True, stop=True).then_inc(qk_ps, 1)

            def v_rows(n, front):
                if front:
                    pe.wait_ge(res_part, (n + 1).at(2, 1))
                elif not n.less(L2 + 1):
                    pe.wait_ge(gated, n.at(1, -L2))
                for j in range(J):
                    ins = pe.matmul(W5[:, j * 128:(j + 1) * 128], xnT[n.p][:, 1 + j * 128:1 + (j + 1) * 128], wqkv2[:, 2, :],
                                    start=True, stop=True)
                ins.then_inc(v2_ps, 1)

            def max_scores(n, k):
                s, (j, g, nh) = k // MU, MAX_UNITS[k % MU]
                if k % (2 * MU) == 0:
                    half = k // (2 * MU)
                    pe.wait_ge(half_loaded[n.p][half], n.own(16 * QK_LOADS, 16 * QK_LOADS - 16 * QK_LOADS * HALVES))
                if not (n.less(L2 + 1) and k < 2):
                    pe.wait_ge(max_read, n.at(MU * SHEETS, k - 1 - MU * SHEETS * L2))
                w = 128 * (j + 1)
                for i in range(nh):
                    h = G * s + g + i
                    ins = pe.matmul(bank[2 + k % 2][:, i * w:(i + 1) * w], QT[n.p][0:MROWS, h, j * 128:(j + 1) * 128],
                                    KT[n.p][0:MROWS, h, 0:w], start=True, stop=True)
                ins.then_inc(max_ps, 1)

            def turn_max(n, before_, front):
                pe.wait_ge(max_read, n.at(MU * SHEETS, MU * SHEETS - MU * SHEETS * L2))
                if before_:
                    pe.wait_ge(yT_sb, (n + -1).at(1, 0))
                elif front:
                    pe.wait_ge(res_part, (n + 1).at(2, 2))
                for j in range(J):
                    ins = pe.transpose(W6[0:H, j * 128:(j + 1) * 128], nmax[:, j, :], ident[:, :])
                ins.then_inc(maxT_ps, 1)

            def shifted_scores(b, s, u):
                k = s * UNITS + u
                if k == 0:
                    pe.wait_ge(shift_loaded[b.p], b.own(16, 16 - 16 * HALVES))
                if not (b.less(L2 + 1) and k < 2):
                    pe.wait_ge(s_sb, b.at(PASS, k - 1 - PASS * L2))
                for g, kb, c in unit_parts(u):
                    h = G * s + g
                    n = T - 128 * kb
                    ins = pe.matmul(bank[k % 2][:, c:c + n], KT[b.p][0:SROWS, h, 128 * kb:128 * kb + 128],
                                    QT[b.p][0:SROWS, h, 128 * kb:T], start=True, stop=True)
                ins.then_inc(s_ps, 1)

            def turn_y2(b, front):
                pe.wait_ge(y_ready, b.at(1, 1))
                if front:
                    pe.wait_ge(res_part, (b + 3).at(2, 2))
                else:
                    pe.wait_ge(r_tanh, (b + 1).at(1, 1 - L2) if within(b + 1) else B)
                for j in range(J):
                    ins = pe.transpose(W6[:, j * 128:(j + 1) * 128], y[:, j, :, :].rearrange("p h d -> p (h d)"), ident[:, :])
                ins.then_inc(yT_ps, 1)

            def project_out2(b):
                pe.wait_ge(yT_sb, b.at(1, 1))
                if within(b + 2):
                    pe.wait_ge(v2_sb, (b + 2).at(1, 1 - L2))
                else:
                    pe.wait_ge(gated, B)
                    if not within(b + 1):
                        pe.wait_ge(out_ready, b.at(1, -L2))
                for j in range(J):
                    ins = pe.matmul(W5[:, j * 128:(j + 1) * 128], yT[:, j * 128:(j + 1) * 128], wo2[:, :], start=True, stop=True)
                ins.then_inc(proj2_ps, 1)

            def k_rows(n, before_):
                pe.wait_ge(mixed, n.at(4, 4 - 4 * L2))
                if before_:
                    pe.wait_ge(out_ready, (n + -1).at(1, -L2))
                else:
                    pe.wait_ge(v2_sb, n.at(1, 1 - L2))
                pe.matmul(W5[:, :], wrkv[:, 1, :], t2[1][:, :], start=True, stop=True).then_inc(k_ps, 1)

            def r_rows(n):
                pe.wait_ge(shift_lo, n.at(1, 1 - L2))
                for j in range(J):
                    ins = pe.matmul(W6[:, j * 128:(j + 1) * 128], t2[0][:, j * 128:(j + 1) * 128], wrkv[:, 0, :], start=True, stop=True)
                ins.then_inc(r_ps, 1)

            def kv_rows(n):
                pe.wait_ge(k_sq, n.at(1, 1 - L2))
                for j in range(J):
                    ins = pe.matmul(W5[:, j * 128:(j + 1) * 128], hr[1][:, j * 128:(j + 1) * 128], wrkv[:, 2, :], start=True, stop=True)
                ins.then_inc(kv_ps, 1)

            def body2(b):
                core, front, after, before_ = within(b), within(b + 2), within(b + 1), within(b + -1)
                at = [0]

                def maxes(n):
                    for _ in range(n):
                        if after and at[0] < MU * SHEETS:
                            max_scores(b + 1, at[0])
                            at[0] += 1

                for u in range(UNITS):
                    maxes(1)
                    if core:
                        shifted_scores(b, 0, u)
                    if u == 1 and before_:
                        turn_oT(b + -1, 3, False)
                for s in range(1, SHEETS):
                    for k in range(J):
                        if core:
                            shifted_scores(b, s, 2 * k)
                        maxes(1)
                        if core:
                            shifted_scores(b, s, 2 * k + 1)
                        maxes(1)
                        if core:
                            pv(b, s - 1, k)
                        if (s, k) == (1, 1) and front:
                            turn_xn(b + 2, False)
                        if (s, k) == (2, 0) and front:
                            q_rows(b + 2, 1)
                        if (s, k) == (3, 0) and before_:
                            turn_y2(b + -1, front)
                        if (s, k) == (3, 2) and before_:
                            project_out2(b + -1)
                        maxes(1)
                    if core:
                        shifted_scores(b, s, 8)
                        shifted_scores(b, s, 9)
                    if s == 1 and front:
                        q_rows(b + 2, 0)
                    if s == 2 and after:
                        v_rows(b + 1, front)
                    if s >= 2 and core:
                        turn_oT(b, s - 2, False)
                maxes(MU * SHEETS)
                if after:
                    turn_max(b + 1, before_, front)
                for k in range(J):
                    if core:
                        pv(b, SHEETS - 1, k)
                    if k == 0 and after:
                        k_rows(b + 1, before_)
                    if k == 1 and core:
                        turn_oT(b, 2, False)
                    if k == 1 and after:
                        r_rows(b + 1)
                    if k == 3 and after:
                        kv_rows(b + 1)

            over_layer2(pe, body2)


def layout(inputs):
    import numpy as _np

    c = _np.ascontiguousarray
    a = {k: _np.asarray(v) for k, v in inputs.items()}
    half = DH // 2
    order = _np.arange(D).reshape(H, DH).T.reshape(D)
    swap = _np.arange(D).reshape(H, 2, half)[:, ::-1].reshape(D)[order]
    wq, wk = a["L0_attn_Wq"], a["L0_attn_Wk"]
    arrays = {"x": c(a["L0_attn_x"])}
    arrays["wqk"] = c(_np.stack([wq[order].T, wq[swap].T, wk[order].T, wk[swap].T], axis=1))
    arrays["wvr"] = c(_np.concatenate([a["L0_attn_Wv"].T, a["L0_ffn_router_w"].T], axis=1))
    arrays["wo"] = c(a["L0_attn_Wo"].T)
    fc = _np.concatenate([a["L0_ffn_w_fc"], a["L0_ffn_shared_fc"][None]])
    pj = _np.concatenate([a["L0_ffn_w_proj"], a["L0_ffn_shared_proj"][None]])
    arrays["fc"] = c(fc.transpose(0, 2, 1))
    arrays["proj"] = c(pj.transpose(0, 2, 1).reshape(E + 1, NB, 128, D).transpose(0, 2, 1, 3))
    w = a["L1_attn_W_qkv"]
    w3 = w.reshape(3, D, D)
    arrays["wqkv2"] = c(_np.stack([w3[0][order].T, w3[1][order].T, w3[2].T], axis=1))
    arrays["wo2"] = c(a["L1_attn_W_out"].T)
    arrays["wrkv"] = c(_np.stack([a["L1_ffn_W_r"].T, a["L1_ffn_W_k"].T, a["L1_ffn_W_v"].T], axis=1))
    arrays["mu"] = c(_np.stack([a["L1_ffn_mu_r"], a["L1_ffn_mu_k"]], axis=1))
    arrays["abd"] = c(_np.broadcast_to(_np.stack([a["L1_attn_a"], a["L1_attn_b"], a["L1_attn_dt"]])[None], (128, 3)))

    f = _np.float32
    freq = (f(10000.0) ** (-_np.arange(half, dtype=f) / f(half))).astype(f)
    ang = _np.arange(T, dtype=f)[None, :] * freq[order % half][:, None]
    sign = _np.where(order % DH < half, -1, 1).astype(f)[:, None]
    arrays["rope"] = c(_np.stack([_np.cos(ang), sign * _np.sin(ang)], axis=1).astype(f))
    i = _np.arange(128)
    causal = (i[:, None] <= i[None, :]).astype(f)
    arrays["tri"] = c(_np.broadcast_to(causal[:, None], (128, 4, 128)))
    arrays["own"] = c(_np.broadcast_to(order[:, None, None] // DH == _np.arange(H)[None, :, None], (128, H, DH + 1)).astype(f))
    arrays["ident"] = _np.eye(128, dtype=f)
    arrays["before"] = c(_np.stack([i[:, None] < i[None, :], _np.ones((128, 128))], axis=1).astype(mybir.dt.np(BF16)))
    e = _np.arange(E)
    arrays["lower"] = c(_np.broadcast_to((e[None, :] < e[:, None]).astype(f), (128, E, E)))
    arrays["incl"] = c(_np.broadcast_to((e[None, :] <= e[:, None]).astype(f), (128, E, E)))
    arrays["ebase"] = c(_np.broadcast_to(_np.stack([e * REGION, e]).astype(f), (128, 2, E)))
    t = _np.arange(NTILES)
    empty = DUMMY + t % SPARE * GT
    arrays["tiles"] = c(_np.broadcast_to(_np.stack([t, t * GT - empty, empty]).astype(f), (128, 3, NTILES)))
    arrays["steps"] = c(_np.broadcast_to((_np.arange(CAP // GT) * GT).astype(f), (128, CAP // GT)))
    tok = _np.arange(T)
    hq = _np.zeros((J, H, T), f)
    hk = _np.zeros((J + 2, H, T), f)
    for j in range(J):
        hq[j][:, (tok // 128 == j) & (tok % 128 < CHUNK)] = 1
        hk[j][:, (tok // 128 == j) & (tok % 128 >= CHUNK)] = MASKED
    hk[J:] = 1
    arrays["half_q"], arrays["half_k"] = hq.astype(mybir.dt.np(BF16)), hk.astype(mybir.dt.np(BF16))
    return arrays


def kernel(**inputs):
    import concourse.bacc as _bacc
    from concourse import mybir as _mybir
    from concourse.bass_utils import run_bass_kernel_spmd as _run

    nc = _bacc.Bacc("TRN2", target_bir_lowering=False, num_devices=1)
    arrays = layout(inputs)
    io = {n: nc.dram_tensor("in_" + n, a.shape, _mybir.dt.from_np(a.dtype), kind="ExternalInput").ap() for n, a in arrays.items()}
    out = nc.dram_tensor("out", (B, T, D), F32, kind="ExternalOutput").ap()
    build(nc, io, out)
    r = _run(nc, [{"in_" + n: a for n, a in arrays.items()}], core_ids=[0])
    return r.results[0]["out"]
```
